# Optimizing a Trainium2 kernel written in Bass

```python
import numpy as np
import jax
import jax.numpy as jnp

def _softmax(x, axis=-1):
    return jax.nn.softmax(x, axis=axis)

def _gelu(x):
    return jax.nn.gelu(x, approximate=True)

def _silu(x):
    return jax.nn.silu(x)

def _sigmoid(x):
    return jax.nn.sigmoid(x)

def _layernorm(x, axis=-1, eps=1e-05):
    m = jnp.mean(x, axis=axis, keepdims=True)
    v = jnp.var(x, axis=axis, keepdims=True)
    return (x - m) / jnp.sqrt(v + eps)

def _scatter_add(tgt, idx, src, axis=0):
    return tgt.at[idx].add(src)

def _segment_sum(src, seg, n):
    return jax.ops.segment_sum(src, seg, n)
kernel_name = 'mk_gnn_resnorm_d4_gnn_r8_f4ad85'

def setup_inputs(seed: int=0):
    np.random.seed(seed)
    _w = jnp.asarray

    def _rec_inputs():
        import jax
        import jax.numpy as jnp
        _gk = jax.random.key(seed)
        x = -0.0002117 + 1 * jax.random.normal(jax.random.fold_in(_gk, 1), (1250, 512), jnp.float32)
        src = jax.random.randint(jax.random.fold_in(_gk, 2), (40000,), 0, 1250, jnp.int32)
        dst = jnp.minimum((1250 * jax.random.uniform(jax.random.fold_in(_gk, 3), (40000,)) ** 2.0).astype(jnp.int32), 9999)
        _o = jnp.argsort(dst, stable=True)
        src = src[_o]
        dst = dst[_o]
        edge_attr_32 = jax.random.uniform(jax.random.fold_in(_gk, 11), (40000, 32), jnp.float32, 0.0, 1)
        edge_attr_4 = 0.000937891 + 0.999965 * jax.random.normal(jax.random.fold_in(_gk, 12), (40000, 4), jnp.float32)
        edge_attr_96 = -4.21973e-05 + 0.999841 * jax.random.normal(jax.random.fold_in(_gk, 13), (40000, 96), jnp.float32)
        return (x, src, dst, edge_attr_32, edge_attr_4, edge_attr_96)
    x, src, dst, edge_attr_32, edge_attr_4, edge_attr_96 = _rec_inputs()

    def _L0_gnn_setup():
        import jax, jax.numpy as jnp
        import numpy as np
        NODE_DIM, EDGE_DIM, HIDDEN, OUT = (512, 96, 1024, 512)
        N_NODES, N_EDGES = (6250, 100000)
        LN_EPS = 1e-05
        key = jax.random.key(seed)
        ks = jax.random.split(key, 12)
        node_feat = jax.random.normal(ks[0], (N_NODES, NODE_DIM), dtype=jnp.float32)
        edge_feat = jax.random.normal(ks[1], (N_EDGES, EDGE_DIM), dtype=jnp.float32)
        edge_index = jax.random.randint(ks[2], (2, N_EDGES), 0, N_NODES, dtype=jnp.int32)
        in_dim = NODE_DIM + EDGE_DIM

        def lin(k, fan_in, fan_out):
            bound = 1.0 / np.sqrt(fan_in)
            kw, kb = jax.random.split(k)
            W = jax.random.uniform(kw, (fan_in, fan_out), minval=-bound, maxval=bound, dtype=jnp.float32)
            b = jax.random.uniform(kb, (fan_out,), minval=-bound, maxval=bound, dtype=jnp.float32)
            return (W, b)
        W1, b1 = lin(ks[3], in_dim, HIDDEN)
        W2, b2 = lin(ks[4], HIDDEN, HIDDEN)
        W3, b3 = lin(ks[5], HIDDEN, OUT)
        gamma = jnp.ones((OUT,), dtype=jnp.float32)
        beta = jnp.zeros((OUT,), dtype=jnp.float32)
        return {'node_feat': node_feat, 'edge_feat': edge_feat, 'edge_index': edge_index, 'n_nodes': N_NODES, 'W1': W1, 'b1': b1, 'W2': W2, 'b2': b2, 'W3': W3, 'b3': b3, 'gamma': gamma, 'beta': beta}
    _L0_gnn_all = _L0_gnn_setup()
    _L0_gnn_in = {k: v for k, v in _L0_gnn_all.items() if k in ('W1', 'b1', 'W2', 'b2', 'W3', 'b3', 'gamma', 'beta')}
    del _L0_gnn_all

    def _L1_gnn_setup():
        import jax, jax.numpy as jnp
        import numpy as np
        import math
        N, E = (2500, 25000)
        MUL = 128
        D = MUL + 3 * MUL
        EDGE_ATTR = 32
        HID = 32
        LOG2 = math.log(2.0)

        def ssp(x):
            return jax.nn.softplus(x) - LOG2

        def split_irreps(x):
            return (x[:, :MUL], x[:, MUL:].reshape(x.shape[0], MUL, 3))

        def merge_irreps(x0, x1):
            return jnp.concatenate([x0, x1.reshape(x1.shape[0], MUL * 3)], axis=-1)

        def irrep_linear(x, W0, b0, W1):
            x0, x1 = split_irreps(x)
            y0 = x0 @ W0 + b0
            y1 = jnp.einsum('nuc,uv->nvc', x1, W1)
            return merge_irreps(y0, y1)
        key = jax.random.key(seed)
        ks = iter(jax.random.split(key, 32))

        def randn(shape, scale=1.0):
            return (scale * jax.random.normal(next(ks), shape)).astype(jnp.float32)
        inp = {'x': randn((N, D)), 'edge_sh': randn((E, 4)), 'edge_attr': jax.random.uniform(next(ks), (E, EDGE_ATTR), dtype=jnp.float32), 'edge_index': jax.random.randint(next(ks), (2, E), 0, N, dtype=jnp.int32), 'W_pre0': randn((MUL, MUL), MUL ** (-0.5)), 'b_pre0': jnp.zeros((MUL,), jnp.float32), 'W_pre1': randn((MUL, MUL), MUL ** (-0.5)), 'W_nd0': randn((MUL, MUL), MUL ** (-0.5)), 'b_nd0': jnp.zeros((MUL,), jnp.float32), 'W_nd1': randn((MUL, MUL), MUL ** (-0.5)), 'W_g1': randn((2 * MUL, 2 * MUL), (2 * MUL) ** (-0.5)), 'b_g1': jnp.zeros((2 * MUL,), jnp.float32), 'W_g2': randn((2 * MUL, 2 * MUL), (2 * MUL) ** (-0.5)), 'b_g2': jnp.zeros((2 * MUL,), jnp.float32), 'W_f1': randn((EDGE_ATTR, HID), EDGE_ATTR ** (-0.5)), 'W_f2': randn((HID, 4 * MUL), HID ** (-0.5)), 'W_s1': randn((3 * MUL, HID), (3 * MUL) ** (-0.5)), 'W_s2': randn((HID, 4 * MUL), HID ** (-0.5)), 'W_o0': randn((MUL, MUL), MUL ** (-0.5)), 'b_o0': jnp.zeros((MUL,), jnp.float32), 'W_o1': randn((MUL, MUL), MUL ** (-0.5))}
        return inp
    _L1_gnn_all = _L1_gnn_setup()
    _L1_gnn_in = {k: v for k, v in _L1_gnn_all.items() if k in ('W_pre0', 'b_pre0', 'W_pre1', 'W_nd0', 'b_nd0', 'W_nd1', 'W_g1', 'b_g1', 'W_g2', 'b_g2', 'W_f1', 'W_f2', 'W_s1', 'W_s2', 'W_o0', 'b_o0', 'W_o1')}
    del _L1_gnn_all

    def _L2_gnn_setup():
        import jax, jax.numpy as jnp
        import numpy as np
        N_NODES = 6250
        N_EDGES = 100000
        D_IN = 512
        D_OUT = 512
        EPS = 1e-05
        key = jax.random.key(seed)
        k1, k2, k3, k4, k5 = jax.random.split(key, 5)
        x = jax.random.normal(k1, (N_NODES, D_IN), dtype=jnp.float32)
        edge_index = jax.random.randint(k2, (2, N_EDGES), 0, N_NODES, dtype=jnp.int64)
        s = 1.0 / np.sqrt(D_IN)
        W_l = jax.random.uniform(k3, (D_OUT, D_IN), jnp.float32, -s, s)
        b_l = jnp.zeros((D_OUT,), jnp.float32)
        W_r = jax.random.uniform(k4, (D_OUT, D_IN), jnp.float32, -s, s)
        gamma = jnp.ones((D_OUT,), jnp.float32)
        beta = jnp.zeros((D_OUT,), jnp.float32)
        return {'x': x, 'edge_index': edge_index, 'W_l': W_l, 'b_l': b_l, 'W_r': W_r, 'gamma': gamma, 'beta': beta}
    _L2_gnn_all = _L2_gnn_setup()
    _L2_gnn_in = {k: v for k, v in _L2_gnn_all.items() if k in ('W_l', 'b_l', 'W_r', 'gamma', 'beta')}
    del _L2_gnn_all

    def _L3_gnn_setup():
        import jax, jax.numpy as jnp
        import numpy as np
        D = 512
        H = 8
        DH = D // H
        F = 256
        L = 2
        N = 2500
        E = 40000
        EPS = 1e-05

        def _xavier(key, shape):
            fan_out, fan_in = (shape[-2], shape[-1])
            lim = float(np.sqrt(6.0 / (fan_in + fan_out)))
            return jax.random.uniform(key, shape, jnp.float32, -lim, lim)

        def _batchnorm(x, g, b):
            mu = jnp.mean(x, axis=0)
            var = jnp.mean(jnp.square(x - mu), axis=0)
            return (x - mu) * jax.lax.rsqrt(var + EPS) * g + b

        def _layernorm(x, g, b):
            mu = jnp.mean(x, axis=-1, keepdims=True)
            var = jnp.mean(jnp.square(x - mu), axis=-1, keepdims=True)
            return (x - mu) * jax.lax.rsqrt(var + EPS) * g + b
        key = jax.random.key(seed)
        ks = jax.random.split(key, 12)
        src = jax.random.normal(ks[0], (N, D), jnp.float32)
        edge_index = jax.random.randint(ks[1], (2, E), 0, N)
        return {'src': src, 'edge_index': edge_index, 'Wq': _xavier(ks[2], (L, D, D)), 'bq': jnp.zeros((L, D), jnp.float32), 'Wk': _xavier(ks[3], (L, D, D)), 'Wv': _xavier(ks[4], (L, D, D)), 'Wo': _xavier(ks[5], (L, D, D)), 'bo': jnp.zeros((L, D), jnp.float32), 'W1': _xavier(ks[6], (L, F, D)), 'b1': jnp.zeros((L, F), jnp.float32), 'W2': _xavier(ks[7], (L, D, F)), 'b2': jnp.zeros((L, D), jnp.float32), 'g1': jnp.ones((L, D), jnp.float32), 'beta1': jnp.zeros((L, D), jnp.float32), 'g2': jnp.ones((L, D), jnp.float32), 'beta2': jnp.zeros((L, D), jnp.float32), 'ln_g': jnp.ones((D,), jnp.float32), 'ln_b': jnp.zeros((D,), jnp.float32)}
    _L3_gnn_all = _L3_gnn_setup()
    _L3_gnn_in = {k: v for k, v in _L3_gnn_all.items() if k in ('Wq', 'bq', 'Wk', 'Wv', 'Wo', 'bo', 'W1', 'b1', 'W2', 'b2', 'g1', 'beta1', 'g2', 'beta2', 'ln_g', 'ln_b')}
    del _L3_gnn_all
    return {'x': x, 'src': src, 'dst': dst, 'edge_attr_32': edge_attr_32, 'edge_attr_4': edge_attr_4, 'edge_attr_96': edge_attr_96, 'L0_gnn_W1': _L0_gnn_in['W1'], 'L0_gnn_b1': _L0_gnn_in['b1'], 'L0_gnn_W2': _L0_gnn_in['W2'], 'L0_gnn_b2': _L0_gnn_in['b2'], 'L0_gnn_W3': _L0_gnn_in['W3'], 'L0_gnn_b3': _L0_gnn_in['b3'], 'L0_gnn_gamma': _L0_gnn_in['gamma'], 'L0_gnn_beta': _L0_gnn_in['beta'], 'L1_gnn_W_pre0': _L1_gnn_in['W_pre0'], 'L1_gnn_b_pre0': _L1_gnn_in['b_pre0'], 'L1_gnn_W_pre1': _L1_gnn_in['W_pre1'], 'L1_gnn_W_nd0': _L1_gnn_in['W_nd0'], 'L1_gnn_b_nd0': _L1_gnn_in['b_nd0'], 'L1_gnn_W_nd1': _L1_gnn_in['W_nd1'], 'L1_gnn_W_g1': _L1_gnn_in['W_g1'], 'L1_gnn_b_g1': _L1_gnn_in['b_g1'], 'L1_gnn_W_g2': _L1_gnn_in['W_g2'], 'L1_gnn_b_g2': _L1_gnn_in['b_g2'], 'L1_gnn_W_f1': _L1_gnn_in['W_f1'], 'L1_gnn_W_f2': _L1_gnn_in['W_f2'], 'L1_gnn_W_s1': _L1_gnn_in['W_s1'], 'L1_gnn_W_s2': _L1_gnn_in['W_s2'], 'L1_gnn_W_o0': _L1_gnn_in['W_o0'], 'L1_gnn_b_o0': _L1_gnn_in['b_o0'], 'L1_gnn_W_o1': _L1_gnn_in['W_o1'], 'L2_gnn_W_l': _L2_gnn_in['W_l'], 'L2_gnn_b_l': _L2_gnn_in['b_l'], 'L2_gnn_W_r': _L2_gnn_in['W_r'], 'L2_gnn_gamma': _L2_gnn_in['gamma'], 'L2_gnn_beta': _L2_gnn_in['beta'], 'L3_gnn_Wq': _L3_gnn_in['Wq'], 'L3_gnn_bq': _L3_gnn_in['bq'], 'L3_gnn_Wk': _L3_gnn_in['Wk'], 'L3_gnn_Wv': _L3_gnn_in['Wv'], 'L3_gnn_Wo': _L3_gnn_in['Wo'], 'L3_gnn_bo': _L3_gnn_in['bo'], 'L3_gnn_W1': _L3_gnn_in['W1'], 'L3_gnn_b1': _L3_gnn_in['b1'], 'L3_gnn_W2': _L3_gnn_in['W2'], 'L3_gnn_b2': _L3_gnn_in['b2'], 'L3_gnn_g1': _L3_gnn_in['g1'], 'L3_gnn_beta1': _L3_gnn_in['beta1'], 'L3_gnn_g2': _L3_gnn_in['g2'], 'L3_gnn_beta2': _L3_gnn_in['beta2'], 'L3_gnn_ln_g': _L3_gnn_in['ln_g'], 'L3_gnn_ln_b': _L3_gnn_in['ln_b']}

def reference(x, src, dst, edge_attr_32, edge_attr_4, edge_attr_96, L0_gnn_W1, L0_gnn_b1, L0_gnn_W2, L0_gnn_b2, L0_gnn_W3, L0_gnn_b3, L0_gnn_gamma, L0_gnn_beta, L1_gnn_W_pre0, L1_gnn_b_pre0, L1_gnn_W_pre1, L1_gnn_W_nd0, L1_gnn_b_nd0, L1_gnn_W_nd1, L1_gnn_W_g1, L1_gnn_b_g1, L1_gnn_W_g2, L1_gnn_b_g2, L1_gnn_W_f1, L1_gnn_W_f2, L1_gnn_W_s1, L1_gnn_W_s2, L1_gnn_W_o0, L1_gnn_b_o0, L1_gnn_W_o1, L2_gnn_W_l, L2_gnn_b_l, L2_gnn_W_r, L2_gnn_gamma, L2_gnn_beta, L3_gnn_Wq, L3_gnn_bq, L3_gnn_Wk, L3_gnn_Wv, L3_gnn_Wo, L3_gnn_bo, L3_gnn_W1, L3_gnn_b1, L3_gnn_W2, L3_gnn_b2, L3_gnn_g1, L3_gnn_beta1, L3_gnn_g2, L3_gnn_beta2, L3_gnn_ln_g, L3_gnn_ln_b):
    import jax
    import jax.numpy as jnp

    def _L0_gnn_ref(node_feat, edge_feat, edge_index, n_nodes, W1, b1, W2, b2, W3, b3, gamma, beta):
        import jax, jax.numpy as jnp
        import numpy as np
        NODE_DIM, EDGE_DIM, HIDDEN, OUT = (512, 96, 1024, 512)
        N_NODES, N_EDGES = (6250, 100000)
        LN_EPS = 1e-05
        dst = edge_index[1]
        agg = jax.ops.segment_sum(edge_feat, dst, num_segments=n_nodes)
        inp = jnp.concatenate([node_feat, agg], axis=-1)
        h = jax.nn.relu(inp @ W1 + b1)
        h = jax.nn.relu(h @ W2 + b2)
        y = h @ W3 + b3
        mu = jnp.mean(y, axis=-1, keepdims=True)
        var = jnp.mean(jnp.square(y - mu), axis=-1, keepdims=True)
        return (y - mu) * jax.lax.rsqrt(var + LN_EPS) * gamma + beta

    def _L1_gnn_ref(x, edge_sh, edge_attr, edge_index, W_pre0, b_pre0, W_pre1, W_nd0, b_nd0, W_nd1, W_g1, b_g1, W_g2, b_g2, W_f1, W_f2, W_s1, W_s2, W_o0, b_o0, W_o1):
        import jax, jax.numpy as jnp
        import numpy as np
        import math
        N, E = (2500, 25000)
        MUL = 128
        D = MUL + 3 * MUL
        EDGE_ATTR = 32
        HID = 32
        LOG2 = math.log(2.0)

        def ssp(x):
            return jax.nn.softplus(x) - LOG2

        def split_irreps(x):
            return (x[:, :MUL], x[:, MUL:].reshape(x.shape[0], MUL, 3))

        def merge_irreps(x0, x1):
            return jnp.concatenate([x0, x1.reshape(x1.shape[0], MUL * 3)], axis=-1)

        def irrep_linear(x, W0, b0, W1):
            x0, x1 = split_irreps(x)
            y0 = x0 @ W0 + b0
            y1 = jnp.einsum('nuc,uv->nvc', x1, W1)
            return merge_irreps(y0, y1)
        edge_dst, edge_src = (edge_index[0], edge_index[1])
        old_x = x
        pre = irrep_linear(x, W_pre0, b_pre0, W_pre1)
        p0, p1 = split_irreps(pre)
        pd0 = p0[edge_dst]
        ip1 = jnp.einsum('eum,eum->eu', p1[edge_dst], p1[edge_src]) / 3.0
        s0 = jnp.concatenate([pd0, pd0, ip1], axis=-1)
        x0, x1 = split_irreps(x)
        n1 = jnp.sqrt(jnp.sum(x1 * x1, axis=-1) / 3.0)
        g = jax.nn.silu(jnp.concatenate([x0, n1], -1) @ W_g1 + b_g1) @ W_g2 + b_g2
        xg = merge_irreps(g[:, :MUL], x1 * g[:, MUL:, None])
        x = irrep_linear(xg, W_nd0, b_nd0, W_nd1)
        self_x = x
        w = ssp(edge_attr @ W_f1) @ W_f2 * (ssp(s0 @ W_s1) @ W_s2)
        w1, w2, w3, w4 = jnp.split(w, 4, axis=-1)
        x0e, x1e = split_irreps(x[edge_src])
        sh0, sh1 = (edge_sh[:, 0], edge_sh[:, 1:4])
        out0 = w1 * x0e * sh0[:, None] + w4 * (jnp.einsum('eum,em->eu', x1e, sh1) / jnp.sqrt(3.0))
        out1 = w2[:, :, None] * x0e[:, :, None] * sh1[:, None, :] + w3[:, :, None] * x1e * sh0[:, None, None]
        edge_feat = merge_irreps(out0, out1)
        out = jax.ops.segment_sum(edge_feat, edge_dst, num_segments=old_x.shape[0])
        out = out + self_x
        out = irrep_linear(out, W_o0, b_o0, W_o1)
        return out + old_x

    def _L2_gnn_ref(x, edge_index, W_l, b_l, W_r, gamma, beta):
        import jax, jax.numpy as jnp
        import numpy as np
        N_NODES = 6250
        N_EDGES = 100000
        D_IN = 512
        D_OUT = 512
        EPS = 1e-05
        N = x.shape[0]
        src = edge_index[0]
        dst = edge_index[1]
        agg = jax.ops.segment_sum(x[src], dst, num_segments=N)
        deg = jax.ops.segment_sum(jnp.ones_like(dst, jnp.float32), dst, num_segments=N)
        mean_nb = agg / jnp.maximum(deg, 1.0)[:, None]
        h = mean_nb @ W_l.T + b_l + x @ W_r.T
        h = jax.nn.relu(h)
        mu = jnp.mean(h, axis=0)
        var = jnp.mean((h - mu) ** 2, axis=0)
        out = (h - mu) * jax.lax.rsqrt(var + EPS) * gamma + beta
        return out

    def _L3_gnn_ref(src, edge_index, Wq, bq, Wk, Wv, Wo, bo, W1, b1, W2, b2, g1, beta1, g2, beta2, ln_g, ln_b):
        import jax, jax.numpy as jnp
        import numpy as np
        D = 512
        H = 8
        DH = D // H
        F = 256
        L = 2
        N = 2500
        E = 40000
        EPS = 1e-05

        def _xavier(key, shape):
            fan_out, fan_in = (shape[-2], shape[-1])
            lim = float(np.sqrt(6.0 / (fan_in + fan_out)))
            return jax.random.uniform(key, shape, jnp.float32, -lim, lim)

        def _batchnorm(x, g, b):
            mu = jnp.mean(x, axis=0)
            var = jnp.mean(jnp.square(x - mu), axis=0)
            return (x - mu) * jax.lax.rsqrt(var + EPS) * g + b

        def _layernorm(x, g, b):
            mu = jnp.mean(x, axis=-1, keepdims=True)
            var = jnp.mean(jnp.square(x - mu), axis=-1, keepdims=True)
            return (x - mu) * jax.lax.rsqrt(var + EPS) * g + b
        n = src.shape[0]
        scaling = float(DH) ** (-0.5)
        tgt = edge_index[1]
        srcidx = edge_index[0]
        x = src
        for l in range(L):
            q = ((x @ Wq[l].T + bq[l]) * scaling).reshape(n, H, DH)
            k = (x @ Wk[l].T).reshape(n, H, DH)
            v = (x @ Wv[l].T).reshape(n, H, DH)
            scores = jnp.einsum('ehd,ehd->eh', q[tgt], k[srcidx])
            m = jax.ops.segment_max(scores, tgt, num_segments=n)
            p = jnp.exp(scores - m[tgt])
            s = jax.ops.segment_sum(p, tgt, num_segments=n)
            w = p / (s[tgt] + 1e-16)
            agg = jax.ops.segment_sum(w[:, :, None] * v[srcidx], tgt, num_segments=n)
            attn = agg.reshape(n, D) @ Wo[l].T + bo[l]
            x = _batchnorm(x + attn, g1[l], beta1[l])
            ff = jax.nn.relu(x @ W1[l].T + b1[l]) @ W2[l].T + b2[l]
            x = _batchnorm(x + ff, g2[l], beta2[l])
        return _layernorm(x, ln_g, ln_b)
    edge_index = jnp.stack([src, dst])
    x = _layernorm(x + _L0_gnn_ref(x, edge_attr_96, edge_index, 1250, L0_gnn_W1, L0_gnn_b1, L0_gnn_W2, L0_gnn_b2, L0_gnn_W3, L0_gnn_b3, L0_gnn_gamma, L0_gnn_beta), axis=-1)
    x = _layernorm(x + _L1_gnn_ref(x, edge_attr_4, edge_attr_32, edge_index, L1_gnn_W_pre0, L1_gnn_b_pre0, L1_gnn_W_pre1, L1_gnn_W_nd0, L1_gnn_b_nd0, L1_gnn_W_nd1, L1_gnn_W_g1, L1_gnn_b_g1, L1_gnn_W_g2, L1_gnn_b_g2, L1_gnn_W_f1, L1_gnn_W_f2, L1_gnn_W_s1, L1_gnn_W_s2, L1_gnn_W_o0, L1_gnn_b_o0, L1_gnn_W_o1), axis=-1)
    x = _layernorm(x + _L2_gnn_ref(x, edge_index, L2_gnn_W_l, L2_gnn_b_l, L2_gnn_W_r, L2_gnn_gamma, L2_gnn_beta), axis=-1)
    x = _layernorm(x + _L3_gnn_ref(x, edge_index, L3_gnn_Wq, L3_gnn_bq, L3_gnn_Wk, L3_gnn_Wv, L3_gnn_Wo, L3_gnn_bo, L3_gnn_W1, L3_gnn_b1, L3_gnn_W2, L3_gnn_b2, L3_gnn_g1, L3_gnn_beta1, L3_gnn_g2, L3_gnn_beta2, L3_gnn_ln_g, L3_gnn_ln_b), axis=-1)
    return x

_drawn_inputs = setup_inputs


def setup_inputs(seed=0):
    import zlib

    import numpy as np

    out = dict(_drawn_inputs(seed))
    spreads = {'L0_gnn_gamma': (1.0, 0.2),
     'L0_gnn_beta': (0.0, 0.1),
     'L1_gnn_b_pre0': (0.0, 0.1),
     'L1_gnn_b_nd0': (0.0, 0.1),
     'L1_gnn_b_g1': (0.0, 0.1),
     'L1_gnn_b_g2': (0.0, 0.1),
     'L1_gnn_b_o0': (0.0, 0.384),
     'L2_gnn_b_l': (0.0, 0.1),
     'L2_gnn_gamma': (1.0, 0.2),
     'L2_gnn_beta': (0.0, 0.1),
     'L3_gnn_bq': (0.0, 0.34),
     'L3_gnn_bo': (0.0, 0.8),
     'L3_gnn_b1': (0.0, 0.1),
     'L3_gnn_b2': (0.0, 0.8),
     'L3_gnn_g1': (1.0, 0.2),
     'L3_gnn_beta1': (0.0, 0.1),
     'L3_gnn_g2': (1.0, 0.2),
     'L3_gnn_beta2': (0.0, 0.1),
     'L3_gnn_ln_g': (1.0, 0.2),
     'L3_gnn_ln_b': (0.0, 0.1)}
    factors = {'L0_gnn_b1': 2.952}
    for name, (base, spread) in spreads.items():
        noise = np.random.default_rng([zlib.crc32(name.encode()), seed]).standard_normal(out[name].shape)
        drawn = base * np.exp(spread * noise) if base else spread * noise
        out[name] = jnp.asarray(drawn.astype(out[name].dtype))
    for name, factor in factors.items():
        out[name] = (out[name] * factor).astype(out[name].dtype)
    return out
```

```python
from contextlib import ExitStack

import concourse.bass as bass
from concourse import mybir

P = 128
NODES, EDGES, D = 1250, 40000, 512
TILES = -(-NODES // P)
COLS = TILES * P
LAST = NODES - (TILES - 1) * P
SUB = 4
GROUP = SUB * P
GROUPS = (EDGES + TILES * (GROUP - 1)) // GROUP
GROUPS += GROUPS % 2
EP = 125
EF = EDGES // EP
CHUNK = 16
EA96, EA32, EA4 = 96, 32, 4
C_OTHER, C_KEY, REC = 132, 133, 136
CHUNKS = ((0, 512), (512, 512), (1024, 256))
BANK = 512
EPS = 1e-5
HEADS, DH = 8, 64
FF = 256
FAR = -1.0e30

F32 = mybir.dt.float32
F16 = mybir.dt.float16
BF16 = mybir.dt.bfloat16
I32 = mybir.dt.int32
ALU = mybir.AluOpType
ACT = mybir.ActivationFunctionType
AX = mybir.AxisListType

class Steps:

    def __init__(self, engine, sem, base=0):
        self.engine, self.sem, self.base, self.n = engine, sem, base, 0

    def done(self, ins):
        ins.then_inc(self.sem, 1)
        self.n += 1

    def settle(self):
        self.engine.wait_ge(self.sem, self.base + self.n)


class Core:

    def __init__(self, nc, ctx, a):
        self.nc, self.ctx, self.a = nc, ctx, a
        self.psum = ctx.enter_context(nc.psum_tensor("psum", [P, 8, BANK], F32))
        self.names = 0

    def sem(self, name):
        return self.ctx.enter_context(self.nc.semaphore(name))

    def keep(self, name, shape, dt=F32):
        return self.ctx.enter_context(self.nc.sbuf_tensor(name, shape, dt))


def sort_edges(k):
    nc, a = k.nc, k.a
    with ExitStack() as ctx:
        def sb(name, shape, dt=F32):
            return ctx.enter_context(nc.sbuf_tensor(name, shape, dt))

        key_i = sb("key_i", [EP, EF], I32)
        other_i = sb("other_i", [EP, EF], I32)
        other_f = sb("other_f", [EP, EF])
        tile_i = sb("tile_i", [EP, EF], I32)
        tile_f = sb("tile_f", [EP, EF])
        key_f = sb("key_f", [EP, EF])
        local = sb("local", [EP, EF])
        ones = sb("ones", [EP, EF])
        member = sb("member", [EP, TILES, EF])
        rank = sb("rank", [EP, TILES, EF])
        total = sb("total", [EP, TILES])
        before = sb("before", [EP, EP])
        every = sb("every", [EP, EP])
        cnt_i = sb("cnt_i", [EP, TILES], I32)
        grp_i = sb("grp_i", [EP, TILES], I32)
        grp = sb("grp", [EP, TILES])
        grp_end = sb("grp_end", [EP, TILES])
        grp_start = sb("grp_start", [EP, TILES])
        offset = sb("offset", [EP, TILES])
        group_no = sb("group_no", [EP, GROUPS])
        group_tile = sb("group_tile", [EP, GROUPS])
        slot_f = sb("slot_f", [EP, EF])
        slot_i = sb("slot_i", [EP, EF], I32)
        blank = sb("blank", [P, SUB, REC])
        stage = [sb(f"stage{b}", [EP, CHUNK, REC]) for b in range(2)]
        index = [sb(f"index{b}", [EP, CHUNK], I32) for b in range(2)]
        parts = [sb(f"attr_parts{b}", [EP, 3, CHUNK, EA96], BF16) for b in range(2)]
        other_c = [sb(f"other_c{b}", [EP, CHUNK]) for b in range(2)]
        rest = sb("attr_rest", [EP, CHUNK, EA96])
        hot = [sb(f"other_hot{b}", [EP, COLS], BF16) for b in range(4)]

        ends_loaded = k.sem("ends_loaded")
        masks_ready = k.sem("masks_ready")
        sorting = k.sem("sorting")
        totals_ready = k.sem("totals_ready")
        offsets_summed = k.sem("offsets_summed")
        blank_ready = k.sem("blank_ready")
        blanked = k.sem("blanked")
        features_in = [k.sem(f"features_in{b}") for b in range(2)]
        staged = [k.sem(f"staged{b}") for b in range(2)]
        k.scattered = [k.sem(f"scattered{b}") for b in range(2)]
        picked = k.sem("picked")
        split_act, split_dve = k.sem("split_act"), k.sem("split_dve")
        hot_ready, hot_used, sums_out = k.sem("hot_ready"), k.sem("hot_used"), k.sem("sums_out")
        ps_before, ps_every = k.psum[0:EP, 0, 0:TILES], k.psum[0:EP, 1, 0:TILES]
        ps_sums = k.psum[0:EA96, 2:5].rearrange("p c n -> p (c n)")
        rounds = EF // CHUNK // 2

        def chunks(engine, chunk):
            chunk(0, 0, True, False)
            chunk(1, 0, True, False)
            with engine.Fori(1, rounds - 1) as i:
                chunk(0, i, False, False)
                chunk(1, i, False, False)
            chunk(0, rounds - 1, False, False)
            chunk(1, rounds - 1, False, True)

        with nc.Block() as block:
            @block.sync
            def _(sp):
                sp.dma_start(key_i[:], a["src"].rearrange("(p f) -> p f", p=EP)).then_inc(ends_loaded, 16)
                sp.dma_start(other_i[:], a["dst"].rearrange("(p f) -> p f", p=EP)).then_inc(ends_loaded, 16)
                sp.wait_ge(blank_ready, 1)
                sp.dma_start(k.records.rearrange("(g p t) c -> p g (t c)", p=P, t=SUB),
                             blank[:].rearrange("p t c -> p (t c)")[:, None, :]
                             .broadcast_to([P, GROUPS, SUB * REC])).then_inc(blanked, 16)
                ea96 = a["edge_attr_96"].rearrange("(p f) d -> p f d", p=EP)
                ea32 = a["edge_attr_32"].rearrange("(p f) d -> p f d", p=EP)
                ea4 = a["edge_attr_4"].rearrange("(p f) d -> p f d", p=EP)

                def fetch(b, i, first, last):
                    at = bass.ds((2 * i + b) * CHUNK, CHUNK)
                    if not first:
                        sp.wait_ge(split_dve, 2 * (2 * i + b) - 2)
                        sp.wait_ge(k.scattered[b], i * 16 * CHUNK)
                    sp.dma_start(stage[b][:, :, 0:EA96], ea96[:, at]).then_inc(features_in[b], 16)
                    sp.dma_start(stage[b][:, :, EA96:EA96 + EA32], ea32[:, at]).then_inc(features_in[b], 16)
                    sp.dma_start(stage[b][:, :, EA96 + EA32:C_OTHER], ea4[:, at]).then_inc(features_in[b], 16)

                chunks(sp, fetch)

            @block.gpsimd
            def _(pool):
                st = Steps(pool, masks_ready)
                st.done(nc.gpsimd.iota(group_no[:], pattern=[[1, GROUPS]], base=0, channel_multiplier=0,
                                       allow_small_or_imprecise_dtypes=True))
                st.done(nc.gpsimd.iota(k.lane[:], pattern=[[1, P]], base=0, channel_multiplier=0,
                                       allow_small_or_imprecise_dtypes=True))
                st.done(nc.gpsimd.iota(k.node[:], pattern=[[1, COLS]], base=0, channel_multiplier=0,
                                       allow_small_or_imprecise_dtypes=True))
                st.done(nc.gpsimd.memset(every[:], 1.0))
                st.done(nc.gpsimd.memset(before[:], 1.0))
                st.done(nc.gpsimd.memset(k.ident[:], 0.0))
                st.settle()
                st.done(nc.gpsimd.affine_select(out=before[:], in_=before[:], compare_op=ALU.is_gt, fill=0.0,
                                                base=0, pattern=[[1, EP]], channel_multiplier=-1))
                st.done(nc.gpsimd.affine_select(out=k.ident[:], in_=k.ident[:], compare_op=ALU.not_equal, fill=1.0,
                                                base=0, pattern=[[-1, P]], channel_multiplier=1))
                st.settle()

                def scatter(b, i, first, last):
                    pool.wait_ge(staged[b], 2 * i + 2)
                    pool.wait_ge(blanked, 16)
                    pool.sem_inc(k.pool_ready, 1)
                    for f in range(CHUNK):
                        nc.gpsimd.indirect_dma_start(
                            k.records[:, :], bass.IndirectOffsetOnAxis(ap=index[b][:, f:f + 1], axis=0),
                            stage[b][:, f, :], None).then_inc(k.scattered[b], 16)

                chunks(pool, scatter)

            @block.tensor
            def _(pe):
                pe.wait_ge(masks_ready, 8)
                pe.wait_ge(totals_ready, 1)
                nc.tensor.matmul(ps_before, before[:], total[:], start=True, stop=True)
                nc.tensor.matmul(ps_every, every[:], total[:], start=True, stop=True).then_inc(offsets_summed, 1)

                def add_up(b, i, first, last):
                    pe.wait_ge(split_dve, 2 * (2 * i + b) + 2)
                    for f in range(CHUNK):
                        pe.wait_ge(hot_ready, (2 * i + b) * CHUNK + f + 1)
                        for j in range(3):
                            for c0, cw in CHUNKS:
                                mm = nc.tensor.matmul(ps_sums[:, c0:c0 + cw], parts[b][:, j, f], hot[f % 4][:, c0:c0 + cw],
                                                      start=first and b == 0 and f == 0 and j == 0,
                                                      stop=last and f == CHUNK - 1 and j == 2)
                        mm.then_inc(hot_used, 1)

                chunks(pe, add_up)

            @block.scalar
            def _(act):
                def split(b, i, first, last):
                    n = 2 * i + b
                    act.wait_ge(features_in[b], 48 * i + 48)
                    if not first:
                        act.wait_ge(hot_used, (n - 1) * CHUNK)
                    nc.scalar.activation(parts[b][:, 0], stage[b][:, :, 0:EA96], ACT.Copy).then_inc(split_act, 1)
                    act.wait_ge(split_dve, 2 * n + 1)
                    nc.scalar.activation(parts[b][:, 1], rest[:], ACT.Copy).then_inc(split_act, 1)

                chunks(act, split)
                act.wait_ge(hot_used, EF)
                nc.scalar.activation(k.sums_t[:], ps_sums[:, 0:COLS], ACT.Copy).then_inc(sums_out, 1)

            @block.vector
            def _(dve):
                v = nc.vector
                st = Steps(dve, sorting)
                st.done(v.memset(blank[:], 0.0))
                st.done(v.memset(ones[:], 1.0))
                st.settle()
                v.memset(blank[:, :, C_KEY:C_KEY + 1], -1.0).then_inc(blank_ready, 1)
                dve.wait_ge(masks_ready, 8)
                st.done(v.tensor_copy(k.ident_b[:], k.ident[:]))
                dve.wait_ge(ends_loaded, 32)
                st.done(v.tensor_scalar(tile_i[:], key_i[:], 7, None, ALU.arith_shift_right))
                st.done(v.tensor_copy(key_f[:], key_i[:]))
                st.done(v.tensor_copy(other_f[:], other_i[:]))
                st.settle()
                st.done(v.tensor_copy(tile_f[:], tile_i[:]))
                st.settle()
                st.done(v.scalar_tensor_tensor(local[:], tile_f[:], -float(P), key_f[:], ALU.mult, ALU.add))
                for b in range(TILES):
                    st.done(v.tensor_scalar(member[:, b], tile_f[:], float(b), None, ALU.is_equal))
                st.settle()
                for b in range(TILES):
                    st.done(v.tensor_tensor_scan(rank[:, b], ones[:], member[:, b], 0.0, ALU.mult, ALU.add))
                st.settle()
                v.tensor_copy(total[:], rank[:, :, EF - 1]).then_inc(totals_ready, 1)
                dve.wait_ge(offsets_summed, 1)
                st.done(v.tensor_scalar(cnt_i[:], ps_every, float(GROUP - 1), None, ALU.add))
                st.settle()
                st.done(v.tensor_scalar(grp_i[:], cnt_i[:], GROUP.bit_length() - 1, None, ALU.arith_shift_right))
                st.settle()
                st.done(v.tensor_copy(grp[:], grp_i[:]))
                st.settle()
                st.done(v.tensor_tensor_scan(grp_end[:], ones[:, 0:TILES], grp[:], 0.0, ALU.mult, ALU.add))
                st.settle()
                st.done(v.tensor_tensor(grp_start[:], grp_end[:], grp[:], ALU.subtract))
                st.settle()
                st.done(v.scalar_tensor_tensor(offset[:], grp_start[:], float(GROUP), ps_before, ALU.mult, ALU.add))
                st.settle()
                for b in range(TILES):
                    st.done(v.scalar_tensor_tensor(rank[:, b], rank[:, b], offset[:, b:b + 1], member[:, b],
                                                   ALU.add, ALU.mult))
                st.settle()
                st.done(v.tensor_reduce(slot_f[:], rank[:].rearrange("p b f -> p f b"), AX.X, ALU.add))
                st.settle()
                st.done(v.tensor_scalar(slot_i[:], slot_f[:], -1.0, None, ALU.add))
                st.done(v.tensor_scalar(group_tile[:], group_no[:], grp_start[:, 1:2], None, ALU.is_ge))
                st.settle()
                for b in range(2, TILES):
                    st.done(v.scalar_tensor_tensor(group_tile[:], group_no[:], grp_start[:, b:b + 1], group_tile[:],
                                                   ALU.is_ge, ALU.add))
                    st.settle()
                st.done(v.tensor_copy(k.group_tile[0:EP, :], group_tile[:]))
                st.settle()

                def fill(b, i, first, last):
                    n = 2 * i + b
                    at = bass.ds(n * CHUNK, CHUNK)
                    dve.wait_ge(features_in[b], 48 * i + 48)
                    if first:
                        st.done(v.memset(stage[b][:, :, C_KEY + 1:REC], 0.0))
                    v.tensor_copy(index[b][:], slot_i[:, at])
                    v.tensor_copy(stage[b][:, :, C_OTHER:C_OTHER + 1].bitcast(I32),
                                  other_i[:, at].unsqueeze(2)).then_inc(staged[b], 1)
                    v.tensor_copy(stage[b][:, :, C_KEY:C_KEY + 1], local[:, at].unsqueeze(2)).then_inc(staged[b], 1)
                    v.tensor_copy(other_c[b][:], other_f[:, at]).then_inc(picked, 1)
                    dve.wait_ge(split_act, 2 * n + 1)
                    v.tensor_tensor(rest[:], stage[b][:, :, 0:EA96], parts[b][:, 0], ALU.subtract).then_inc(split_dve, 1)
                    dve.wait_ge(split_act, 2 * n + 2)
                    v.tensor_tensor(parts[b][:, 2], rest[:], parts[b][:, 1], ALU.subtract).then_inc(split_dve, 1)
                    dve.wait_ge(picked, n + 1)
                    for f in range(CHUNK):
                        if not (first and b == 0 and f < 4):
                            dve.wait_ge(hot_used, n * CHUNK + f - 3)
                        v.tensor_scalar(hot[f % 4][:], k.node[0:EP, :], other_c[b][:, f:f + 1], None,
                                        ALU.is_equal).then_inc(hot_ready, 1)

                chunks(dve, fill)


def count_edges(k):
    nc = k.nc
    with ExitStack() as ctx:
        def sb(name, shape, dt=F32):
            return ctx.enter_context(nc.sbuf_tensor(name, shape, dt))

        counts = sb("counts", [P, TILES * COLS])
        record = [sb(f"record{b}", [P, SUB, REC]) for b in range(2)]
        src_f = [sb(f"src_f{b}", [P, SUB]) for b in range(2)]
        to_b = [sb(f"to_b{b}", [P, SUB, P], BF16) for b in range(2)]
        frm = [sb(f"frm{b}", [P, COLS], BF16) for b in range(2)]

        cleared = k.sem("cleared")
        rec_in = [k.sem(f"rec_in{b}") for b in range(2)]
        targets_hot = k.sem("targets_hot")
        src_float = k.sem("src_float")
        source_hot = k.sem("source_hot")
        tile_counted = k.sem("tile_counted")
        group_added = k.sem("group_added")
        counts_out = k.sem("counts_out")
        k.counts_out = counts_out

        ps = [k.psum[:, 4 * b:4 * b + 4, :] for b in range(2)]
        with nc.Block() as block:
            @block.sync
            def _(sp):
                for b in range(2):
                    sp.wait_ge(k.scattered[b], EF // CHUNK // 2 * 16 * CHUNK)
                view = k.records.rearrange("(g p t) c -> g p t c", p=P, t=SUB)
                for b in range(2):
                    sp.dma_start(record[b][:], view[b]).then_inc(rec_in[b], 16)
                with sp.Fori(1, GROUPS // 2) as i:
                    for b in range(2):
                        sp.wait_ge(tile_counted, i * 2 * SUB + (b - 1) * SUB)
                        sp.dma_start(record[b][:], k.records[bass.ds(i * 2 * GROUP + b * GROUP, GROUP), :]
                                     .rearrange("(p t) c -> p t c", p=P)).then_inc(rec_in[b], 16)
                sp.wait_ge(group_added, GROUPS)
                sp.dma_start(k.counts_d[:, :], counts[:]).then_inc(counts_out, 16)
                sp.wait_ge(counts_out, 16)

            @block.gpsimd
            def _(pool):
                nc.gpsimd.memset(counts[:], 0.0).then_inc(cleared, 1)

                def one_hots(b):
                    nc.gpsimd.tensor_copy(src_f[b][:], record[b][:, :, C_OTHER].bitcast(I32)).then_inc(src_float, 1)
                    for t in range(SUB):
                        last = nc.gpsimd.tensor_scalar(to_b[b][:, t], k.lane[:], record[b][:, t, C_KEY:C_KEY + 1], None, ALU.is_equal)
                    last.then_inc(targets_hot, 1)

                for b in range(2):
                    pool.wait_ge(rec_in[b], 16)
                    one_hots(b)
                with pool.Fori(1, GROUPS // 2) as i:
                    for b in range(2):
                        pool.wait_ge(rec_in[b], i * 16 + 16)
                        pool.sem_inc(k.pool_ready, 1)
                        one_hots(b)

            @block.tensor
            def _(pe):
                def count(b, i, first):
                    pe.wait_ge(targets_hot, i * 2 + b + 1)
                    if not first:
                        pe.wait_ge(group_added, i * 2 + b - 1)
                    for t in range(SUB):
                        pe.wait_ge(source_hot, (i * 2 + b) * SUB + t + 1)
                        for c, (c0, cw) in enumerate(CHUNKS):
                            last = nc.tensor.matmul(ps[b][:, c, 0:cw], to_b[b][:, t], frm[t % 2][:, c0:c0 + cw],
                                                    start=t == 0, stop=t == SUB - 1)
                        last.then_inc(tile_counted, 1)

                for b in range(2):
                    count(b, 0, True)
                with pe.Fori(1, GROUPS // 2) as i:
                    for b in range(2):
                        count(b, i, False)

            @block.vector
            def _(dve):
                v = nc.vector
                dve.wait_ge(cleared, 1)

                def add(b, g):
                    dve.wait_ge(tile_counted, g * SUB + SUB)
                    nt = dve.value_load(k.group_tile[0:1, bass.ds(g, 1)], min_val=0, max_val=TILES - 1)
                    here = counts[:, bass.ds(nt * COLS, COLS)]
                    v.tensor_tensor(here, here, ps[b].rearrange("p c n -> p (c n)")[:, 0:COLS],
                                    ALU.add).then_inc(group_added, 1)

                def hot(b, i, first):
                    dve.wait_ge(src_float, i * 2 + b + 1)
                    for t in range(SUB):
                        n = (i * 2 + b) * SUB + t
                        if not (first and b == 0 and t < 2):
                            dve.wait_ge(tile_counted, n - 1)
                        v.tensor_scalar(frm[t % 2][:], k.node[:], src_f[b][:, t:t + 1], None,
                                        ALU.is_equal).then_inc(source_hot, 1)

                hot(0, 0, True)
                hot(1, 0, True)
                add(0, 0)
                with dve.Fori(1, GROUPS // 2) as i:
                    hot(0, i, False)
                    dve.wait_ge(group_added, i * 2 - 1)
                    add(1, i * 2 - 1)
                    hot(1, i, False)
                    dve.wait_ge(group_added, i * 2)
                    add(0, i * 2)
                dve.wait_ge(group_added, GROUPS - 1)
                add(1, GROUPS - 1)


def copy_to(k, act, out, in_):
    if act:
        return k.nc.scalar.activation(out, in_, ACT.Copy)
    return k.nc.vector.tensor_copy(out, in_)


def add_bias(k, act, out, in_, bias, relu=False):
    if act:
        return k.nc.scalar.activation(out, in_, ACT.Relu if relu else ACT.Identity, bias=bias)
    if relu:
        return k.nc.vector.tensor_scalar(out, in_, bias, 0.0, ALU.add, ALU.max)
    return k.nc.vector.tensor_scalar(out, in_, bias, None, ALU.add)


def load(k, sem, pairs):
    with k.nc.Block() as block:
        @block.sync
        def _(sp):
            for out, in_ in pairs:
                sp.dma_start(out, in_).then_inc(sem, 16)
    return 16 * len(pairs)


def through_banks(k, count, fill, drain, needs=()):
    filled, by_act, by_dve = k.filled, k.by_act, k.by_dve
    f0, a0, d0 = k.filled_n, k.by_act_n, k.by_dve_n
    acts, dves = (count + 1) // 2, count // 2
    with k.nc.Block() as block:
        @block.tensor
        def _(pe):
            for sem, value in needs:
                pe.wait_ge(sem, value)
            for n in range(count):
                if n >= 8:
                    pe.wait_ge(*((by_dve, d0 + n // 2 - 3) if n % 2 else (by_act, a0 + n // 2 - 3)))
                fill(n, k.psum[:, n % 8]).then_inc(filled, 1)

        @block.scalar
        def _(act):
            for sem, value in needs:
                act.wait_ge(sem, value)
            for n in range(0, count, 2):
                act.wait_ge(filled, f0 + n + 1)
                drain(True, n, k.psum[:, n % 8]).then_inc(by_act, 1)

        @block.vector
        def _(dve):
            for sem, value in needs:
                dve.wait_ge(sem, value)
            for n in range(1, count, 2):
                dve.wait_ge(filled, f0 + n + 1)
                drain(False, n, k.psum[:, n % 8]).then_inc(by_dve, 1)

    k.filled_n, k.by_act_n, k.by_dve_n = f0 + count, a0 + acts, d0 + dves


def flip(k, tiles, pieces, out, needs=()):
    piece, wide = pieces
    batches = [(t, j, min(4, wide - j)) for t in range(tiles) for j in range(0, wide, 4)]

    def fill(n, bank):
        t, j, w = batches[n]
        for i in range(w):
            x = piece(t, j + i)
            last = k.nc.tensor.transpose(bank[0:x.shape[1], i * P:(i + 1) * P], x, k.ident[:])
        return last

    def drain(act, n, bank):
        t, j, w = batches[n]
        o = out(j, w, t)
        return copy_to(k, act, o, bank[0:o.shape[0], 0:w * P].rearrange("p (j c) -> p j c", j=w))

    through_banks(k, len(batches), fill, drain, needs)


def features_out(k, outs, terms, finish, needs=()):
    def fill(n, bank):
        j, (c0, cw) = n // len(CHUNKS), CHUNKS[n % len(CHUNKS)]
        ts = terms(j)
        for i, (w, x) in enumerate(ts):
            last = k.nc.tensor.matmul(bank[:, 0:cw], w, x[:, c0:c0 + cw], start=i == 0, stop=i == len(ts) - 1)
        return last

    def drain(act, n, bank):
        j, (c0, cw) = n // len(CHUNKS), CHUNKS[n % len(CHUNKS)]
        return finish(act, j, slice(c0, c0 + cw), bank[:, 0:cw])

    through_banks(k, outs * len(CHUNKS), fill, drain, needs)


def rows_out(k, terms, finish, needs=()):
    def fill(n, bank):
        ts = terms(n)
        for i, (x, w, at) in enumerate(ts):
            last = k.nc.tensor.matmul(bank[:, at], x, w, start=i == 0 or ts[i - 1][2] != at,
                                      stop=i == len(ts) - 1 or ts[i + 1][2] != at)
        return last

    through_banks(k, TILES, fill, lambda act, n, bank: finish(act, n, bank), needs)


def normalize(k, mean_of, x, pieces, width, scale=None, shift=None, plus=None, before=None, needs=()):
    nc = k.nc
    chunks = [(c, min(BANK, mean_of - c)) for c in range(0, mean_of, BANK)]
    with ExitStack() as ctx:
        k.names += 1
        stats = ctx.enter_context(nc.sbuf_tensor(f"stats{k.names}", [P, pieces, len(chunks), 6], F32))
        mv = ctx.enter_context(nc.sbuf_tensor(f"mv{k.names}", [P, pieces, 2], F32))
        root = ctx.enter_context(nc.sbuf_tensor(f"root{k.names}", [P, pieces], F32))
        base, r0 = k.norm_n, k.root_n
        with nc.Block() as block:
            @block.scalar
            def _(act):
                act.wait_ge(k.variances, r0 + 1)
                nc.scalar.activation(root[:], mv[:, :, 1], ACT.Sqrt).then_inc(k.roots, 1)

            @block.vector
            def _(dve):
                v = nc.vector
                for sem, value in needs:
                    dve.wait_ge(sem, value)
                st = Steps(dve, k.norm, base)
                if before:
                    before(v, st)
                    st.settle()
                for t in range(pieces):
                    for c, (c0, cw) in enumerate(chunks):
                        st.done(v.bn_stats(stats[:, t, c], x[:, t, c0:c0 + cw]))
                st.settle()
                for t in range(pieces):
                    st.done(v.bn_aggr(mv[:, t], stats[:, t]))
                st.settle()
                v.tensor_scalar(mv[:, :, 1], mv[:, :, 1], EPS, None, ALU.add).then_inc(k.variances, 1)
                dve.wait_ge(k.roots, r0 + 1)
                st.done(v.reciprocal(root[:], root[:]))
                st.settle()
                for t in range(pieces):
                    st.done(v.tensor_scalar(x[:, t, 0:width], x[:, t, 0:width], mv[:, t, 0:1], root[:, t:t + 1],
                                            ALU.subtract, ALU.mult))
                for other, op in ((scale, ALU.mult), (shift, ALU.add)):
                    if other is not None:
                        st.settle()
                        if other.shape[1] == pieces:
                            for t in range(pieces):
                                st.done(v.tensor_scalar(x[:, t, 0:width], x[:, t, 0:width], other[:, t:t + 1], None, op))
                        else:
                            st.done(v.tensor_tensor(x[:], x[:], other[:][:, None, :].broadcast_to([P, pieces, width]), op))
                if plus is not None:
                    st.settle()
                    st.done(v.tensor_tensor(x[:], x[:], plus[:], ALU.add))
                st.settle()
                k.norm_n += st.n
        k.root_n += 1


def row_of(ap, n=D):
    return ap.rearrange("(o d) -> o d", o=1)


def spread(ap, n=D):
    return row_of(ap).broadcast_to([P, n])


def columns(ap):
    return ap.rearrange("(t p) -> p t", p=P)


def weight(ap):
    return ap.rearrange("(t p) j -> p t j", p=P)


def mlp_layer(k):
    nc, a = k.nc, k.a
    with ExitStack() as ctx:
        def sb(name, shape, dt=F32):
            return ctx.enter_context(nc.sbuf_tensor(name, shape, dt))

        w1, w1e, w2, w3 = sb("w1", [P, 4, 1024]), sb("w1e", [EA96, 1024]), sb("w2", [P, 8, 1024]), sb("w3", [P, 8, D])
        b1, b2, b3 = sb("b1", [P, 8]), sb("b2", [P, 8]), sb("b3", [1, D])
        g, be = sb("g0", [P, D]), sb("be0", [P, D])
        loaded = k.sem("mlp_loaded")
        n = load(k, loaded, [
            (w1[:], weight(a["L0_gnn_W1"][0:D, :])), (w1e[:], a["L0_gnn_W1"][D:D + EA96, :]),
            (b1[:], columns(a["L0_gnn_b1"])), (w2[:], weight(a["L0_gnn_W2"])), (b2[:], columns(a["L0_gnn_b2"])),
            (w3[:], weight(a["L0_gnn_W3"])), (b3[:], row_of(a["L0_gnn_b3"])),
            (g[:], spread(a["L0_gnn_gamma"])), (be[:], spread(a["L0_gnn_beta"]))])
        needs = [(loaded, n)]
        h1 = sb("h1", [P, 8, COLS])
        with ExitStack() as inner:
            xt = inner.enter_context(nc.sbuf_tensor("xt0", [P, 4, COLS], F32))
            flip(k, TILES, (lambda t, j: k.x[:, t, j * P:(j + 1) * P], 4),
                 lambda j, w, t: xt[:, j:j + w, t * P:(t + 1) * P], [(k.x_loaded, 32)])
            features_out(k, 8, lambda j: [(w1[:, i, j * P:(j + 1) * P], xt[:, i]) for i in range(4)]
                         + [(w1e[:, j * P:(j + 1) * P], k.sums_t)],
                         lambda act, j, at, ps: add_bias(k, act, h1[:, j, at], ps, b1[:, j:j + 1], relu=True), needs)
        h2 = sb("h2", [P, 8, COLS])
        features_out(k, 8, lambda j: [(w2[:, i, j * P:(j + 1) * P], h1[:, i]) for i in range(8)],
                     lambda act, j, at, ps: add_bias(k, act, h2[:, j, at], ps, b2[:, j:j + 1], relu=True))
        y = h1[:, 0:4].rearrange("p a b -> p (a b)").rearrange("p (t d) -> p t d", d=D)
        rows_out(k, lambda t: [(h2[:, i, t * P:(t + 1) * P], w3[:, i], slice(0, D)) for i in range(8)]
                 + [(k.ones[0:1, :], b3[:], slice(0, D))],
                 lambda act, t, ps: copy_to(k, act, y[:, t], ps))
        normalize(k, D, y, TILES, D, scale=g, shift=be, plus=k.x)

        def keep(v, st):
            st.done(v.tensor_copy(k.x[:], y))

        normalize(k, D, k.x, TILES, D, before=keep)


def split3(k, v, st, src, parts, rest):
    st.done(v.tensor_copy(parts[0], src))
    st.settle()
    st.done(v.tensor_tensor(rest, src, parts[0], ALU.subtract))
    st.settle()
    st.done(v.tensor_copy(parts[1], rest))
    st.settle()
    st.done(v.tensor_tensor(parts[2], rest, parts[1], ALU.subtract))
    st.settle()


def tensor_nodes(k, ctx):
    nc, a = k.nc, k.a
    outer = ctx

    def keep(name, shape, dt=F32):
        return outer.enter_context(nc.sbuf_tensor(name, shape, dt))

    k.p1_parts = keep("p1_parts", [P, TILES * 3 * 384], BF16)
    k.ph_parts = keep("ph_parts", [P, TILES * 3 * P], BF16)
    k.hid_f = keep("hid_f", [EA32, P])
    k.hid_s = keep("hid_s", [P, P])
    k.mix = keep("mix", [P, 2, 2, D], BF16)
    with ExitStack() as ctx:
        def sb(name, shape, dt=F32):
            return ctx.enter_context(nc.sbuf_tensor(name, shape, dt))

        wp0, wp1, wn0, wn1 = (sb(n, [P, P]) for n in ("wp0", "wp1", "wn0", "wn1"))
        bp0, bn0 = sb("bp0", [P, 1]), sb("bn0", [1, P])
        wg1, wg2, bg1, bg2 = sb("wg1", [P, 2, 256]), sb("wg2", [P, 2, 256]), sb("bg1", [P, 2]), sb("bg2", [P, 2])
        ws1 = sb("ws1", [P, 3, 32])
        wsum = sb("wsum", [P, P])
        mixf = sb("mixf", [P, 2, D])
        part = sb("part", [P, 3, 2, D], BF16)
        rest = sb("rest", [P, 2, D])
        xp = sb("xp", [P, 4, COLS])
        p0 = sb("p0", [P, COLS])
        p1 = sb("p1", [P, TILES, D])
        loaded = k.sem("node_loaded")
        pairs = [(wp0[:], a["L1_gnn_W_pre0"]), (wp1[:], a["L1_gnn_W_pre1"]), (wn0[:], a["L1_gnn_W_nd0"]),
                 (wn1[:], a["L1_gnn_W_nd1"]), (bp0[:], columns(a["L1_gnn_b_pre0"])), (bn0[:], row_of(a["L1_gnn_b_nd0"])),
                 (wg1[:], weight(a["L1_gnn_W_g1"])), (wg2[:], weight(a["L1_gnn_W_g2"])),
                 (bg1[:], columns(a["L1_gnn_b_g1"])), (bg2[:], columns(a["L1_gnn_b_g2"])),
                 (ws1[:], weight(a["L1_gnn_W_s1"]))]
        for r in range(4):
            pairs.append((mixf[32 * r:32 * r + 32, 0], a["L1_gnn_W_f2"]))
            pairs.append((mixf[32 * r:32 * r + 32, 1], a["L1_gnn_W_s2"]))
        pairs.append((k.hid_f[:, 0:32], a["L1_gnn_W_f1"]))
        pairs.append((k.hid_f[:, 64:96], a["L1_gnn_W_f1"]))
        n = load(k, loaded, pairs)
        steps, masked = k.sem("node_steps"), k.sem("node_masked")

        with nc.Block() as block:
            @block.gpsimd
            def _(pool):
                st = Steps(pool, masked)
                st.done(nc.gpsimd.memset(k.hid_f[:, 32:64], 0.0))
                st.done(nc.gpsimd.memset(k.hid_f[:, 96:128], 0.0))
                st.done(nc.gpsimd.memset(k.hid_s[:], 0.0))
                st.done(nc.gpsimd.memset(wsum[:], 0.0))
                st.done(nc.gpsimd.memset(k.mix[:], 0.0))

            @block.vector
            def _(dve):
                v = nc.vector
                dve.wait_ge(loaded, n)
                dve.wait_ge(masked, 5)
                st = Steps(dve, steps)
                for r in (32, 96):
                    st.done(v.tensor_tensor(wsum[:, r:r + 32], ws1[:, 0], ws1[:, 1], ALU.add))
                    st.done(v.tensor_scalar(k.hid_s[:, r:r + 32], ws1[:, 2], 1.0 / 3.0, None, ALU.mult))
                st.done(v.tensor_scalar(mixf[:, 1, 384:512], mixf[:, 1, 384:512], 3.0 ** -0.5, None, ALU.mult))
                st.settle()
                split3(k, v, st, mixf[:], [part[:, i] for i in range(3)], rest[:])
                for r, first, second in ((0, 0, None), (1, 0, 1), (2, 0, 1), (3, 2, None)):
                    rows = slice(32 * r, 32 * r + 32)
                    st.done(v.tensor_copy(k.mix[rows, :, 0], part[rows, first]))
                    if second:
                        st.done(v.tensor_copy(k.mix[rows, :, 1], part[rows, second]))
                st.settle()

        def planar(t, j):
            return k.x[:, t, 0:P] if j == 0 else k.x[:, t, P + j - 1:D:3]

        flip(k, TILES, (planar, 4), lambda j, w, t: xp[:, j:j + w, t * P:(t + 1) * P])
        features_out(k, 1, lambda j: [(wp0[:], xp[:, 0])],
                     lambda act, j, at, ps: add_bias(k, act, p0[:, at], ps, bp0[:, 0:1]))
        rows_out(k, lambda t: [(xp[:, 1 + m, t * P:(t + 1) * P], wp1[:], slice(m * P, m * P + P)) for m in range(3)]
                 + [(p0[:, t * P:(t + 1) * P], wsum[:], slice(384, 512))],
                 lambda act, t, ps: copy_to(k, act, p1[:, t], ps))
        s2 = k.sem("node_split")
        k.tables = k.sem("tables")
        rest2 = sb("rest2", [P, TILES, 384])
        with nc.Block() as block:
            @block.sync
            def _(sp):
                sp.dma_start(k.p1_d.rearrange("(t p) c -> p t c", p=P), p1[:, :, 0:384]).then_inc(k.tables, 16)
                sp.wait_ge(k.tables, 16)

            @block.vector
            def _(dve):
                st = Steps(dve, s2)
                pv = k.p1_parts[:].rearrange("p (t i c) -> p t i c", t=TILES, i=3)
                split3(k, nc.vector, st, p1[:, :, 0:384], [pv[:, :, i] for i in range(3)], rest2[:])
                pv = k.ph_parts[:].rearrange("p (t i c) -> p t i c", t=TILES, i=3)
                split3(k, nc.vector, st, p1[:, :, 384:512], [pv[:, :, i] for i in range(3)], rest2[:, :, 0:P])

        n1 = sb("n1", [P, COLS])
        hid = sb("hid", [P, 2, COLS])
        gate = sb("gate", [P, COLS])
        s3, s4 = k.sem("norms_summed"), k.sem("norms_rooted")
        with nc.Block() as block:
            @block.scalar
            def _(act):
                act.wait_ge(s3, 4)
                nc.scalar.activation(n1[:], n1[:], ACT.Sqrt, scale=1.0 / 3.0).then_inc(s4, 1)

            @block.vector
            def _(dve):
                v = nc.vector
                st = Steps(dve, s3)
                st.done(v.tensor_tensor(hid[:, 0], xp[:, 1], xp[:, 1], ALU.mult))
                st.done(v.tensor_tensor(hid[:, 1], xp[:, 2], xp[:, 2], ALU.mult))
                st.settle()
                v.tensor_tensor(n1[:], hid[:, 0], hid[:, 1], ALU.add)
                st.done(v.tensor_tensor(gate[:], xp[:, 3], xp[:, 3], ALU.mult))
                st.settle()
                st.done(v.tensor_tensor(n1[:], n1[:], gate[:], ALU.add))
        sig = sb("sig", [P, 2, COLS])
        features_out(k, 2, lambda j: [(wg1[:, 0, j * P:(j + 1) * P], xp[:, 0]), (wg1[:, 1, j * P:(j + 1) * P], n1[:])],
                     lambda act, j, at, ps: add_bias(k, act, hid[:, j, at], ps, bg1[:, j:j + 1]))
        s5, s6 = k.sem("sigmoid_done"), k.sem("silu_done")
        with nc.Block() as block:
            @block.scalar
            def _(act):
                nc.scalar.activation(sig[:], hid[:], ACT.Sigmoid).then_inc(s5, 1)

            @block.vector
            def _(dve):
                dve.wait_ge(s5, 1)
                nc.vector.tensor_tensor(hid[:], hid[:], sig[:], ALU.mult).then_inc(s6, 1)
        g0 = sig[:, 0]
        features_out(k, 2, lambda j: [(wg2[:, i, j * P:(j + 1) * P], hid[:, i]) for i in range(2)],
                     lambda act, j, at, ps: add_bias(k, act, (gate if j else g0)[:, at], ps, bg2[:, j:j + 1]))
        s7 = k.sem("gated")
        with nc.Block() as block:
            @block.vector
            def _(dve):
                nc.vector.tensor_tensor(xp[:, 1:4], xp[:, 1:4], gate[:][:, None, :].broadcast_to([P, 3, COLS]),
                                        ALU.mult).then_inc(s7, 1)
        xs = sb("xs", [P, TILES, D])
        rows_out(k, lambda t: [(g0[:, t * P:(t + 1) * P], wn0[:], slice(0, P)), (k.ones[0:1, :], bn0[:], slice(0, P))]
                 + [(xp[:, 1 + m, t * P:(t + 1) * P], wn1[:], slice((1 + m) * P, (2 + m) * P)) for m in range(3)],
                 lambda act, t, ps: copy_to(k, act, xs[:, t], ps))
        with nc.Block() as block:
            @block.sync
            def _(sp):
                sp.dma_start(k.xs_d.rearrange("(t p) c -> p t c", p=P), xs[:]).then_inc(k.tables, 16)
                sp.wait_ge(k.tables, 32)


def paired(engine, front, back):
    rounds = GROUPS // 2
    front(0, 0, True)
    front(1, 0, True)
    back(0, 0, True)
    front(0, 1, False)
    back(1, 0, True)
    front(1, 1, False)
    back(0, 1, False)
    with engine.Fori(2, rounds) as i:
        front(0, i, False)
        back(1, i - 1, False)
        front(1, i, False)
        back(0, i, False)
    back(1, rounds - 1, False)


def edge_hidden(k):
    nc = k.nc
    with ExitStack() as ctx:
        def sb(name, shape, dt=F32):
            return ctx.enter_context(nc.sbuf_tensor(name, shape, dt))

        record = [sb(f"rec_h{b}", [P, SUB, REC]) for b in range(2)]
        source = [sb(f"source{b}", [P, SUB, 384]) for b in range(2)]
        hot = [sb(f"hot{b}", [P, SUB, P], BF16) for b in range(2)]
        hot_t = [sb(f"hot_t{b}", [P, GROUP], BF16) for b in range(2)]
        attr_t = [sb(f"attr_t{b}", [EA32, GROUP]) for b in range(2)]
        prod = [sb(f"prod{b}", [P, 3, P]) for b in range(2)]
        ip = [sb(f"ip{b}", [P, SUB, P]) for b in range(2)]
        ip_t = sb("ip_t", [P, GROUP])
        size = sb("size", [64, GROUP])
        hidden = sb("hidden", [64, GROUP])
        parts = [sb(f"parts{b}", [64, 3, GROUP], BF16) for b in range(2)]
        half = sb("half", [64, 1])

        rec_in = [k.sem(f"h_rec_in{b}") for b in range(2)]
        source_in = [k.sem(f"h_source_in{b}") for b in range(2)]
        stored = [k.sem(f"h_stored{b}") for b in range(2)]
        hot_ready, flipped, copied = k.sem("h_hot"), k.sem("h_flipped"), k.sem("h_copied")
        target_out, multiplied, summed = k.sem("h_target"), k.sem("h_multiplied"), k.sem("h_summed")
        ip_flipped, ip_copied = k.sem("h_ip_flipped"), k.sem("h_ip_copied")
        hidden_in, soft, divided = k.sem("h_in"), k.sem("h_soft"), k.sem("h_divided")
        halved = k.sem("h_halved")
        k.stored = stored

        ps_hot = k.psum[:, 0].bitcast(BF16)[:, 0:GROUP]
        ps_attr = k.psum[0:EA32, 1]
        ps_target = [k.psum[:, 2 + b, 0:384] for b in range(2)]
        ps_ip, ps_hid = k.psum[:, 4], k.psum[:, 5]

        with nc.Block() as block:
            @block.sync
            def _(sp):
                def front(b, i, first):
                    if not first:
                        sp.wait_ge(flipped, 2 * i + b - 1)
                        sp.sem_inc(k.sp_ready, 1)
                        sp.wait_ge(source_in[b], 64 * i)
                    sp.dma_start(record[b][:], k.records[bass.ds((2 * i + b) * GROUP, GROUP), :]
                                 .rearrange("(p t) c -> p t c", p=P)).then_inc(rec_in[b], 16)

                def back(b, i, first):
                    sp.wait_ge(divided, 5 * (2 * i + b) + 5)
                    for blk, part in enumerate((2, 0, 1, 0)):
                        sp.dma_start(k.stack_d[bass.ds((2 * i + b) * 256 + blk * 64, 64), :],
                                     parts[b][:, part]).then_inc(stored[b], 16)

                paired(sp, front, back)

            @block.gpsimd
            def _(pool):
                nc.gpsimd.memset(half[:], 0.5).then_inc(halved, 1)

                def gather(b, i, first):
                    pool.wait_ge(rec_in[b], 16 * i + 16)
                    if not first:
                        pool.wait_ge(multiplied, (2 * i + b - 1) * SUB)
                    pool.wait_ge(k.tables, 32)
                    pool.sem_inc(k.pool_ready, 1)
                    for t in range(SUB):
                        nc.gpsimd.indirect_dma_start(
                            source[b][:, t, :], None, k.p1_d[:, :],
                            bass.IndirectOffsetOnAxis(ap=record[b][:, t, C_OTHER:C_OTHER + 1].bitcast(I32), axis=0)
                        ).then_inc(source_in[b], 16)

                gather(0, 0, True)
                gather(1, 0, True)
                with pool.Fori(1, GROUPS // 2) as i:
                    gather(0, i, False)
                    gather(1, i, False)

            @block.tensor
            def _(pe):
                def front(b, i, first):
                    g = 2 * i + b
                    pe.wait_ge(hot_ready, g + 1)
                    if not (first and b == 0):
                        pe.wait_ge(copied, 2 * g)
                    for t in range(SUB):
                        nc.tensor.transpose(ps_hot[:, t * P:(t + 1) * P], hot[b][:, t], k.ident_b[:])
                    for t in range(SUB):
                        last = nc.tensor.transpose(ps_attr[:, t * P:(t + 1) * P], record[b][:, t, EA96:EA96 + EA32],
                                                   k.ident[:])
                    last.then_inc(flipped, 1)
                    pe.wait_ge(copied, 2 * g + 2)
                    nt = pe.value_load(k.group_tile[0:1, bass.ds(g, 1)], min_val=0, max_val=TILES - 1)
                    for t in range(SUB):
                        if not (first and b == 0 and t < 2):
                            pe.wait_ge(multiplied, g * SUB + t - 1)
                        for j in range(3):
                            last = nc.tensor.matmul(ps_target[t % 2], hot_t[b][:, t * P:(t + 1) * P],
                                                    k.p1_parts[:, bass.ds(nt * (3 * 384) + j * 384, 384)],
                                                    start=j == 0, stop=j == 2)
                        last.then_inc(target_out, 1)

                def back(b, i, first):
                    g = 2 * i + b
                    pe.wait_ge(summed, g * SUB + SUB)
                    if not (first and b == 0):
                        pe.wait_ge(ip_copied, g)
                        pe.wait_ge(divided, 5 * g - 4)
                    for t in range(SUB):
                        last = nc.tensor.transpose(ps_ip[:, t * P:(t + 1) * P], ip[b][:, t], k.ident[:])
                    last.then_inc(ip_flipped, 1)
                    nt = pe.value_load(k.group_tile[0:1, bass.ds(g, 1)], min_val=0, max_val=TILES - 1)
                    nc.tensor.matmul(ps_hid, k.hid_f[:], attr_t[b][:], start=True, stop=False)
                    for j in range(3):
                        nc.tensor.matmul(ps_hid, k.ph_parts[:, bass.ds(nt * (3 * P) + j * P, P)], hot_t[b][:],
                                         start=False, stop=False)
                    pe.wait_ge(ip_copied, g + 1)
                    nc.tensor.matmul(ps_hid, k.hid_s[:], ip_t[:], start=False, stop=True).then_inc(hidden_in, 1)

                paired(pe, front, back)

            @block.scalar
            def _(act):
                s = nc.scalar
                act.wait_ge(halved, 1)

                def front(b, i, first):
                    g = 2 * i + b
                    act.wait_ge(flipped, g + 1)
                    if not first:
                        act.wait_ge(hidden_in, g - 1)
                    s.activation(hot_t[b][:], ps_hot, ACT.Copy).then_inc(copied, 1)
                    s.activation(attr_t[b][:], ps_attr, ACT.Copy).then_inc(copied, 1)

                def back(b, i, first):
                    g = 2 * i + b
                    act.wait_ge(ip_flipped, g + 1)
                    if not (first and b == 0):
                        act.wait_ge(hidden_in, g)
                        act.wait_ge(divided, 5 * g - 4)
                    s.activation(ip_t[:], ps_ip, ACT.Copy).then_inc(ip_copied, 1)
                    act.wait_ge(hidden_in, g + 1)
                    s.activation(size[:], ps_hid[0:64], ACT.Abs).then_inc(soft, 1)
                    act.wait_ge(soft, 3 * g + 1)
                    s.activation(size[:], size[:], ACT.Exp, scale=-1.0).then_inc(soft, 1)
                    act.wait_ge(soft, 3 * g + 2)
                    s.activation(size[:], size[:], ACT.Ln, scale=0.5, bias=half[:, 0:1]).then_inc(soft, 1)

                paired(act, front, back)

            @block.vector
            def _(dve):
                v = nc.vector

                def front(b, i, first):
                    g = 2 * i + b
                    dve.wait_ge(rec_in[b], 16 * i + 16)
                    if not first:
                        dve.wait_ge(flipped, g - 1)
                    for t in range(SUB):
                        last = v.tensor_scalar(hot[b][:, t], k.lane[:], record[b][:, t, C_KEY:C_KEY + 1], None,
                                               ALU.is_equal)
                    last.then_inc(hot_ready, 1)
                    dve.wait_ge(source_in[b], 64 * i + 64)
                    if not first:
                        dve.wait_ge(ip_flipped, g - 1)
                    for t in range(SUB):
                        n = g * SUB + t
                        dve.wait_ge(target_out, n + 1)
                        if not (first and b == 0 and t < 2):
                            dve.wait_ge(summed, n - 1)
                        v.tensor_tensor(prod[t % 2][:], ps_target[t % 2].rearrange("p (m u) -> p m u", m=3),
                                        source[b][:, t].rearrange("p (m u) -> p m u", m=3),
                                        ALU.mult).then_inc(multiplied, 1)
                        dve.wait_ge(multiplied, n + 1)
                        v.tensor_reduce(ip[b][:, t], prod[t % 2][:].rearrange("p m u -> p u m"), AX.X,
                                        ALU.add).then_inc(summed, 1)

                def back(b, i, first):
                    g = 2 * i + b
                    dve.wait_ge(soft, 3 * g + 3)
                    if not (first and b == 0):
                        dve.wait_ge(divided, 5 * g)
                    v.scalar_tensor_tensor(hidden[:], ps_hid[0:64], 0.0, size[:], ALU.max, ALU.add).then_inc(divided, 1)
                    if not first:
                        dve.wait_ge(stored[b], 64 * i)
                    dve.wait_ge(divided, 5 * g + 1)
                    v.tensor_copy(parts[b][:, 0], hidden[:]).then_inc(divided, 1)
                    dve.wait_ge(divided, 5 * g + 2)
                    v.tensor_tensor(hidden[:], hidden[:], parts[b][:, 0], ALU.subtract).then_inc(divided, 1)
                    dve.wait_ge(divided, 5 * g + 3)
                    v.tensor_copy(parts[b][:, 1], hidden[:]).then_inc(divided, 1)
                    dve.wait_ge(divided, 5 * g + 4)
                    v.tensor_tensor(parts[b][:, 2], hidden[:], parts[b][:, 1], ALU.subtract).then_inc(divided, 1)

                paired(dve, front, back)


def edge_messages(k, summed_x):
    nc = k.nc
    with ExitStack() as ctx:
        def sb(name, shape, dt=F32):
            return ctx.enter_context(nc.sbuf_tensor(name, shape, dt))

        record = [sb(f"rec_m{b}", [P, SUB, REC]) for b in range(2)]
        source = [sb(f"xsrc{b}", [P, SUB, D]) for b in range(2)]
        stack = [sb(f"stack{b}", [P, 2, GROUP], BF16) for b in range(2)]
        hot = [sb(f"mhot{b}", [P, SUB, P]) for b in range(2)]
        left = [sb(f"left{b}", [P, 4, P]) for b in range(2)]
        w = [sb(f"weights{b}", [P, 4, P]) for b in range(2)]
        z = [sb(f"z{b}", [P, P]) for b in range(2)]
        vz = [sb(f"vz{b}", [P, P]) for b in range(2)]
        message = [sb(f"message{b}", [P, 4, P]) for b in range(2)]

        rec_in = [k.sem(f"m_rec_in{b}") for b in range(2)]
        stack_in = [k.sem(f"m_stack_in{b}") for b in range(2)]
        source_in = [k.sem(f"m_source_in{b}") for b in range(2)]
        cleared, hot_ready, weights_in, left_out = k.sem("m_cleared"), k.sem("m_hot"), k.sem("m_weights"), k.sem("m_left")
        work, message_ready, sent = k.sem("m_work"), k.sem("m_ready"), k.sem("m_sent")
        outer_done, added = k.sem("m_outer"), k.sem("m_added")

        ps_f = [k.psum[:, b].rearrange("p (q u) -> p q u", q=4) for b in range(2)]
        ps_s = [k.psum[:, 2 + b].rearrange("p (q u) -> p q u", q=4) for b in range(2)]
        ps_sum = [k.psum[:, 4 + b] for b in range(2)]
        WORK = 8

        with nc.Block() as block:
            @block.sync
            def _(sp):
                for b in range(2):
                    sp.wait_ge(k.stored[b], GROUPS // 2 * 64)

                def fetch(b, i, first):
                    if not first:
                        sp.wait_ge(sent, (2 * i + b - 1) * SUB)
                        sp.sem_inc(k.sp_ready, 1)
                        sp.wait_ge(source_in[b], 64 * i)
                    sp.dma_start(record[b][:], k.records[bass.ds((2 * i + b) * GROUP, GROUP), :]
                                 .rearrange("(p t) c -> p t c", p=P)).then_inc(rec_in[b], 16)
                    for blk in range(4):
                        sp.dma_start(stack[b][32 * blk:32 * blk + 32],
                                     k.stack_d[bass.ds((2 * i + b) * 256 + blk * 64, 64), :]
                                     .rearrange("(s r) c -> r s c", s=2)).then_inc(stack_in[b], 16)

                fetch(0, 0, True)
                fetch(1, 0, True)
                with sp.Fori(1, GROUPS // 2) as i:
                    fetch(0, i, False)
                    fetch(1, i, False)

            @block.gpsimd
            def _(pool):
                nc.gpsimd.memset(summed_x[:], 0.0).then_inc(cleared, 1)

                def gather(b, i, first):
                    pool.wait_ge(rec_in[b], 16 * i + 16)
                    if not first:
                        pool.wait_ge(message_ready, (2 * i + b - 1) * SUB)
                    pool.wait_ge(k.tables, 32)
                    pool.sem_inc(k.pool_ready, 1)
                    for t in range(SUB):
                        nc.gpsimd.indirect_dma_start(
                            source[b][:, t, :], None, k.xs_d[:, :],
                            bass.IndirectOffsetOnAxis(ap=record[b][:, t, C_OTHER:C_OTHER + 1].bitcast(I32), axis=0)
                        ).then_inc(source_in[b], 16)

                gather(0, 0, True)
                gather(1, 0, True)
                with pool.Fori(1, GROUPS // 2) as i:
                    gather(0, i, False)
                    gather(1, i, False)

            @block.tensor
            def _(pe):
                def mix(b, i, t, first):
                    n = (2 * i + b) * SUB + t
                    if not (first and b == 0 and t < 2):
                        pe.wait_ge(outer_done, n - 1)
                    for ps, kind in ((ps_f, 0), (ps_s, 1)):
                        for j in range(2):
                            last = nc.tensor.matmul(ps[t % 2].rearrange("p q u -> p (q u)"),
                                                    stack[b][:, kind, t * P:(t + 1) * P], k.mix[:, kind, j],
                                                    start=j == 0, stop=j == 1)
                    last.then_inc(weights_in, 1)

                def send(b, i, t, first):
                    n = (2 * i + b) * SUB + t
                    if t == 0:
                        pe.wait_ge(hot_ready, 2 * i + b + 1)
                        if not first:
                            pe.wait_ge(added, 2 * i + b - 1)
                    pe.wait_ge(message_ready, n + 1)
                    nc.tensor.matmul(ps_sum[b], hot[b][:, t], message[t % 2][:].rearrange("p q u -> p (q u)"),
                                     start=t == 0, stop=t == SUB - 1).then_inc(sent, 1)

                def group(b, i, first):
                    pe.wait_ge(stack_in[b], 64 * i + 64)
                    for t in range(SUB):
                        mix(b, i, t, first)
                        if t > 0:
                            send(b, i, t - 1, first)
                    send(b, i, SUB - 1, first)

                group(0, 0, True)
                group(1, 0, True)
                with pe.Fori(1, GROUPS // 2) as i:
                    group(0, i, False)
                    group(1, i, False)

            @block.scalar
            def _(act):
                def left_factor(b, i, first):
                    act.wait_ge(rec_in[b], 16 * i + 16)
                    for t in range(SUB):
                        n = (2 * i + b) * SUB + t
                        act.wait_ge(weights_in, n + 1)
                        if not (first and b == 0 and t < 2):
                            act.wait_ge(outer_done, n - 1)
                        nc.scalar.activation(left[t % 2][:, 0:4:2], ps_f[t % 2][:, 0:4:2], ACT.Copy,
                                             scale=record[b][:, t, EA96 + EA32:EA96 + EA32 + 1]).then_inc(left_out, 1)
                        nc.scalar.activation(left[t % 2][:, 1:4:2], ps_f[t % 2][:, 1:4:2], ACT.Copy).then_inc(left_out, 1)

                left_factor(0, 0, True)
                left_factor(1, 0, True)
                with act.Fori(1, GROUPS // 2) as i:
                    left_factor(0, i, False)
                    left_factor(1, i, False)

            @block.vector
            def _(dve):
                v = nc.vector
                dve.wait_ge(cleared, 1)

                def tile(b, i, t, first):
                    n = (2 * i + b) * SUB + t
                    st = Steps(dve, work, n * WORK)
                    x0 = source[b][:, t, 0:P]
                    x1 = source[b][:, t, P:D].rearrange("p (m u) -> p m u", m=3)
                    sh = [record[b][:, t, EA96 + EA32 + 1 + m:EA96 + EA32 + 2 + m] for m in range(3)]
                    wt, zt, vt, mt = w[t % 2], z[t % 2], vz[t % 2], message[t % 2]
                    if not (first and b == 0 and t < 2):
                        dve.wait_ge(message_ready, n - 1)
                    st.done(v.tensor_scalar(zt[:], x1[:, 0], sh[0], None, ALU.mult))
                    dve.wait_ge(left_out, 2 * n + 2)
                    v.tensor_tensor(wt[:], left[t % 2][:], ps_s[t % 2], ALU.mult).then_inc(outer_done, 1)
                    st.settle()
                    st.done(v.scalar_tensor_tensor(zt[:], x1[:, 1], sh[1], zt[:], ALU.mult, ALU.add))
                    dve.wait_ge(outer_done, n + 1)
                    st.done(v.tensor_tensor(vt[:], wt[:, 1], x0, ALU.mult))
                    if not (first and b == 0 and t < 2):
                        dve.wait_ge(sent, n - 1)
                    st.settle()
                    st.done(v.scalar_tensor_tensor(zt[:], x1[:, 2], sh[2], zt[:], ALU.mult, ALU.add))
                    st.done(v.tensor_tensor(mt[:, 1:4], x1, wt[:, 2:3].broadcast_to([P, 3, P]), ALU.mult))
                    st.done(v.tensor_tensor(mt[:, 0], wt[:, 0], x0, ALU.mult))
                    st.settle()
                    st.done(v.tensor_tensor(zt[:], zt[:], wt[:, 3], ALU.mult))
                    for m in range(3):
                        last = v.scalar_tensor_tensor(mt[:, 1 + m], vt[:], sh[m], mt[:, 1 + m], ALU.mult, ALU.add)
                    st.done(last)
                    st.settle()
                    v.tensor_tensor(mt[:, 0], mt[:, 0], zt[:], ALU.add).then_inc(message_ready, 1)
                    assert st.n == WORK

                def add(b, i):
                    g = 2 * i + b
                    dve.wait_ge(sent, g * SUB + SUB)
                    nt = dve.value_load(k.group_tile[0:1, bass.ds(g, 1)], min_val=0, max_val=TILES - 1)
                    here = summed_x[:, bass.ds(nt * D, D)]
                    v.tensor_tensor(here, here, ps_sum[b], ALU.add).then_inc(added, 1)

                def front(b, i, first):
                    dve.wait_ge(rec_in[b], 16 * i + 16)
                    if not first:
                        dve.wait_ge(sent, (2 * i + b - 1) * SUB)
                    for t in range(SUB):
                        last = v.tensor_scalar(hot[b][:, t], k.lane[:], record[b][:, t, C_KEY:C_KEY + 1], None,
                                               ALU.is_equal)
                    last.then_inc(hot_ready, 1)
                    dve.wait_ge(source_in[b], 64 * i + 64)
                    for t in range(SUB):
                        tile(b, i, t, first)

                def back(b, i, first):
                    if not (first and b == 0):
                        dve.wait_ge(added, 2 * i + b)
                    add(b, i)

                paired(dve, front, back)


def tensor_output(k, summed_x, xs_in):
    nc, a = k.nc, k.a
    with ExitStack() as ctx:
        def sb(name, shape, dt=F32):
            return ctx.enter_context(nc.sbuf_tensor(name, shape, dt))

        wo0, wo1, bo0 = sb("wo0", [P, P]), sb("wo1", [P, P]), sb("bo0", [1, P])
        own = sb("own", [P, TILES * D])
        zt = sb("zt", [P, 4, COLS])
        y = sb("y1", [P, TILES, D])
        loaded, joined = k.sem("out_loaded"), k.sem("own_joined")
        n = load(k, loaded, [(own[:].rearrange("p (t c) -> p t c", c=D), k.xs_d.rearrange("(t p) c -> p t c", p=P)),
                             (wo0[:], a["L1_gnn_W_o0"]), (wo1[:], a["L1_gnn_W_o1"]), (bo0[:], row_of(a["L1_gnn_b_o0"]))])
        with nc.Block() as block:
            @block.vector
            def _(dve):
                dve.wait_ge(loaded, n)
                nc.vector.tensor_tensor(own[:], own[:], summed_x[:], ALU.add).then_inc(joined, 1)
        flip(k, TILES, (lambda t, j: own[:, t * D + j * P:t * D + j * P + P], 4),
             lambda j, w, t: zt[:, j:j + w, t * P:(t + 1) * P], [(loaded, n)])

        def finish(act, t, ps):
            copy_to(k, act, y[:, t, 0:P], ps[:, 0:P])
            return copy_to(k, act, y[:, t, P:D].rearrange("p (u m) -> p m u", m=3),
                           ps[:, P:D].rearrange("p (m u) -> p m u", m=3))

        rows_out(k, lambda t: [(zt[:, 0, t * P:(t + 1) * P], wo0[:], slice(0, P)), (k.ones[0:1, :], bo0[:], slice(0, P))]
                 + [(zt[:, 1 + m, t * P:(t + 1) * P], wo1[:], slice((1 + m) * P, (2 + m) * P)) for m in range(3)],
                 finish)

        def residual(v, st):
            st.done(v.scalar_tensor_tensor(k.x[:].rearrange("p t d -> p (t d)"), k.x[:].rearrange("p t d -> p (t d)"), 2.0,
                                           y[:].rearrange("p t d -> p (t d)"), ALU.mult, ALU.add))

        normalize(k, D, k.x, TILES, D, before=residual)


def mean_layer(k):
    nc, a = k.nc, k.a
    with ExitStack() as ctx:
        def sb(name, shape, dt=F32):
            return ctx.enter_context(nc.sbuf_tensor(name, shape, dt))

        wl, wr = sb("wl", [P, 4, D]), sb("wr", [P, 4, D])
        bl, g, be = sb("bl", [P, 4]), sb("g2", [P, 4]), sb("be2", [P, 4])
        mean_t = sb("mean_t", [P, 4, COLS])
        inv = sb("inv", [P, TILES])
        loaded, loaded_c, degree = k.sem("mean_loaded"), k.sem("counts_in"), k.sem("degree")
        with ExitStack() as inner:
            mean = inner.enter_context(nc.sbuf_tensor("mean", [P, TILES, D], F32))
            ct = inner.enter_context(nc.sbuf_tensor("ct", [P, TILES, COLS], F32))
            with ExitStack() as inmost:
                c = inmost.enter_context(nc.sbuf_tensor("c", [P, TILES, COLS], F32))
                nl = load(k, loaded_c, [(ct[:].rearrange("p t s -> p (t s)"), k.counts_d[:, :])])
                n = load(k, loaded, [(wl[:], weight(a["L2_gnn_W_l"])), (wr[:], weight(a["L2_gnn_W_r"])),
                                     (bl[:], columns(a["L2_gnn_b_l"])), (g[:], columns(a["L2_gnn_gamma"])),
                                     (be[:], columns(a["L2_gnn_beta"]))])
                flip(k, TILES, (lambda t, j: ct[:, t, j * P:(j + 1) * P], TILES),
                     lambda j, w, t: c[:, j:j + w, t * P:(t + 1) * P], [(loaded_c, nl)])
                with nc.Block() as block:
                    @block.sync
                    def _(sp):
                        sp.dma_start(k.by_target_d[:, :], c[:].rearrange("p t s -> p (t s)")).then_inc(loaded_c, 16)
                        sp.wait_ge(loaded_c, nl + 16)

                    @block.vector
                    def _(dve):
                        st = Steps(dve, degree)
                        st.done(nc.vector.tensor_reduce(inv[:], c[:], AX.X, ALU.add))
                        st.settle()
                        st.done(nc.vector.tensor_scalar(inv[:], inv[:], 1.0, None, ALU.max))
                        st.settle()
                        st.done(nc.vector.reciprocal(inv[:], inv[:]))
                        st.settle()

            def finish(act, t, ps):
                if act:
                    return nc.scalar.activation(mean[:, t], ps, ACT.Copy, scale=inv[:, t:t + 1])
                return nc.vector.tensor_scalar(mean[:, t], ps, inv[:, t:t + 1], None, ALU.mult)

            rows_out(k, lambda t: [(ct[:, s, t * P:(t + 1) * P], k.x[:, s], slice(0, D)) for s in range(TILES)], finish)
            flip(k, TILES, (lambda t, j: mean[:, t, j * P:(j + 1) * P], 4),
                 lambda j, w, t: mean_t[:, j:j + w, t * P:(t + 1) * P])
        xt, h = sb("xt2", [P, 4, COLS]), sb("h_2", [P, 4, COLS])
        flip(k, TILES, (lambda t, j: k.x[:, t, j * P:(j + 1) * P], 4),
             lambda j, w, t: xt[:, j:j + w, t * P:(t + 1) * P])
        features_out(k, 4, lambda j: [(wl[:, i, j * P:(j + 1) * P], mean_t[:, i]) for i in range(4)]
                     + [(wr[:, i, j * P:(j + 1) * P], xt[:, i]) for i in range(4)],
                     lambda act, j, at, ps: add_bias(k, act, h[:, j, at], ps, bl[:, j:j + 1], relu=True), [(loaded, n)])
        normalize(k, NODES, h, 4, COLS, scale=g, shift=be)
        join_rows(k, h)


def join_rows(k, h, scale=None, shift=None):
    with ExitStack() as ctx:
        rows = ctx.enter_context(k.nc.sbuf_tensor(f"rows{k.root_n}", [P, TILES, D], F32))
        batch = [(j, t) for j in range(4) for t in range(TILES)]

        def fill(n, bank):
            for j in range(4):
                last = k.nc.tensor.transpose(bank[:, j * P:(j + 1) * P], h[:, j, n * P:(n + 1) * P], k.ident[:])
            return last

        through_banks(k, TILES, fill, lambda act, n, bank: copy_to(k, act, rows[:, n], bank))
        if scale is not None:
            normalize(k, D, rows, TILES, D, scale=scale, shift=shift)

        def residual(v, st):
            st.done(v.tensor_tensor(k.x[:], k.x[:], rows[:], ALU.add))

        normalize(k, D, k.x, TILES, D, before=residual)


def attention(k, qt, kt, vr, agg):
    nc = k.nc
    with ExitStack() as ctx:
        k.names += 1
        def sb(name, shape, dt=F32):
            return ctx.enter_context(nc.sbuf_tensor(f"{name}_{k.names}", shape, dt))

        c = [sb(f"c{b}", [P, COLS]) for b in range(2)]
        far = [sb(f"far{b}", [P, COLS]) for b in range(2)]
        q = [sb(f"q{b}", [P, 4, P]) for b in range(2)]
        s = [sb(f"s{b}", [P, COLS]) for b in range(2)]
        p = [sb(f"p{b}", [P, COLS]) for b in range(2)]
        pt = [sb(f"pt{b}", [P, TILES, P]) for b in range(2)]
        top = [sb(f"top{b}", [P, 4]) for b in range(2)]
        names = k.names

        def sem(name):
            return k.sem(f"{name}_{names}")

        c_in = [sem(f"c_in{b}") for b in range(2)]
        q_in, far_ready = sem("q_in"), sem("far_ready")
        scored, masked, negated, raised = sem("scored"), sem("masked"), sem("negated"), sem("raised")
        weighed, inverted, turned, out_act, out_dve = sem("weighed"), sem("inverted"), sem("turned"), sem("pt_act"), sem("pt_dve")
        mixed, written = sem("mixed"), sem("written")
        ps_s = k.psum[:, 0:3].rearrange("p c n -> p (c n)")
        ps_t = k.psum[:, 3:6].rearrange("p c n -> p (c n)")
        ps_o = [k.psum[:, 6 + b, 0:DH] for b in range(2)]
        HALF = TILES // 2
        BOTH = 8

        def tiles(engine, tile):
            tile(0, 0, True)
            tile(1, 0, True)
            with engine.Fori(1, HALF) as i:
                tile(0, i, False)
                tile(1, i, False)

        with nc.Block() as block:
            @block.sync
            def _(sp):
                def tile(b, i, first):
                    if not first:
                        sp.wait_ge(weighed, (2 * i + b - 1) * HEADS)
                    sp.dma_start(c[b][:], k.by_target_d[:, bass.ds((2 * i + b) * COLS, COLS)]).then_inc(c_in[b], 16)

                tiles(sp, tile)

            @block.gpsimd
            def _(pool):
                def tile(b, i, first):
                    if not first:
                        pool.wait_ge(scored, (2 * i + b - 1) * HEADS)
                    pool.wait_ge(k.filled, k.filled_n)
                    nc.gpsimd.tensor_copy(q[b][:], qt[:, :, bass.ds((2 * i + b) * P, P)]).then_inc(q_in, 1)

                tiles(pool, tile)

            @block.tensor
            def _(pe):
                def score(b, i, h, first):
                    n = (2 * i + b) * HEADS + h
                    if h == 0:
                        pe.wait_ge(q_in, 2 * i + b + 1)
                    if not (first and b == 0 and h == 0):
                        pe.wait_ge(masked, n)
                    rows = slice(DH * (h % 2), DH * (h % 2) + DH)
                    for c0, cw in CHUNKS:
                        last = nc.tensor.matmul(ps_s[:, c0:c0 + cw], q[b][rows, h // 2], kt[rows, h // 2, c0:c0 + cw],
                                                start=True, stop=True)
                    last.then_inc(scored, 1)

                def mix(b, i, h, first):
                    n = (2 * i + b) * HEADS + h
                    pe.wait_ge(weighed, n + 1)
                    if not (first and b == 0 and h == 0):
                        pe.wait_ge(out_act, n)
                        pe.wait_ge(out_dve, n)
                    for j in range(TILES):
                        last = nc.tensor.transpose(ps_t[:, j * P:(j + 1) * P], p[h % 2][:, j * P:(j + 1) * P], k.ident[:])
                    last.then_inc(turned, 1)
                    pe.wait_ge(out_act, n + 1)
                    pe.wait_ge(out_dve, n + 1)
                    if not (first and b == 0 and h < 2):
                        pe.wait_ge(written, n - 1)
                    for j in range(TILES):
                        last = nc.tensor.matmul(ps_o[h % 2], pt[h % 2][:, j], vr[:, j, h * DH:(h + 1) * DH],
                                                start=j == 0, stop=j == TILES - 1)
                    last.then_inc(mixed, 1)

                def tile(b, i, first):
                    score(b, i, 0, first)
                    for h in range(HEADS):
                        if h + 1 < HEADS:
                            score(b, i, h + 1, first)
                        mix(b, i, h, first)

                tiles(pe, tile)

            @block.scalar
            def _(act):
                def raise_(b, i, h, first):
                    n = (2 * i + b) * HEADS + h
                    act.wait_ge(negated, n + 1)
                    nc.scalar.activation(s[h % 2][:], s[h % 2][:], ACT.Exp, bias=top[h % 2][:, 1:2]).then_inc(raised, 1)

                def turn(b, i, h, first):
                    n = (2 * i + b) * HEADS + h
                    act.wait_ge(turned, n + 1)
                    if not (first and b == 0 and h < 2):
                        act.wait_ge(mixed, n - 1)
                    nc.scalar.activation(pt[h % 2][:, 0:BOTH], ps_t[:, 0:BOTH * P].rearrange("p (j n) -> p j n", n=P),
                                         ACT.Copy).then_inc(out_act, 1)

                def tile(b, i, first):
                    raise_(b, i, 0, first)
                    for h in range(HEADS):
                        if h + 1 < HEADS:
                            raise_(b, i, h + 1, first)
                        turn(b, i, h, first)

                tiles(act, tile)

            @block.vector
            def _(dve):
                v = nc.vector

                def mask(b, i, h, first):
                    n = (2 * i + b) * HEADS + h
                    dve.wait_ge(scored, n + 1)
                    if not (first and b == 0 and h < 2):
                        dve.wait_ge(weighed, n - 1)
                        dve.wait_ge(inverted, 2 * n - 2)
                    dve.sem_inc(k.dve_ready, 1)
                    v.tensor_tensor_reduce(out=s[h % 2][:], in0=ps_s[:, 0:COLS], in1=far[b][:], scale=1.0, scalar=2 * FAR,
                                           op0=ALU.add, op1=ALU.max, accum_out=top[h % 2][:, 0:1]).then_inc(masked, 1)
                    dve.wait_ge(masked, n + 1)
                    v.tensor_scalar(top[h % 2][:, 1:2], top[h % 2][:, 0:1], -1.0, None, ALU.mult).then_inc(negated, 1)

                def weigh(b, i, h, first):
                    n = (2 * i + b) * HEADS + h
                    dve.wait_ge(raised, n + 1)
                    if not (first and b == 0 and h < 2):
                        dve.wait_ge(turned, n - 1)
                        dve.wait_ge(written, n - 1)
                    v.tensor_tensor_reduce(out=p[h % 2][:], in0=s[h % 2][:], in1=c[b][:], scale=1.0, scalar=0.0,
                                           op0=ALU.mult, op1=ALU.add, accum_out=top[h % 2][:, 2:3]).then_inc(weighed, 1)
                    dve.wait_ge(weighed, n + 1)
                    v.tensor_scalar(top[h % 2][:, 3:4], top[h % 2][:, 2:3], 1e-16, None, ALU.add).then_inc(inverted, 1)
                    dve.wait_ge(inverted, 2 * n + 1)
                    v.reciprocal(top[h % 2][:, 3:4], top[h % 2][:, 3:4]).then_inc(inverted, 1)

                def turn(b, i, h, first):
                    n = (2 * i + b) * HEADS + h
                    dve.wait_ge(turned, n + 1)
                    if not (first and b == 0 and h < 2):
                        dve.wait_ge(mixed, n - 1)
                    v.tensor_copy(pt[h % 2][:, BOTH:TILES], ps_t[:, BOTH * P:COLS].rearrange("p (j n) -> p j n", n=P)
                                  ).then_inc(out_dve, 1)

                def write(b, i, h, first):
                    n = (2 * i + b) * HEADS + h
                    dve.wait_ge(mixed, n + 1)
                    dve.wait_ge(inverted, 2 * n + 2)
                    v.tensor_scalar(agg[:, bass.ds((2 * i + b) * D + h * DH, DH)], ps_o[h % 2], top[h % 2][:, 3:4], None,
                                    ALU.mult).then_inc(written, 1)

                def tile(b, i, first):
                    dve.wait_ge(c_in[b], 16 * i + 16)
                    if not first:
                        dve.wait_ge(masked, (2 * i + b - 1) * HEADS)
                    v.tensor_scalar(far[b][:], c[b][:], 0.0, FAR, ALU.is_equal, ALU.mult).then_inc(far_ready, 1)
                    dve.wait_ge(far_ready, 2 * i + b + 1)
                    mask(b, i, 0, first)
                    for h in range(HEADS):
                        if h + 1 < HEADS:
                            mask(b, i, h + 1, first)
                        weigh(b, i, h, first)
                        turn(b, i, h, first)
                        if h > 0:
                            write(b, i, h - 1, first)
                    write(b, i, HEADS - 1, first)

                tiles(dve, tile)


def attention_layers(k):
    nc, a = k.nc, k.a
    with ExitStack() as ctx:
        def sb(name, shape, dt=F32):
            return ctx.enter_context(nc.sbuf_tensor(name, shape, dt))

        wq, wk, wv, wo = (sb(n, [P, 4, D]) for n in ("wq", "wk", "wv", "wo"))
        w1, w2 = sb("wf1", [P, 4, FF]), sb("wf2", [P, 2, D])
        vectors = [("bq", 4), ("bo", 4), ("b1", 2), ("b2", 4), ("g1", 4), ("beta1", 4), ("g2", 4), ("beta2", 4)]
        small = {n: sb("l3_" + n, [P, w]) for n, w in vectors}
        lg, lb = sb("lg", [P, D]), sb("lb", [P, D])
        xt = sb("xt3", [P, 4, COLS])
        kept, loaded, scaled = k.sem("x_kept"), k.sem("att_loaded"), k.sem("bq_scaled")
        nl = 0
        flip(k, TILES, (lambda t, j: k.x[:, t, j * P:(j + 1) * P], 4),
             lambda j, w, t: xt[:, j:j + w, t * P:(t + 1) * P])
        with nc.Block() as block:
            @block.sync
            def _(sp):
                sp.dma_start(k.x_d[:, :], k.x[:].rearrange("p t d -> p (t d)")).then_inc(kept, 16)
                sp.wait_ge(kept, 16)
        agg = k.x[:].rearrange("p t d -> p (t d)")
        for layer in range(2):
            pairs = [(wq[:], weight(a["L3_gnn_Wq"][layer])), (wk[:], weight(a["L3_gnn_Wk"][layer])),
                     (wv[:], weight(a["L3_gnn_Wv"][layer])), (wo[:], weight(a["L3_gnn_Wo"][layer])),
                     (w1[:], weight(a["L3_gnn_W1"][layer])), (w2[:], weight(a["L3_gnn_W2"][layer]))]
            pairs += [(small[n][:], columns(a["L3_gnn_" + n][layer])) for n, _ in vectors]
            if layer == 0:
                pairs += [(lg[:], spread(a["L3_gnn_ln_g"])), (lb[:], spread(a["L3_gnn_ln_b"]))]
            nl += load(k, loaded, pairs)
            with nc.Block() as block:
                @block.vector
                def _(dve):
                    dve.wait_ge(loaded, nl)
                    nc.vector.tensor_scalar(small["bq"][:], small["bq"][:], DH ** -0.5, None, ALU.mult).then_inc(scaled, 1)
            with ExitStack() as inner:
                with ExitStack() as inmost:
                    qt = inmost.enter_context(nc.sbuf_tensor(f"qt{layer}", [P, 4, COLS], F32))
                    kt = inmost.enter_context(nc.sbuf_tensor(f"kt{layer}", [P, 4, COLS], F32))
                    vr = inmost.enter_context(nc.sbuf_tensor(f"vr{layer}", [P, TILES, D], F32))

                    def scaled_q(act, j, at, ps):
                        if act:
                            return nc.scalar.activation(qt[:, j, at], ps, ACT.Identity, bias=small["bq"][:, j:j + 1],
                                                        scale=DH ** -0.5)
                        return nc.vector.tensor_scalar(qt[:, j, at], ps, DH ** -0.5, small["bq"][:, j:j + 1], ALU.mult, ALU.add)

                    features_out(k, 4, lambda j: [(wq[:, i, j * P:(j + 1) * P], xt[:, i]) for i in range(4)], scaled_q,
                                 [(loaded, nl)])
                    features_out(k, 4, lambda j: [(wk[:, i, j * P:(j + 1) * P], xt[:, i]) for i in range(4)],
                                 lambda act, j, at, ps: copy_to(k, act, kt[:, j, at], ps))
                    rows_out(k, lambda t: [(xt[:, i, t * P:(t + 1) * P], wv[:, i], slice(0, D)) for i in range(4)],
                             lambda act, t, ps: copy_to(k, act, vr[:, t], ps))
                    attention(k, qt, kt, vr, agg)
                at_ = inner.enter_context(nc.sbuf_tensor(f"agg_t{layer}", [P, 4, COLS], F32))
                new = inner.enter_context(nc.sbuf_tensor(f"new{layer}", [P, 4, COLS], F32))
                ff = inner.enter_context(nc.sbuf_tensor(f"ff{layer}", [P, 2, COLS], F32))
                flip(k, TILES, (lambda t, j: agg[:, t * D + j * P:t * D + (j + 1) * P], 4),
                     lambda j, w, t: at_[:, j:j + w, t * P:(t + 1) * P])
                features_out(k, 4, lambda j: [(wo[:, i, j * P:(j + 1) * P], at_[:, i]) for i in range(4)],
                             lambda act, j, at, ps: add_bias(k, act, new[:, j, at], ps, small["bo"][:, j:j + 1]))

                def plus(v, st):
                    st.done(v.tensor_tensor(xt[:], xt[:], new[:], ALU.add))

                normalize(k, NODES, xt, 4, COLS, scale=small["g1"], shift=small["beta1"], before=plus)
                features_out(k, 2, lambda j: [(w1[:, i, j * P:(j + 1) * P], xt[:, i]) for i in range(4)],
                             lambda act, j, at, ps: add_bias(k, act, ff[:, j, at], ps, small["b1"][:, j:j + 1], relu=True))
                features_out(k, 4, lambda j: [(w2[:, i, j * P:(j + 1) * P], ff[:, i]) for i in range(2)],
                             lambda act, j, at, ps: add_bias(k, act, new[:, j, at], ps, small["b2"][:, j:j + 1]))
                normalize(k, NODES, xt, 4, COLS, scale=small["g2"], shift=small["beta2"], before=plus)
        with nc.Block() as block:
            @block.sync
            def _(sp):
                sp.dma_start(agg, k.x_d[:, :]).then_inc(kept, 16)
                sp.wait_ge(kept, 32)
        join_rows(k, xt, lg, lb)


def program(nc, a, out):
    with ExitStack() as ctx:
        ctx.enter_context(nc.allow_non_contiguous_dma("rows of records"))
        k = Core(nc, ctx, a)
        k.records = nc.dram_tensor("records", [GROUPS * GROUP, REC], F32).ap()
        k.counts_d = nc.dram_tensor("counts_d", [P, TILES * COLS], F32).ap()
        k.lane = k.keep("lane", [P, P], F16)
        k.node = k.keep("node", [P, COLS], F16)
        k.ident = k.keep("ident", [P, P])
        k.ident_b = k.keep("ident_b", [P, P], BF16)
        k.group_tile = k.keep("group_tile_i", [P, GROUPS], I32)
        k.sums_t = k.keep("sums_t", [EA96, COLS])
        k.ones = k.keep("ones_row", [P, P])
        k.x = k.keep("x_rows", [P, TILES, D])
        k.filled, k.by_act, k.by_dve = k.sem("bank_filled"), k.sem("bank_out_act"), k.sem("bank_out_dve")
        k.filled_n = k.by_act_n = k.by_dve_n = 0
        k.norm, k.variances, k.roots = k.sem("norm_steps"), k.sem("variances"), k.sem("roots")
        k.norm_n = k.root_n = 0
        k.p1_d = nc.dram_tensor("p1_d", [COLS, 384], F32).ap()
        k.xs_d = nc.dram_tensor("xs_d", [COLS, D], F32).ap()
        k.by_target_d = nc.dram_tensor("by_target_d", [P, TILES * COLS], F32).ap()
        k.x_d = nc.dram_tensor("x_d", [P, TILES * D], F32).ap()
        k.stack_d = nc.dram_tensor("stack_d", [GROUPS * 256, GROUP], BF16).ap()
        k.x_loaded = k.sem("x_loaded")
        k.pool_ready, k.dve_ready, k.sp_ready = k.sem("pool_ready"), k.sem("dve_ready"), k.sem("sp_ready")
        x_cleared = k.sem("x_cleared")
        with nc.Block() as block:
            @block.gpsimd
            def _(pool):
                nc.gpsimd.memset(k.x[:, TILES - 1], 0.0).then_inc(x_cleared, 1)
                nc.gpsimd.memset(k.ones[:], 1.0).then_inc(x_cleared, 1)

            @block.sync
            def _(sp):
                whole = (TILES - 1) * P
                sp.dma_start(k.x[:, 0:TILES - 1], a["x"][0:whole, :].rearrange("(t p) d -> p t d", p=P)).then_inc(k.x_loaded, 16)
                sp.wait_ge(x_cleared, 2)
                sp.dma_start(k.x[0:LAST, TILES - 1], a["x"][whole:NODES, :]).then_inc(k.x_loaded, 16)

        sort_edges(k)
        count_edges(k)
        mlp_layer(k)
        with ExitStack() as tensor_layer:
            tensor_nodes(k, tensor_layer)
            edge_hidden(k)
            summed_x = tensor_layer.enter_context(nc.sbuf_tensor("summed_x", [P, TILES * D], F32))
            edge_messages(k, summed_x)
            tensor_output(k, summed_x, None)
        mean_layer(k)
        attention_layers(k)
        if out is None:
            out = nc.dram_tensor("out", [NODES, D], F32, kind="ExternalOutput").ap()
        returned = k.sem("returned")
        with nc.Block() as block:
            @block.sync
            def _(sp):
                whole = (TILES - 1) * P
                sp.dma_start(out[0:whole, :].rearrange("(t p) d -> p t d", p=P), k.x[:, 0:TILES - 1]).then_inc(returned, 16)
                sp.dma_start(out[whole:NODES, :], k.x[0:LAST, TILES - 1]).then_inc(returned, 16)
                sp.wait_ge(returned, 32)


TURNED = ("L2_gnn_W_l", "L2_gnn_W_r", "L3_gnn_Wq", "L3_gnn_Wk", "L3_gnn_Wv", "L3_gnn_Wo", "L3_gnn_W1", "L3_gnn_W2")


def layout(name, array):
    return array.swapaxes(-1, -2) if name in TURNED else array


def kernel(**inputs):
    import numpy as np
    from concourse import bacc
    from concourse.bass_utils import run_bass_kernel_spmd

    nc = bacc.Bacc("TRN2", target_bir_lowering=False, num_devices=1)
    arrays, handles = {}, {}
    for name, array in inputs.items():
        arrays["in_" + name] = np.ascontiguousarray(layout(name, np.asarray(array)))
        handles[name] = nc.dram_tensor("in_" + name, arrays["in_" + name].shape,
                                       mybir.dt.from_np(arrays["in_" + name].dtype), kind="ExternalInput").ap()
    out = nc.dram_tensor("out_0", (NODES, D), F32, kind="ExternalOutput").ap()
    program(nc, handles, out)
    got = run_bass_kernel_spmd(nc, [arrays], core_ids=[0])
    return got.results[0]["out_0"]
```

```python
from contextlib import ExitStack

import concourse.bass as bass
from concourse import mybir

P = 128
NODES, EDGES, D = 1250, 40000, 512
TILES = -(-NODES // P)
COLS = TILES * P
LAST = NODES - (TILES - 1) * P
SUB = 4
GROUP = SUB * P
GROUPS = (EDGES + TILES * (GROUP - 1)) // GROUP
GROUPS += -GROUPS % 4
EP = 125
EF = EDGES // EP
SLOTS = 4
CHUNK = 16
EA96, EA32, EA4 = 96, 32, 4
C_OTHER, C_KEY, REC = 132, 133, 136
CHUNKS = ((0, 512), (512, 512), (1024, 256))
BANK = 512
EPS = 1e-5
HEADS, DH = 8, 64
FF = 256
FAR = -1.0e30

F32 = mybir.dt.float32
F16 = mybir.dt.float16
BF16 = mybir.dt.bfloat16
I32 = mybir.dt.int32
ALU = mybir.AluOpType
ACT = mybir.ActivationFunctionType
AX = mybir.AxisListType

class Steps:

    def __init__(self, engine, sem, base=0):
        self.engine, self.sem, self.base, self.n = engine, sem, base, 0

    def done(self, ins):
        ins.then_inc(self.sem, 1)
        self.n += 1

    def settle(self):
        self.engine.wait_ge(self.sem, self.base + self.n)


class Core:

    def __init__(self, nc, ctx, a):
        self.nc, self.ctx, self.a = nc, ctx, a
        self.psum = ctx.enter_context(nc.psum_tensor("psum", [P, 8, BANK], F32))
        self.names = 0

    def sem(self, name):
        return self.ctx.enter_context(self.nc.semaphore(name))

    def keep(self, name, shape, dt=F32):
        return self.ctx.enter_context(self.nc.sbuf_tensor(name, shape, dt))


def sort_edges(k):
    nc, a = k.nc, k.a
    with ExitStack() as ctx:
        def sb(name, shape, dt=F32):
            return ctx.enter_context(nc.sbuf_tensor(name, shape, dt))

        key_i = sb("key_i", [EP, EF], I32)
        other_i = sb("other_i", [EP, EF], I32)
        other_f = sb("other_f", [EP, EF])
        tile_i = sb("tile_i", [EP, EF], I32)
        tile_f = sb("tile_f", [EP, EF])
        key_f = sb("key_f", [EP, EF])
        local = sb("local", [EP, EF])
        ones = sb("ones", [EP, EF])
        member = sb("member", [EP, TILES, EF])
        rank = sb("rank", [EP, TILES, EF])
        total = sb("total", [EP, TILES])
        before = sb("before", [EP, EP])
        every = sb("every", [EP, EP])
        cnt_i = sb("cnt_i", [EP, TILES], I32)
        grp_i = sb("grp_i", [EP, TILES], I32)
        grp = sb("grp", [EP, TILES])
        grp_end = sb("grp_end", [EP, TILES])
        grp_start = sb("grp_start", [EP, TILES])
        offset = sb("offset", [EP, TILES])
        group_no = sb("group_no", [EP, GROUPS])
        group_tile = sb("group_tile", [EP, GROUPS])
        slot_f = sb("slot_f", [EP, EF])
        slot_i = sb("slot_i", [EP, EF], I32)
        blank = sb("blank", [P, SUB, REC])
        stage = [sb(f"stage{b}", [EP, CHUNK, REC]) for b in range(2)]
        index = [sb(f"index{b}", [EP, CHUNK], I32) for b in range(2)]
        parts = [sb(f"attr_parts{b}", [EP, 3, CHUNK, EA96], BF16) for b in range(2)]
        other_c = [sb(f"other_c{b}", [EP, CHUNK]) for b in range(2)]
        rest = sb("attr_rest", [EP, CHUNK, EA96])
        hot = [sb(f"other_hot{b}", [EP, COLS], BF16) for b in range(4)]

        ends_loaded = k.sem("ends_loaded")
        masks_ready = k.sem("masks_ready")
        sorting = k.sem("sorting")
        totals_ready = k.sem("totals_ready")
        offsets_summed = k.sem("offsets_summed")
        blank_ready = k.sem("blank_ready")
        blanked = k.sem("blanked")
        features_in = [k.sem(f"features_in{b}") for b in range(2)]
        staged = [k.sem(f"staged{b}") for b in range(2)]
        k.scattered = [k.sem(f"scattered{b}") for b in range(2)]
        picked = k.sem("picked")
        split_act, split_dve = k.sem("split_act"), k.sem("split_dve")
        hot_ready, hot_used, sums_out = k.sem("hot_ready"), k.sem("hot_used"), k.sem("sums_out")
        ps_before, ps_every = k.psum[0:EP, 0, 0:TILES], k.psum[0:EP, 1, 0:TILES]
        ps_sums = k.psum[0:EA96, 2:5].rearrange("p c n -> p (c n)")
        rounds = EF // CHUNK // 2

        def chunks(engine, chunk):
            chunk(0, 0, True, False)
            chunk(1, 0, True, False)
            with engine.Fori(1, rounds - 1) as i:
                chunk(0, i, False, False)
                chunk(1, i, False, False)
            chunk(0, rounds - 1, False, False)
            chunk(1, rounds - 1, False, True)

        with nc.Block() as block:
            @block.sync
            def _(sp):
                sp.dma_start(key_i[:], a["src"].rearrange("(p f) -> p f", p=EP)).then_inc(ends_loaded, 16)
                sp.dma_start(other_i[:], a["dst"].rearrange("(p f) -> p f", p=EP)).then_inc(ends_loaded, 16)
                sp.wait_ge(blank_ready, 1)
                sp.dma_start(k.records.rearrange("(g p t) c -> p g (t c)", p=P, t=SUB),
                             blank[:].rearrange("p t c -> p (t c)")[:, None, :]
                             .broadcast_to([P, GROUPS, SUB * REC])).then_inc(blanked, 16)
                ea96 = a["edge_attr_96"].rearrange("(p f) d -> p f d", p=EP)
                ea32 = a["edge_attr_32"].rearrange("(p f) d -> p f d", p=EP)
                ea4 = a["edge_attr_4"].rearrange("(p f) d -> p f d", p=EP)

                def fetch(b, i, first, last):
                    at = bass.ds((2 * i + b) * CHUNK, CHUNK)
                    if not first:
                        sp.wait_ge(split_dve, 2 * (2 * i + b) - 2)
                        sp.wait_ge(k.scattered[b], i * 16 * CHUNK)
                    sp.dma_start(stage[b][:, :, 0:EA96], ea96[:, at]).then_inc(features_in[b], 16)
                    sp.dma_start(stage[b][:, :, EA96:EA96 + EA32], ea32[:, at]).then_inc(features_in[b], 16)
                    sp.dma_start(stage[b][:, :, EA96 + EA32:C_OTHER], ea4[:, at]).then_inc(features_in[b], 16)

                chunks(sp, fetch)

            @block.gpsimd
            def _(pool):
                st = Steps(pool, masks_ready)
                st.done(nc.gpsimd.iota(group_no[:], pattern=[[1, GROUPS]], base=0, channel_multiplier=0,
                                       allow_small_or_imprecise_dtypes=True))
                st.done(nc.gpsimd.iota(k.lane[:], pattern=[[1, P]], base=0, channel_multiplier=0,
                                       allow_small_or_imprecise_dtypes=True))
                st.done(nc.gpsimd.iota(k.node[:], pattern=[[1, COLS]], base=0, channel_multiplier=0,
                                       allow_small_or_imprecise_dtypes=True))
                st.done(nc.gpsimd.memset(every[:], 1.0))
                st.done(nc.gpsimd.memset(before[:], 1.0))
                st.done(nc.gpsimd.memset(k.ident[:], 0.0))
                st.settle()
                st.done(nc.gpsimd.affine_select(out=before[:], in_=before[:], compare_op=ALU.is_gt, fill=0.0,
                                                base=0, pattern=[[1, EP]], channel_multiplier=-1))
                st.done(nc.gpsimd.affine_select(out=k.ident[:], in_=k.ident[:], compare_op=ALU.not_equal, fill=1.0,
                                                base=0, pattern=[[-1, P]], channel_multiplier=1))
                st.settle()

                def scatter(b, i, first, last):
                    pool.wait_ge(staged[b], 2 * i + 2)
                    pool.wait_ge(blanked, 16)
                    pool.sem_inc(k.pool_ready, 1)
                    for f in range(CHUNK):
                        nc.gpsimd.indirect_dma_start(
                            k.records[:, :], bass.IndirectOffsetOnAxis(ap=index[b][:, f:f + 1], axis=0),
                            stage[b][:, f, :], None).then_inc(k.scattered[b], 16)

                chunks(pool, scatter)

            @block.tensor
            def _(pe):
                pe.wait_ge(masks_ready, 8)
                pe.wait_ge(totals_ready, 1)
                nc.tensor.matmul(ps_before, before[:], total[:], start=True, stop=True)
                nc.tensor.matmul(ps_every, every[:], total[:], start=True, stop=True).then_inc(offsets_summed, 1)

                def add_up(b, i, first, last):
                    pe.wait_ge(split_dve, 2 * (2 * i + b) + 2)
                    for f in range(CHUNK):
                        pe.wait_ge(hot_ready, (2 * i + b) * CHUNK + f + 1)
                        for j in range(3):
                            for c0, cw in CHUNKS:
                                mm = nc.tensor.matmul(ps_sums[:, c0:c0 + cw], parts[b][:, j, f], hot[f % 4][:, c0:c0 + cw],
                                                      start=first and b == 0 and f == 0 and j == 0,
                                                      stop=last and f == CHUNK - 1 and j == 2)
                        mm.then_inc(hot_used, 1)

                chunks(pe, add_up)

            @block.scalar
            def _(act):
                def split(b, i, first, last):
                    n = 2 * i + b
                    act.wait_ge(features_in[b], 48 * i + 48)
                    if not first:
                        act.wait_ge(hot_used, (n - 1) * CHUNK)
                    nc.scalar.activation(parts[b][:, 0], stage[b][:, :, 0:EA96], ACT.Copy).then_inc(split_act, 1)
                    act.wait_ge(split_dve, 2 * n + 1)
                    nc.scalar.activation(parts[b][:, 1], rest[:], ACT.Copy).then_inc(split_act, 1)

                chunks(act, split)
                act.wait_ge(hot_used, EF)
                nc.scalar.activation(k.sums_t[:], ps_sums[:, 0:COLS], ACT.Copy).then_inc(sums_out, 1)

            @block.vector
            def _(dve):
                v = nc.vector
                st = Steps(dve, sorting)
                st.done(v.memset(blank[:], 0.0))
                st.done(v.memset(ones[:], 1.0))
                st.settle()
                v.memset(blank[:, :, C_KEY:C_KEY + 1], -1.0).then_inc(blank_ready, 1)
                dve.wait_ge(masks_ready, 8)
                st.done(v.tensor_copy(k.ident_b[:], k.ident[:]))
                dve.wait_ge(ends_loaded, 32)
                st.done(v.tensor_scalar(tile_i[:], key_i[:], 7, None, ALU.arith_shift_right))
                st.done(v.tensor_copy(key_f[:], key_i[:]))
                st.done(v.tensor_copy(other_f[:], other_i[:]))
                st.settle()
                st.done(v.tensor_copy(tile_f[:], tile_i[:]))
                st.settle()
                st.done(v.scalar_tensor_tensor(local[:], tile_f[:], -float(P), key_f[:], ALU.mult, ALU.add))
                for b in range(TILES):
                    st.done(v.tensor_scalar(member[:, b], tile_f[:], float(b), None, ALU.is_equal))
                st.settle()
                for b in range(TILES):
                    st.done(v.tensor_tensor_scan(rank[:, b], ones[:], member[:, b], 0.0, ALU.mult, ALU.add))
                st.settle()
                v.tensor_copy(total[:], rank[:, :, EF - 1]).then_inc(totals_ready, 1)
                dve.wait_ge(offsets_summed, 1)
                st.done(v.tensor_scalar(cnt_i[:], ps_every, float(GROUP - 1), None, ALU.add))
                st.settle()
                st.done(v.tensor_scalar(grp_i[:], cnt_i[:], GROUP.bit_length() - 1, None, ALU.arith_shift_right))
                st.settle()
                st.done(v.tensor_copy(grp[:], grp_i[:]))
                st.settle()
                st.done(v.tensor_tensor_scan(grp_end[:], ones[:, 0:TILES], grp[:], 0.0, ALU.mult, ALU.add))
                st.settle()
                st.done(v.tensor_tensor(grp_start[:], grp_end[:], grp[:], ALU.subtract))
                st.settle()
                st.done(v.scalar_tensor_tensor(offset[:], grp_start[:], float(GROUP), ps_before, ALU.mult, ALU.add))
                st.settle()
                for b in range(TILES):
                    st.done(v.scalar_tensor_tensor(rank[:, b], rank[:, b], offset[:, b:b + 1], member[:, b],
                                                   ALU.add, ALU.mult))
                st.settle()
                st.done(v.tensor_reduce(slot_f[:], rank[:].rearrange("p b f -> p f b"), AX.X, ALU.add))
                st.settle()
                st.done(v.tensor_scalar(slot_i[:], slot_f[:], -1.0, None, ALU.add))
                st.done(v.tensor_scalar(group_tile[:], group_no[:], grp_start[:, 1:2], None, ALU.is_ge))
                st.settle()
                for b in range(2, TILES):
                    st.done(v.scalar_tensor_tensor(group_tile[:], group_no[:], grp_start[:, b:b + 1], group_tile[:],
                                                   ALU.is_ge, ALU.add))
                    st.settle()
                st.done(v.tensor_copy(k.group_tile[0:EP, :], group_tile[:]))
                st.settle()

                def fill(b, i, first, last):
                    n = 2 * i + b
                    at = bass.ds(n * CHUNK, CHUNK)
                    dve.wait_ge(features_in[b], 48 * i + 48)
                    if first:
                        st.done(v.memset(stage[b][:, :, C_KEY + 1:REC], 0.0))
                    v.tensor_copy(index[b][:], slot_i[:, at])
                    v.tensor_copy(stage[b][:, :, C_OTHER:C_OTHER + 1].bitcast(I32),
                                  other_i[:, at].unsqueeze(2)).then_inc(staged[b], 1)
                    v.tensor_copy(stage[b][:, :, C_KEY:C_KEY + 1], local[:, at].unsqueeze(2)).then_inc(staged[b], 1)
                    v.tensor_copy(other_c[b][:], other_f[:, at]).then_inc(picked, 1)
                    dve.wait_ge(split_act, 2 * n + 1)
                    v.tensor_tensor(rest[:], stage[b][:, :, 0:EA96], parts[b][:, 0], ALU.subtract).then_inc(split_dve, 1)
                    dve.wait_ge(split_act, 2 * n + 2)
                    v.tensor_tensor(parts[b][:, 2], rest[:], parts[b][:, 1], ALU.subtract).then_inc(split_dve, 1)
                    dve.wait_ge(picked, n + 1)
                    for f in range(CHUNK):
                        if not (first and b == 0 and f < 4):
                            dve.wait_ge(hot_used, n * CHUNK + f - 3)
                        v.tensor_scalar(hot[f % 4][:], k.node[0:EP, :], other_c[b][:, f:f + 1], None,
                                        ALU.is_equal).then_inc(hot_ready, 1)

                chunks(dve, fill)


def count_edges(k):
    nc = k.nc
    with ExitStack() as ctx:
        def sb(name, shape, dt=F32):
            return ctx.enter_context(nc.sbuf_tensor(name, shape, dt))

        counts = sb("counts", [P, TILES * COLS])
        record = [sb(f"record{b}", [P, SUB, REC]) for b in range(2)]
        src_f = [sb(f"src_f{b}", [P, SUB]) for b in range(2)]
        to_b = [sb(f"to_b{b}", [P, SUB, P], BF16) for b in range(2)]
        frm = [sb(f"frm{b}", [P, COLS], BF16) for b in range(2)]

        cleared = k.sem("cleared")
        rec_in = [k.sem(f"rec_in{b}") for b in range(2)]
        targets_hot = k.sem("targets_hot")
        src_float = k.sem("src_float")
        source_hot = k.sem("source_hot")
        tile_counted = k.sem("tile_counted")
        group_added = k.sem("group_added")
        counts_out = k.sem("counts_out")
        k.counts_out = counts_out

        ps = [k.psum[:, 4 * b:4 * b + 4, :] for b in range(2)]
        with nc.Block() as block:
            @block.sync
            def _(sp):
                for b in range(2):
                    sp.wait_ge(k.scattered[b], EF // CHUNK // 2 * 16 * CHUNK)
                view = k.records.rearrange("(g p t) c -> g p t c", p=P, t=SUB)
                for b in range(2):
                    sp.dma_start(record[b][:], view[b]).then_inc(rec_in[b], 16)
                with sp.Fori(1, GROUPS // 2) as i:
                    for b in range(2):
                        sp.wait_ge(tile_counted, i * 2 * SUB + (b - 1) * SUB)
                        sp.dma_start(record[b][:], k.records[bass.ds(i * 2 * GROUP + b * GROUP, GROUP), :]
                                     .rearrange("(p t) c -> p t c", p=P)).then_inc(rec_in[b], 16)
                sp.wait_ge(group_added, GROUPS)
                sp.dma_start(k.counts_d[:, :], counts[:]).then_inc(counts_out, 16)
                sp.wait_ge(counts_out, 16)

            @block.gpsimd
            def _(pool):
                nc.gpsimd.memset(counts[:], 0.0).then_inc(cleared, 1)

                def one_hots(b):
                    nc.gpsimd.tensor_copy(src_f[b][:], record[b][:, :, C_OTHER].bitcast(I32)).then_inc(src_float, 1)
                    for t in range(SUB):
                        last = nc.gpsimd.tensor_scalar(to_b[b][:, t], k.lane[:], record[b][:, t, C_KEY:C_KEY + 1], None, ALU.is_equal)
                    last.then_inc(targets_hot, 1)

                for b in range(2):
                    pool.wait_ge(rec_in[b], 16)
                    one_hots(b)
                with pool.Fori(1, GROUPS // 2) as i:
                    for b in range(2):
                        pool.wait_ge(rec_in[b], i * 16 + 16)
                        pool.sem_inc(k.pool_ready, 1)
                        one_hots(b)

            @block.tensor
            def _(pe):
                def count(b, i, first):
                    pe.wait_ge(targets_hot, i * 2 + b + 1)
                    if not first:
                        pe.wait_ge(group_added, i * 2 + b - 1)
                    for t in range(SUB):
                        pe.wait_ge(source_hot, (i * 2 + b) * SUB + t + 1)
                        for c, (c0, cw) in enumerate(CHUNKS):
                            last = nc.tensor.matmul(ps[b][:, c, 0:cw], to_b[b][:, t], frm[t % 2][:, c0:c0 + cw],
                                                    start=t == 0, stop=t == SUB - 1)
                        last.then_inc(tile_counted, 1)

                for b in range(2):
                    count(b, 0, True)
                with pe.Fori(1, GROUPS // 2) as i:
                    for b in range(2):
                        count(b, i, False)

            @block.vector
            def _(dve):
                v = nc.vector
                dve.wait_ge(cleared, 1)

                def add(b, g):
                    dve.wait_ge(tile_counted, g * SUB + SUB)
                    nt = dve.value_load(k.group_tile[0:1, bass.ds(g, 1)], min_val=0, max_val=TILES - 1)
                    here = counts[:, bass.ds(nt * COLS, COLS)]
                    v.tensor_tensor(here, here, ps[b].rearrange("p c n -> p (c n)")[:, 0:COLS],
                                    ALU.add).then_inc(group_added, 1)

                def hot(b, i, first):
                    dve.wait_ge(src_float, i * 2 + b + 1)
                    for t in range(SUB):
                        n = (i * 2 + b) * SUB + t
                        if not (first and b == 0 and t < 2):
                            dve.wait_ge(tile_counted, n - 1)
                        v.tensor_scalar(frm[t % 2][:], k.node[:], src_f[b][:, t:t + 1], None,
                                        ALU.is_equal).then_inc(source_hot, 1)

                hot(0, 0, True)
                hot(1, 0, True)
                add(0, 0)
                with dve.Fori(1, GROUPS // 2) as i:
                    hot(0, i, False)
                    dve.wait_ge(group_added, i * 2 - 1)
                    add(1, i * 2 - 1)
                    hot(1, i, False)
                    dve.wait_ge(group_added, i * 2)
                    add(0, i * 2)
                dve.wait_ge(group_added, GROUPS - 1)
                add(1, GROUPS - 1)


def copy_to(k, act, out, in_):
    if act:
        return k.nc.scalar.activation(out, in_, ACT.Copy)
    return k.nc.vector.tensor_copy(out, in_)


def add_bias(k, act, out, in_, bias, relu=False):
    if act:
        return k.nc.scalar.activation(out, in_, ACT.Relu if relu else ACT.Identity, bias=bias)
    if relu:
        return k.nc.vector.tensor_scalar(out, in_, bias, 0.0, ALU.add, ALU.max)
    return k.nc.vector.tensor_scalar(out, in_, bias, None, ALU.add)


def load(k, sem, pairs):
    with k.nc.Block() as block:
        @block.sync
        def _(sp):
            for out, in_ in pairs:
                sp.dma_start(out, in_).then_inc(sem, 16)
    return 16 * len(pairs)


def through_banks(k, count, fill, drain, needs=()):
    filled, by_act, by_dve = k.filled, k.by_act, k.by_dve
    f0, a0, d0 = k.filled_n, k.by_act_n, k.by_dve_n
    acts, dves = (count + 1) // 2, count // 2
    with k.nc.Block() as block:
        @block.tensor
        def _(pe):
            for sem, value in needs:
                pe.wait_ge(sem, value)
            for n in range(count):
                if n >= 8:
                    pe.wait_ge(*((by_dve, d0 + n // 2 - 3) if n % 2 else (by_act, a0 + n // 2 - 3)))
                fill(n, k.psum[:, n % 8]).then_inc(filled, 1)

        @block.scalar
        def _(act):
            for sem, value in needs:
                act.wait_ge(sem, value)
            for n in range(0, count, 2):
                act.wait_ge(filled, f0 + n + 1)
                drain(True, n, k.psum[:, n % 8]).then_inc(by_act, 1)

        @block.vector
        def _(dve):
            for sem, value in needs:
                dve.wait_ge(sem, value)
            for n in range(1, count, 2):
                dve.wait_ge(filled, f0 + n + 1)
                drain(False, n, k.psum[:, n % 8]).then_inc(by_dve, 1)

    k.filled_n, k.by_act_n, k.by_dve_n = f0 + count, a0 + acts, d0 + dves


def flip(k, tiles, pieces, out, needs=()):
    piece, wide = pieces
    batches = [(t, j, min(4, wide - j)) for t in range(tiles) for j in range(0, wide, 4)]

    def fill(n, bank):
        t, j, w = batches[n]
        for i in range(w):
            x = piece(t, j + i)
            last = k.nc.tensor.transpose(bank[0:x.shape[1], i * P:(i + 1) * P], x, k.ident[:])
        return last

    def drain(act, n, bank):
        t, j, w = batches[n]
        o = out(j, w, t)
        return copy_to(k, act, o, bank[0:o.shape[0], 0:w * P].rearrange("p (j c) -> p j c", j=w))

    through_banks(k, len(batches), fill, drain, needs)


def features_out(k, outs, terms, finish, needs=()):
    def fill(n, bank):
        j, (c0, cw) = n // len(CHUNKS), CHUNKS[n % len(CHUNKS)]
        ts = terms(j)
        for i, (w, x) in enumerate(ts):
            last = k.nc.tensor.matmul(bank[:, 0:cw], w, x[:, c0:c0 + cw], start=i == 0, stop=i == len(ts) - 1)
        return last

    def drain(act, n, bank):
        j, (c0, cw) = n // len(CHUNKS), CHUNKS[n % len(CHUNKS)]
        return finish(act, j, slice(c0, c0 + cw), bank[:, 0:cw])

    through_banks(k, outs * len(CHUNKS), fill, drain, needs)


def rows_out(k, terms, finish, needs=()):
    def fill(n, bank):
        ts = terms(n)
        for i, (x, w, at) in enumerate(ts):
            last = k.nc.tensor.matmul(bank[:, at], x, w, start=i == 0 or ts[i - 1][2] != at,
                                      stop=i == len(ts) - 1 or ts[i + 1][2] != at)
        return last

    through_banks(k, TILES, fill, lambda act, n, bank: finish(act, n, bank), needs)


def normalize(k, mean_of, x, pieces, width, scale=None, shift=None, plus=None, before=None, needs=()):
    nc = k.nc
    chunks = [(c, min(BANK, mean_of - c)) for c in range(0, mean_of, BANK)]
    with ExitStack() as ctx:
        k.names += 1
        stats = ctx.enter_context(nc.sbuf_tensor(f"stats{k.names}", [P, pieces, len(chunks), 6], F32))
        mv = ctx.enter_context(nc.sbuf_tensor(f"mv{k.names}", [P, pieces, 2], F32))
        root = ctx.enter_context(nc.sbuf_tensor(f"root{k.names}", [P, pieces], F32))
        base, r0 = k.norm_n, k.root_n
        with nc.Block() as block:
            @block.scalar
            def _(act):
                act.wait_ge(k.variances, r0 + 1)
                nc.scalar.activation(root[:], mv[:, :, 1], ACT.Sqrt).then_inc(k.roots, 1)

            @block.vector
            def _(dve):
                v = nc.vector
                for sem, value in needs:
                    dve.wait_ge(sem, value)
                st = Steps(dve, k.norm, base)
                if before:
                    before(v, st)
                    st.settle()
                for t in range(pieces):
                    for c, (c0, cw) in enumerate(chunks):
                        st.done(v.bn_stats(stats[:, t, c], x[:, t, c0:c0 + cw]))
                st.settle()
                for t in range(pieces):
                    st.done(v.bn_aggr(mv[:, t], stats[:, t]))
                st.settle()
                v.tensor_scalar(mv[:, :, 1], mv[:, :, 1], EPS, None, ALU.add).then_inc(k.variances, 1)
                dve.wait_ge(k.roots, r0 + 1)
                st.done(v.reciprocal(root[:], root[:]))
                st.settle()
                for t in range(pieces):
                    st.done(v.tensor_scalar(x[:, t, 0:width], x[:, t, 0:width], mv[:, t, 0:1], root[:, t:t + 1],
                                            ALU.subtract, ALU.mult))
                for other, op in ((scale, ALU.mult), (shift, ALU.add)):
                    if other is not None:
                        st.settle()
                        if other.shape[1] == pieces:
                            for t in range(pieces):
                                st.done(v.tensor_scalar(x[:, t, 0:width], x[:, t, 0:width], other[:, t:t + 1], None, op))
                        else:
                            st.done(v.tensor_tensor(x[:], x[:], other[:][:, None, :].broadcast_to([P, pieces, width]), op))
                if plus is not None:
                    st.settle()
                    st.done(v.tensor_tensor(x[:], x[:], plus[:], ALU.add))
                st.settle()
                k.norm_n += st.n
        k.root_n += 1


def row_of(ap, n=D):
    return ap.rearrange("(o d) -> o d", o=1)


def spread(ap, n=D):
    return row_of(ap).broadcast_to([P, n])


def columns(ap):
    return ap.rearrange("(t p) -> p t", p=P)


def weight(ap):
    return ap.rearrange("(t p) j -> p t j", p=P)


def mlp_layer(k):
    nc, a = k.nc, k.a
    with ExitStack() as ctx:
        def sb(name, shape, dt=F32):
            return ctx.enter_context(nc.sbuf_tensor(name, shape, dt))

        w1, w1e, w2, w3 = sb("w1", [P, 4, 1024]), sb("w1e", [EA96, 1024]), sb("w2", [P, 8, 1024]), sb("w3", [P, 8, D])
        b1, b2, b3 = sb("b1", [P, 8]), sb("b2", [P, 8]), sb("b3", [1, D])
        g, be = sb("g0", [P, D]), sb("be0", [P, D])
        loaded = k.sem("mlp_loaded")
        n = load(k, loaded, [
            (w1[:], weight(a["L0_gnn_W1"][0:D, :])), (w1e[:], a["L0_gnn_W1"][D:D + EA96, :]),
            (b1[:], columns(a["L0_gnn_b1"])), (w2[:], weight(a["L0_gnn_W2"])), (b2[:], columns(a["L0_gnn_b2"])),
            (w3[:], weight(a["L0_gnn_W3"])), (b3[:], row_of(a["L0_gnn_b3"])),
            (g[:], spread(a["L0_gnn_gamma"])), (be[:], spread(a["L0_gnn_beta"]))])
        needs = [(loaded, n)]
        h1 = sb("h1", [P, 8, COLS])
        with ExitStack() as inner:
            xt = inner.enter_context(nc.sbuf_tensor("xt0", [P, 4, COLS], F32))
            flip(k, TILES, (lambda t, j: k.x[:, t, j * P:(j + 1) * P], 4),
                 lambda j, w, t: xt[:, j:j + w, t * P:(t + 1) * P], [(k.x_loaded, 32)])
            features_out(k, 8, lambda j: [(w1[:, i, j * P:(j + 1) * P], xt[:, i]) for i in range(4)]
                         + [(w1e[:, j * P:(j + 1) * P], k.sums_t)],
                         lambda act, j, at, ps: add_bias(k, act, h1[:, j, at], ps, b1[:, j:j + 1], relu=True), needs)
        h2 = sb("h2", [P, 8, COLS])
        features_out(k, 8, lambda j: [(w2[:, i, j * P:(j + 1) * P], h1[:, i]) for i in range(8)],
                     lambda act, j, at, ps: add_bias(k, act, h2[:, j, at], ps, b2[:, j:j + 1], relu=True))
        y = h1[:, 0:4].rearrange("p a b -> p (a b)").rearrange("p (t d) -> p t d", d=D)
        rows_out(k, lambda t: [(h2[:, i, t * P:(t + 1) * P], w3[:, i], slice(0, D)) for i in range(8)]
                 + [(k.ones[0:1, :], b3[:], slice(0, D))],
                 lambda act, t, ps: copy_to(k, act, y[:, t], ps))
        normalize(k, D, y, TILES, D, scale=g, shift=be, plus=k.x)

        def keep(v, st):
            st.done(v.tensor_copy(k.x[:], y))

        normalize(k, D, k.x, TILES, D, before=keep)


def split3(k, v, st, src, parts, rest):
    st.done(v.tensor_copy(parts[0], src))
    st.settle()
    st.done(v.tensor_tensor(rest, src, parts[0], ALU.subtract))
    st.settle()
    st.done(v.tensor_copy(parts[1], rest))
    st.settle()
    st.done(v.tensor_tensor(parts[2], rest, parts[1], ALU.subtract))
    st.settle()


def tensor_nodes(k, ctx):
    nc, a = k.nc, k.a
    outer = ctx

    def keep(name, shape, dt=F32):
        return outer.enter_context(nc.sbuf_tensor(name, shape, dt))

    k.p1_parts = keep("p1_parts", [P, TILES * 3 * 384], BF16)
    k.ph_parts = keep("ph_parts", [P, TILES * 3 * P], BF16)
    k.hid_f = keep("hid_f", [EA32, P])
    k.hid_s = keep("hid_s", [P, P])
    k.mix = keep("mix", [P, 2, 2, D], BF16)
    with ExitStack() as ctx:
        def sb(name, shape, dt=F32):
            return ctx.enter_context(nc.sbuf_tensor(name, shape, dt))

        wp0, wp1, wn0, wn1 = (sb(n, [P, P]) for n in ("wp0", "wp1", "wn0", "wn1"))
        bp0, bn0 = sb("bp0", [P, 1]), sb("bn0", [1, P])
        wg1, wg2, bg1, bg2 = sb("wg1", [P, 2, 256]), sb("wg2", [P, 2, 256]), sb("bg1", [P, 2]), sb("bg2", [P, 2])
        ws1 = sb("ws1", [P, 3, 32])
        wsum = sb("wsum", [P, P])
        mixf = sb("mixf", [P, 2, D])
        part = sb("part", [P, 3, 2, D], BF16)
        rest = sb("rest", [P, 2, D])
        xp = sb("xp", [P, 4, COLS])
        p0 = sb("p0", [P, COLS])
        p1 = sb("p1", [P, TILES, D])
        loaded = k.sem("node_loaded")
        pairs = [(wp0[:], a["L1_gnn_W_pre0"]), (wp1[:], a["L1_gnn_W_pre1"]), (wn0[:], a["L1_gnn_W_nd0"]),
                 (wn1[:], a["L1_gnn_W_nd1"]), (bp0[:], columns(a["L1_gnn_b_pre0"])), (bn0[:], row_of(a["L1_gnn_b_nd0"])),
                 (wg1[:], weight(a["L1_gnn_W_g1"])), (wg2[:], weight(a["L1_gnn_W_g2"])),
                 (bg1[:], columns(a["L1_gnn_b_g1"])), (bg2[:], columns(a["L1_gnn_b_g2"])),
                 (ws1[:], weight(a["L1_gnn_W_s1"]))]
        for r in range(4):
            pairs.append((mixf[32 * r:32 * r + 32, 0], a["L1_gnn_W_f2"]))
            pairs.append((mixf[32 * r:32 * r + 32, 1], a["L1_gnn_W_s2"]))
        pairs.append((k.hid_f[:, 0:32], a["L1_gnn_W_f1"]))
        pairs.append((k.hid_f[:, 64:96], a["L1_gnn_W_f1"]))
        n = load(k, loaded, pairs)
        steps, masked = k.sem("node_steps"), k.sem("node_masked")

        with nc.Block() as block:
            @block.gpsimd
            def _(pool):
                st = Steps(pool, masked)
                st.done(nc.gpsimd.memset(k.hid_f[:, 32:64], 0.0))
                st.done(nc.gpsimd.memset(k.hid_f[:, 96:128], 0.0))
                st.done(nc.gpsimd.memset(k.hid_s[:], 0.0))
                st.done(nc.gpsimd.memset(wsum[:], 0.0))
                st.done(nc.gpsimd.memset(k.mix[:], 0.0))

            @block.vector
            def _(dve):
                v = nc.vector
                dve.wait_ge(loaded, n)
                dve.wait_ge(masked, 5)
                st = Steps(dve, steps)
                for r in (32, 96):
                    st.done(v.tensor_tensor(wsum[:, r:r + 32], ws1[:, 0], ws1[:, 1], ALU.add))
                    st.done(v.tensor_scalar(k.hid_s[:, r:r + 32], ws1[:, 2], 1.0 / 3.0, None, ALU.mult))
                st.done(v.tensor_scalar(mixf[:, 1, 384:512], mixf[:, 1, 384:512], 3.0 ** -0.5, None, ALU.mult))
                st.settle()
                split3(k, v, st, mixf[:], [part[:, i] for i in range(3)], rest[:])
                for r, first, second in ((0, 0, None), (1, 0, 1), (2, 0, 1), (3, 2, None)):
                    rows = slice(32 * r, 32 * r + 32)
                    st.done(v.tensor_copy(k.mix[rows, :, 0], part[rows, first]))
                    if second:
                        st.done(v.tensor_copy(k.mix[rows, :, 1], part[rows, second]))
                st.settle()

        def planar(t, j):
            return k.x[:, t, 0:P] if j == 0 else k.x[:, t, P + j - 1:D:3]

        flip(k, TILES, (planar, 4), lambda j, w, t: xp[:, j:j + w, t * P:(t + 1) * P])
        features_out(k, 1, lambda j: [(wp0[:], xp[:, 0])],
                     lambda act, j, at, ps: add_bias(k, act, p0[:, at], ps, bp0[:, 0:1]))
        rows_out(k, lambda t: [(xp[:, 1 + m, t * P:(t + 1) * P], wp1[:], slice(m * P, m * P + P)) for m in range(3)]
                 + [(p0[:, t * P:(t + 1) * P], wsum[:], slice(384, 512))],
                 lambda act, t, ps: copy_to(k, act, p1[:, t], ps))
        s2 = k.sem("node_split")
        k.tables = k.sem("tables")
        rest2 = sb("rest2", [P, TILES, 384])
        with nc.Block() as block:
            @block.sync
            def _(sp):
                sp.dma_start(k.p1_d.rearrange("(t p) c -> p t c", p=P), p1[:, :, 0:384]).then_inc(k.tables, 16)
                sp.wait_ge(k.tables, 16)

            @block.vector
            def _(dve):
                st = Steps(dve, s2)
                pv = k.p1_parts[:].rearrange("p (t i c) -> p t i c", t=TILES, i=3)
                split3(k, nc.vector, st, p1[:, :, 0:384], [pv[:, :, i] for i in range(3)], rest2[:])
                pv = k.ph_parts[:].rearrange("p (t i c) -> p t i c", t=TILES, i=3)
                split3(k, nc.vector, st, p1[:, :, 384:512], [pv[:, :, i] for i in range(3)], rest2[:, :, 0:P])

        n1 = sb("n1", [P, COLS])
        hid = sb("hid", [P, 2, COLS])
        gate = sb("gate", [P, COLS])
        s3, s4 = k.sem("norms_summed"), k.sem("norms_rooted")
        with nc.Block() as block:
            @block.scalar
            def _(act):
                act.wait_ge(s3, 4)
                nc.scalar.activation(n1[:], n1[:], ACT.Sqrt, scale=1.0 / 3.0).then_inc(s4, 1)

            @block.vector
            def _(dve):
                v = nc.vector
                st = Steps(dve, s3)
                st.done(v.tensor_tensor(hid[:, 0], xp[:, 1], xp[:, 1], ALU.mult))
                st.done(v.tensor_tensor(hid[:, 1], xp[:, 2], xp[:, 2], ALU.mult))
                st.settle()
                v.tensor_tensor(n1[:], hid[:, 0], hid[:, 1], ALU.add)
                st.done(v.tensor_tensor(gate[:], xp[:, 3], xp[:, 3], ALU.mult))
                st.settle()
                st.done(v.tensor_tensor(n1[:], n1[:], gate[:], ALU.add))
        sig = sb("sig", [P, 2, COLS])
        features_out(k, 2, lambda j: [(wg1[:, 0, j * P:(j + 1) * P], xp[:, 0]), (wg1[:, 1, j * P:(j + 1) * P], n1[:])],
                     lambda act, j, at, ps: add_bias(k, act, hid[:, j, at], ps, bg1[:, j:j + 1]))
        s5, s6 = k.sem("sigmoid_done"), k.sem("silu_done")
        with nc.Block() as block:
            @block.scalar
            def _(act):
                nc.scalar.activation(sig[:], hid[:], ACT.Sigmoid).then_inc(s5, 1)

            @block.vector
            def _(dve):
                dve.wait_ge(s5, 1)
                nc.vector.tensor_tensor(hid[:], hid[:], sig[:], ALU.mult).then_inc(s6, 1)
        g0 = sig[:, 0]
        features_out(k, 2, lambda j: [(wg2[:, i, j * P:(j + 1) * P], hid[:, i]) for i in range(2)],
                     lambda act, j, at, ps: add_bias(k, act, (gate if j else g0)[:, at], ps, bg2[:, j:j + 1]))
        s7 = k.sem("gated")
        with nc.Block() as block:
            @block.vector
            def _(dve):
                nc.vector.tensor_tensor(xp[:, 1:4], xp[:, 1:4], gate[:][:, None, :].broadcast_to([P, 3, COLS]),
                                        ALU.mult).then_inc(s7, 1)
        xs = sb("xs", [P, TILES, D])
        rows_out(k, lambda t: [(g0[:, t * P:(t + 1) * P], wn0[:], slice(0, P)), (k.ones[0:1, :], bn0[:], slice(0, P))]
                 + [(xp[:, 1 + m, t * P:(t + 1) * P], wn1[:], slice((1 + m) * P, (2 + m) * P)) for m in range(3)],
                 lambda act, t, ps: copy_to(k, act, xs[:, t], ps))
        with nc.Block() as block:
            @block.sync
            def _(sp):
                sp.dma_start(k.xs_d.rearrange("(t p) c -> p t c", p=P), xs[:]).then_inc(k.tables, 16)
                sp.wait_ge(k.tables, 32)


def paired(engine, front, back):
    rounds = GROUPS // 2
    front(0, 0, True)
    front(1, 0, True)
    back(0, 0, True)
    front(0, 1, False)
    back(1, 0, True)
    front(1, 1, False)
    back(0, 1, False)
    with engine.Fori(2, rounds) as i:
        front(0, i, False)
        back(1, i - 1, False)
        front(1, i, False)
        back(0, i, False)
    back(1, rounds - 1, False)


class Turn:

    def __init__(self, rnd, slot, slots, count):
        self.round, self.slot = rnd + slot // slots, slot % slots
        self.g = self.round * slots + self.slot
        self.count = count
        self.fixed = isinstance(rnd, int)
        self.two = self.slot % 2

    def exists(self):
        return not self.fixed or 0 <= self.g < self.count

    def reaches(self, g):
        return not self.fixed or self.g >= g


def in_turn(engine, step, ahead, behind, slots, count, peeled):
    def at(rnd, slot):
        step(lambda d: Turn(rnd, slot + d, slots, count))

    for g in range(-ahead, peeled * slots):
        at(0, g)
    with engine.Fori(peeled, count // slots - 1) as i:
        for slot in range(slots):
            at(i, slot)
    for g in range(count - slots, count + behind):
        at(0, g)


def over_groups(engine, step, ahead, behind):
    in_turn(engine, step, ahead, behind, SLOTS, GROUPS, 2)


def over_tiles(engine, step, ahead, behind):
    in_turn(engine, step, ahead, behind, 2, TILES, 1)


def edge_hidden(k):
    nc = k.nc
    with ExitStack() as ctx:
        def sb(name, shape, dt=F32):
            return ctx.enter_context(nc.sbuf_tensor(name, shape, dt))

        record = [sb(f"rec_h{b}", [P, SUB, REC]) for b in range(SLOTS)]
        source = [sb(f"source{b}", [P, SUB, 384]) for b in range(SLOTS)]
        hot = [sb(f"hot{b}", [P, SUB, P], BF16) for b in range(2)]
        hot_t = [sb(f"hot_t{b}", [P, GROUP], BF16) for b in range(2)]
        attr_t = [sb(f"attr_t{b}", [EA32, GROUP]) for b in range(2)]
        prod = [sb(f"prod{b}", [P, 3, P]) for b in range(2)]
        ip = [sb(f"ip{b}", [P, SUB, P]) for b in range(2)]
        ip_t = sb("ip_t", [P, GROUP])
        size = sb("size", [64, GROUP])
        hidden = sb("hidden", [64, GROUP])
        parts = [sb(f"parts{b}", [64, 3, GROUP], BF16) for b in range(SLOTS)]
        half = sb("half", [64, 1])

        rec_in = [k.sem(f"h_rec_in{b}") for b in range(SLOTS)]
        source_in = [k.sem(f"h_source_in{b}") for b in range(SLOTS)]
        stored = [k.sem(f"h_stored{b}") for b in range(SLOTS)]
        hot_ready, flipped, hot_copied = k.sem("h_hot"), k.sem("h_flipped"), k.sem("h_hot_copied")
        attr_copied = k.sem("h_attr_copied")
        target_out, multiplied, summed = k.sem("h_target"), k.sem("h_multiplied"), k.sem("h_summed")
        ip_flipped, ip_copied = k.sem("h_ip_flipped"), k.sem("h_ip_copied")
        begun, hidden_in, soft, hidden_out = k.sem("h_begun"), k.sem("h_in"), k.sem("h_soft"), k.sem("h_out")
        cast, rest_out = k.sem("h_cast"), k.sem("h_rest")
        halved = k.sem("h_halved")
        k.stored = stored

        ps_hot = k.psum[:, 0].bitcast(BF16)[:, 0:GROUP]
        ps_attr = k.psum[0:EA32, 1]
        ps_target = [k.psum[:, 2 + b, 0:384] for b in range(2)]
        ps_ip = k.psum[:, 4]
        ps_hid = [k.psum[:, 5 + b] for b in range(2)]

        with nc.Block() as block:
            @block.sync
            def _(sp):
                def fetch(n):
                    if n.reaches(SLOTS):
                        sp.wait_ge(flipped, n.g - SLOTS + 1)
                        sp.sem_inc(k.sp_ready, 1)
                        sp.wait_ge(source_in[n.slot], 64 * n.round)
                    sp.dma_start(record[n.slot][:], k.records[bass.ds(n.g * GROUP, GROUP), :]
                                 .rearrange("(p t) c -> p t c", p=P)).then_inc(rec_in[n.slot], 16)

                def store(n):
                    sp.wait_ge(cast, 2 * n.g + 2)
                    sp.sem_inc(k.sp_ready, 1)
                    sp.wait_ge(rest_out, 2 * n.g + 2)
                    for blk, part in enumerate((2, 0, 1, 0)):
                        sp.dma_start(k.stack_d[bass.ds(n.g * 256 + blk * 64, 64), :],
                                     parts[n.slot][:, part]).then_inc(stored[n.slot], 16)

                def step(near):
                    if near(3).exists():
                        fetch(near(3))
                    if near(-3).exists():
                        store(near(-3))

                over_groups(sp, step, 3, 3)

            @block.gpsimd
            def _(pool):
                nc.gpsimd.memset(half[:], 0.5).then_inc(halved, 1)

                def gather(near):
                    n = near(0)
                    pool.wait_ge(rec_in[n.slot], 16 * n.round + 16)
                    if n.reaches(SLOTS):
                        pool.wait_ge(multiplied, (n.g - SLOTS + 1) * SUB)
                    pool.wait_ge(k.tables, 32)
                    pool.sem_inc(k.pool_ready, 1)
                    for t in range(SUB):
                        nc.gpsimd.indirect_dma_start(
                            source[n.slot][:, t, :], None, k.p1_d[:, :],
                            bass.IndirectOffsetOnAxis(ap=record[n.slot][:, t, C_OTHER:C_OTHER + 1].bitcast(I32), axis=0)
                        ).then_inc(source_in[n.slot], 16)

                over_groups(pool, gather, 0, 0)

            @block.tensor
            def _(pe):
                def flips(n):
                    pe.wait_ge(hot_ready, n.g + 1)
                    if n.reaches(1):
                        pe.wait_ge(hot_copied, n.g)
                        pe.wait_ge(attr_copied, n.g)
                    for t in range(SUB):
                        nc.tensor.transpose(ps_hot[:, t * P:(t + 1) * P], hot[n.two][:, t], k.ident_b[:])
                    for t in range(SUB):
                        last = nc.tensor.transpose(ps_attr[:, t * P:(t + 1) * P], record[n.slot][:, t, EA96:EA96 + EA32],
                                                   k.ident[:])
                    last.then_inc(flipped, 1)

                def target(n, row_tile, t):
                    if n.reaches(1) or t >= 2:
                        pe.wait_ge(multiplied, n.g * SUB + t - 1)
                    for j in range(3):
                        last = nc.tensor.matmul(ps_target[t % 2], hot_t[n.two][:, t * P:(t + 1) * P],
                                                k.p1_parts[:, bass.ds(row_tile * (3 * 384) + j * 384, 384)],
                                                start=j == 0, stop=j == 2)
                    last.then_inc(target_out, 1)

                def ip_flips(n):
                    pe.wait_ge(summed, n.g * SUB + SUB)
                    if n.reaches(1):
                        pe.wait_ge(ip_copied, n.g)
                    for t in range(SUB):
                        last = nc.tensor.transpose(ps_ip[:, t * P:(t + 1) * P], ip[n.two][:, t], k.ident[:])
                    last.then_inc(ip_flipped, 1)

                def begin_hidden(n, row_tile):
                    pe.wait_ge(attr_copied, n.g + 1)
                    if n.reaches(2):
                        pe.wait_ge(hidden_out, n.g - 1)
                    nc.tensor.matmul(ps_hid[n.two], k.hid_f[:], attr_t[n.two][:], start=True, stop=False)
                    for j in range(3):
                        last = nc.tensor.matmul(ps_hid[n.two], k.ph_parts[:, bass.ds(row_tile * (3 * P) + j * P, P)],
                                                hot_t[n.two][:], start=False, stop=False)
                    last.then_inc(begun, 1)

                def end_hidden(n):
                    pe.wait_ge(ip_copied, n.g + 1)
                    nc.tensor.matmul(ps_hid[n.two], k.hid_s[:], ip_t[:], start=False, stop=True).then_inc(hidden_in, 1)

                def step(near):
                    here, ahead, behind = near(0), near(1), near(-1)
                    if here.exists():
                        pe.wait_ge(hot_copied, here.g + 1)
                        row_tile = pe.value_load(k.group_tile[0:1, bass.ds(here.g, 1)], min_val=0, max_val=TILES - 1)
                        target(here, row_tile, 0)
                        target(here, row_tile, 1)
                    if behind.exists():
                        ip_flips(behind)
                    if ahead.exists():
                        flips(ahead)
                    if here.exists():
                        target(here, row_tile, 2)
                    if behind.exists():
                        end_hidden(behind)
                    if here.exists():
                        target(here, row_tile, 3)
                        begin_hidden(here, row_tile)

                over_groups(pe, step, 1, 1)

            @block.scalar
            def _(act):
                s = nc.scalar
                act.wait_ge(halved, 1)

                def soften(n):
                    act.wait_ge(hidden_in, n.g + 1)
                    if n.reaches(1):
                        act.wait_ge(hidden_out, n.g)
                    s.activation(size[:], ps_hid[n.two][0:64], ACT.Abs).then_inc(soft, 1)
                    act.wait_ge(soft, 3 * n.g + 1)
                    s.activation(size[:], size[:], ACT.Exp, scale=-1.0).then_inc(soft, 1)
                    act.wait_ge(soft, 3 * n.g + 2)
                    s.activation(size[:], size[:], ACT.Ln, scale=0.5, bias=half[:, 0:1]).then_inc(soft, 1)

                def copy_ip(n):
                    act.wait_ge(ip_flipped, n.g + 1)
                    if n.reaches(1):
                        act.wait_ge(hidden_in, n.g)
                    s.activation(ip_t[:], ps_ip, ACT.Copy).then_inc(ip_copied, 1)

                def cast_part(n, j):
                    if j == 0:
                        act.wait_ge(hidden_out, n.g + 1)
                        if n.reaches(SLOTS):
                            act.wait_ge(stored[n.slot], 64 * n.round)
                    else:
                        act.wait_ge(rest_out, 2 * n.g + 1)
                    s.activation(parts[n.slot][:, j], hidden[:], ACT.Copy).then_inc(cast, 1)

                def copy_hot(n):
                    act.wait_ge(flipped, n.g + 1)
                    if n.reaches(2):
                        act.wait_ge(begun, n.g - 1)
                    s.activation(hot_t[n.two][:], ps_hot, ACT.Copy).then_inc(hot_copied, 1)

                def copy_attr(n):
                    s.activation(attr_t[n.two][:], ps_attr, ACT.Copy).then_inc(attr_copied, 1)

                def step(near):
                    ahead, behind, last = near(1), near(-1), near(-2)
                    if last.exists():
                        soften(last)
                    if behind.exists():
                        copy_ip(behind)
                    if ahead.exists():
                        copy_hot(ahead)
                    if last.exists():
                        cast_part(last, 0)
                    if ahead.exists():
                        copy_attr(ahead)
                    if last.exists():
                        cast_part(last, 1)

                over_groups(act, step, 1, 2)

            @block.vector
            def _(dve):
                v = nc.vector

                def one_hots(n):
                    dve.wait_ge(rec_in[n.slot], 16 * n.round + 16)
                    if n.reaches(2):
                        dve.wait_ge(flipped, n.g - 1)
                    for t in range(SUB):
                        last = v.tensor_scalar(hot[n.two][:, t], k.lane[:], record[n.slot][:, t, C_KEY:C_KEY + 1], None,
                                               ALU.is_equal)
                    last.then_inc(hot_ready, 1)

                def multiply(n, t):
                    e = n.g * SUB + t
                    if t == 0:
                        dve.wait_ge(source_in[n.slot], 64 * n.round + 64)
                    dve.wait_ge(target_out, e + 1)
                    if n.reaches(1) or t >= 2:
                        dve.wait_ge(summed, e - 1)
                    v.tensor_tensor(prod[t % 2][:], ps_target[t % 2].rearrange("p (m u) -> p m u", m=3),
                                    source[n.slot][:, t].rearrange("p (m u) -> p m u", m=3),
                                    ALU.mult).then_inc(multiplied, 1)

                def sum_up(n, t):
                    e = n.g * SUB + t
                    if t == 0 and n.reaches(2):
                        dve.wait_ge(ip_flipped, n.g - 1)
                    dve.wait_ge(multiplied, e + 1)
                    v.tensor_reduce(ip[n.two][:, t], prod[t % 2][:].rearrange("p m u -> p u m"), AX.X,
                                    ALU.add).then_inc(summed, 1)

                def join(n):
                    dve.wait_ge(soft, 3 * n.g + 3)
                    if n.reaches(1):
                        dve.wait_ge(rest_out, 2 * n.g)
                    v.scalar_tensor_tensor(hidden[:], ps_hid[n.two][0:64], 0.0, size[:], ALU.max, ALU.add
                                           ).then_inc(hidden_out, 1)

                def take_off(n, j):
                    dve.wait_ge(cast, 2 * n.g + j + 1)
                    if j:
                        dve.wait_ge(rest_out, 2 * n.g + 1)
                    v.tensor_tensor(hidden[:] if j == 0 else parts[n.slot][:, 2], hidden[:], parts[n.slot][:, j],
                                    ALU.subtract).then_inc(rest_out, 1)

                def step(near):
                    here, ahead, last = near(0), near(1), near(-2)
                    if ahead.exists():
                        one_hots(ahead)
                    if here.exists():
                        multiply(here, 0)
                        multiply(here, 1)
                        sum_up(here, 0)
                    if last.exists():
                        join(last)
                    if here.exists():
                        sum_up(here, 1)
                        multiply(here, 2)
                        multiply(here, 3)
                    if last.exists():
                        take_off(last, 0)
                    if here.exists():
                        sum_up(here, 2)
                        sum_up(here, 3)
                    if last.exists():
                        take_off(last, 1)

                over_groups(dve, step, 1, 2)


def edge_messages(k, summed_x):
    nc = k.nc
    with ExitStack() as ctx:
        def sb(name, shape, dt=F32):
            return ctx.enter_context(nc.sbuf_tensor(name, shape, dt))

        record = [sb(f"rec_m{b}", [P, SUB, REC]) for b in range(SLOTS)]
        source = [sb(f"xsrc{b}", [P, SUB, D]) for b in range(SLOTS)]
        stack = [sb(f"stack{b}", [P, 2, GROUP], BF16) for b in range(SLOTS)]
        hot = [sb(f"mhot{b}", [P, SUB, P]) for b in range(2)]
        left = [sb(f"left{b}", [P, 4, P]) for b in range(2)]
        w = [sb(f"weights{b}", [P, 4, P]) for b in range(2)]
        z = [sb(f"z{b}", [P, P]) for b in range(2)]
        vz = [sb(f"vz{b}", [P, P]) for b in range(2)]
        message = [sb(f"message{t}", [P, 4, P]) for t in range(SUB)]
        second = [sb(f"second{t}", [P, 3, P]) for t in range(SUB)]

        rec_in = [k.sem(f"m_rec_in{b}") for b in range(SLOTS)]
        stack_in = [k.sem(f"m_stack_in{b}") for b in range(SLOTS)]
        source_in = [k.sem(f"m_source_in{b}") for b in range(SLOTS)]
        cleared, hot_ready, weights_in, left_out = k.sem("m_cleared"), k.sem("m_hot"), k.sem("m_weights"), k.sem("m_left")
        work, message_ready, sent = k.sem("m_work"), k.sem("m_ready"), k.sem("m_sent")
        outer_done, added = k.sem("m_outer"), k.sem("m_added")
        z_begun, v_ready, second_ready = k.sem("m_z_begun"), k.sem("m_v_ready"), k.sem("m_second_ready")

        ps_f = [k.psum[:, b].rearrange("p (q u) -> p q u", q=4) for b in range(2)]
        ps_s = [k.psum[:, 2 + b].rearrange("p (q u) -> p q u", q=4) for b in range(2)]
        ps_sum = [k.psum[:, 4 + b] for b in range(2)]
        SH = EA96 + EA32
        WORK = 5

        def at(near, t):
            return near(t // SUB), t % SUB

        with nc.Block() as block:
            @block.sync
            def _(sp):
                for b in range(SLOTS):
                    sp.wait_ge(k.stored[b], GROUPS // SLOTS * 64)

                def fetch(near):
                    n = near(2)
                    if not n.exists():
                        return
                    if n.reaches(SLOTS):
                        sp.wait_ge(sent, (n.g - SLOTS + 1) * SUB)
                        sp.sem_inc(k.sp_ready, 1)
                        sp.wait_ge(source_in[n.slot], 64 * n.round)
                    sp.dma_start(record[n.slot][:], k.records[bass.ds(n.g * GROUP, GROUP), :]
                                 .rearrange("(p t) c -> p t c", p=P)).then_inc(rec_in[n.slot], 16)
                    for blk in range(4):
                        sp.dma_start(stack[n.slot][32 * blk:32 * blk + 32],
                                     k.stack_d[bass.ds(n.g * 256 + blk * 64, 64), :]
                                     .rearrange("(s r) c -> r s c", s=2)).then_inc(stack_in[n.slot], 16)

                over_groups(sp, fetch, 2, 0)

            @block.gpsimd
            def _(pool):
                nc.gpsimd.memset(summed_x[:], 0.0).then_inc(cleared, 1)

                def gather(n):
                    pool.wait_ge(rec_in[n.slot], 16 * n.round + 16)
                    if n.reaches(SLOTS):
                        pool.wait_ge(message_ready, (n.g - SLOTS + 1) * SUB)
                    pool.wait_ge(k.tables, 32)
                    pool.sem_inc(k.pool_ready, 1)
                    for t in range(SUB):
                        nc.gpsimd.indirect_dma_start(
                            source[n.slot][:, t, :], None, k.xs_d[:, :],
                            bass.IndirectOffsetOnAxis(ap=record[n.slot][:, t, C_OTHER:C_OTHER + 1].bitcast(I32), axis=0)
                        ).then_inc(source_in[n.slot], 16)

                def one_hots(n):
                    if n.reaches(2):
                        pool.wait_ge(sent, (n.g - 1) * SUB)
                        pool.sem_inc(k.pool_ready, 1)
                    for t in range(SUB):
                        last = nc.gpsimd.tensor_scalar(hot[n.two][:, t], k.lane[:], record[n.slot][:, t, C_KEY:C_KEY + 1],
                                                       None, ALU.is_equal)
                    last.then_inc(hot_ready, 1)

                def step(near):
                    if near(1).exists():
                        gather(near(1))
                    if near(0).exists():
                        one_hots(near(0))

                over_groups(pool, step, 1, 0)

            @block.tensor
            def _(pe):
                def mix(n, t):
                    e = n.g * SUB + t
                    if t == 0:
                        pe.wait_ge(stack_in[n.slot], 64 * n.round + 64)
                    if n.reaches(1) or t >= 2:
                        pe.wait_ge(outer_done, e - 1)
                    for ps, kind in ((ps_f, 0), (ps_s, 1)):
                        for j in range(2):
                            last = nc.tensor.matmul(ps[t % 2].rearrange("p q u -> p (q u)"),
                                                    stack[n.slot][:, kind, t * P:(t + 1) * P], k.mix[:, kind, j],
                                                    start=j == 0, stop=j == 1)
                    last.then_inc(weights_in, 1)

                def send(n, t):
                    e = n.g * SUB + t
                    if t == 0:
                        pe.wait_ge(hot_ready, n.g + 1)
                        if n.reaches(2):
                            pe.wait_ge(added, n.g - 1)
                    pe.wait_ge(message_ready, e + 1)
                    nc.tensor.matmul(ps_sum[n.two], hot[n.two][:, t], message[t][:].rearrange("p q u -> p (q u)"),
                                     start=t == 0, stop=False)
                    pe.wait_ge(second_ready, e + 1)
                    nc.tensor.matmul(ps_sum[n.two][:, P:D], hot[n.two][:, t], second[t][:].rearrange("p q u -> p (q u)"),
                                     start=False, stop=t == SUB - 1).then_inc(sent, 1)

                def step(near):
                    for t in range(SUB):
                        if at(near, t + 1)[0].exists():
                            mix(*at(near, t + 1))
                        if at(near, t - 1)[0].exists():
                            send(*at(near, t - 1))

                over_groups(pe, step, 1, 1)

            @block.scalar
            def _(act):
                def left_factor(n, t):
                    e = n.g * SUB + t
                    if t == 0:
                        act.wait_ge(rec_in[n.slot], 16 * n.round + 16)
                    act.wait_ge(weights_in, e + 1)
                    if n.reaches(1) or t >= 2:
                        act.wait_ge(outer_done, e - 1)
                    nc.scalar.activation(left[t % 2][:, 0:4:2], ps_f[t % 2][:, 0:4:2], ACT.Copy,
                                         scale=record[n.slot][:, t, SH:SH + 1]).then_inc(left_out, 1)
                    nc.scalar.activation(left[t % 2][:, 1:4:2], ps_f[t % 2][:, 1:4:2], ACT.Copy).then_inc(left_out, 1)

                def begin_z(n, t):
                    e = n.g * SUB + t
                    if t == 0:
                        act.wait_ge(source_in[n.slot], 64 * n.round + 64)
                    if n.reaches(1) or t >= 2:
                        act.wait_ge(message_ready, e - 1)
                    nc.scalar.activation(z[t % 2][:], source[n.slot][:, t, P:2 * P], ACT.Copy,
                                         scale=record[n.slot][:, t, SH + 1:SH + 2]).then_inc(z_begun, 1)

                def second_part(n, t):
                    e = n.g * SUB + t
                    act.wait_ge(v_ready, e + 1)
                    if n.reaches(1):
                        act.wait_ge(sent, e - SUB + 1)
                    for m in range(3):
                        last = nc.scalar.activation(second[t][:, m], vz[t % 2][:], ACT.Copy,
                                                    scale=record[n.slot][:, t, SH + 1 + m:SH + 2 + m])
                    last.then_inc(second_ready, 1)

                def step(near):
                    for t in range(SUB):
                        if at(near, t + 1)[0].exists():
                            left_factor(*at(near, t + 1))
                            begin_z(*at(near, t + 1))
                        if near(0).exists():
                            second_part(near(0), t)

                over_groups(act, step, 1, 0)

            @block.vector
            def _(dve):
                v = nc.vector
                dve.wait_ge(cleared, 1)

                def tile(n, t):
                    e = n.g * SUB + t
                    st = Steps(dve, work, e * WORK)
                    x0 = source[n.slot][:, t, 0:P]
                    x1 = source[n.slot][:, t, P:D].rearrange("p (m u) -> p m u", m=3)
                    sh = [record[n.slot][:, t, SH + 1 + m:SH + 2 + m] for m in range(3)]
                    wt, zt, vt, mt = w[t % 2], z[t % 2], vz[t % 2], message[t]
                    if n.reaches(1) or t >= 2:
                        dve.wait_ge(message_ready, e - 1)
                        dve.wait_ge(second_ready, e - 1)
                    dve.wait_ge(left_out, 2 * e + 2)
                    v.tensor_tensor(wt[:], left[t % 2][:], ps_s[t % 2], ALU.mult).then_inc(outer_done, 1)
                    dve.wait_ge(z_begun, e + 1)
                    st.done(v.scalar_tensor_tensor(zt[:], x1[:, 1], sh[1], zt[:], ALU.mult, ALU.add))
                    dve.wait_ge(outer_done, e + 1)
                    v.tensor_tensor(vt[:], wt[:, 1], x0, ALU.mult).then_inc(v_ready, 1)
                    st.settle()
                    st.done(v.scalar_tensor_tensor(zt[:], x1[:, 2], sh[2], zt[:], ALU.mult, ALU.add))
                    if n.reaches(1):
                        dve.wait_ge(sent, e - SUB + 1)
                    st.done(v.tensor_tensor(mt[:, 0], wt[:, 0], x0, ALU.mult))
                    dve.wait_ge(work, e * WORK + 2)
                    st.done(v.tensor_tensor(zt[:], zt[:], wt[:, 3], ALU.mult))
                    st.done(v.tensor_tensor(mt[:, 1:4], x1, wt[:, 2:3].broadcast_to([P, 3, P]), ALU.mult))
                    dve.wait_ge(work, e * WORK + 4)
                    v.tensor_tensor(mt[:, 0], mt[:, 0], zt[:], ALU.add).then_inc(message_ready, 1)
                    assert st.n == WORK

                def add(n):
                    dve.wait_ge(sent, n.g * SUB + SUB)
                    if n.reaches(1):
                        dve.wait_ge(added, n.g)
                    nt = dve.value_load(k.group_tile[0:1, bass.ds(n.g, 1)], min_val=0, max_val=TILES - 1)
                    here = summed_x[:, bass.ds(nt * D, D)]
                    v.tensor_tensor(here, here, ps_sum[n.two], ALU.add).then_inc(added, 1)

                def step(near):
                    for t in range(SUB):
                        if near(0).exists():
                            if t == 0:
                                dve.wait_ge(source_in[near(0).slot], 64 * near(0).round + 64)
                            tile(near(0), t)
                        if t == 1 and near(-1).exists():
                            add(near(-1))

                over_groups(dve, step, 0, 1)


def tensor_output(k, summed_x, xs_in):
    nc, a = k.nc, k.a
    with ExitStack() as ctx:
        def sb(name, shape, dt=F32):
            return ctx.enter_context(nc.sbuf_tensor(name, shape, dt))

        wo0, wo1, bo0 = sb("wo0", [P, P]), sb("wo1", [P, P]), sb("bo0", [1, P])
        own = sb("own", [P, TILES * D])
        zt = sb("zt", [P, 4, COLS])
        y = sb("y1", [P, TILES, D])
        loaded, joined = k.sem("out_loaded"), k.sem("own_joined")
        n = load(k, loaded, [(own[:].rearrange("p (t c) -> p t c", c=D), k.xs_d.rearrange("(t p) c -> p t c", p=P)),
                             (wo0[:], a["L1_gnn_W_o0"]), (wo1[:], a["L1_gnn_W_o1"]), (bo0[:], row_of(a["L1_gnn_b_o0"]))])
        with nc.Block() as block:
            @block.vector
            def _(dve):
                dve.wait_ge(loaded, n)
                nc.vector.tensor_tensor(own[:], own[:], summed_x[:], ALU.add).then_inc(joined, 1)
        flip(k, TILES, (lambda t, j: own[:, t * D + j * P:t * D + j * P + P], 4),
             lambda j, w, t: zt[:, j:j + w, t * P:(t + 1) * P], [(loaded, n)])

        def finish(act, t, ps):
            copy_to(k, act, y[:, t, 0:P], ps[:, 0:P])
            return copy_to(k, act, y[:, t, P:D].rearrange("p (u m) -> p m u", m=3),
                           ps[:, P:D].rearrange("p (m u) -> p m u", m=3))

        rows_out(k, lambda t: [(zt[:, 0, t * P:(t + 1) * P], wo0[:], slice(0, P)), (k.ones[0:1, :], bo0[:], slice(0, P))]
                 + [(zt[:, 1 + m, t * P:(t + 1) * P], wo1[:], slice((1 + m) * P, (2 + m) * P)) for m in range(3)],
                 finish)

        def residual(v, st):
            st.done(v.scalar_tensor_tensor(k.x[:].rearrange("p t d -> p (t d)"), k.x[:].rearrange("p t d -> p (t d)"), 2.0,
                                           y[:].rearrange("p t d -> p (t d)"), ALU.mult, ALU.add))

        normalize(k, D, k.x, TILES, D, before=residual)


def mean_layer(k):
    nc, a = k.nc, k.a
    with ExitStack() as ctx:
        def sb(name, shape, dt=F32):
            return ctx.enter_context(nc.sbuf_tensor(name, shape, dt))

        wl, wr = sb("wl", [P, 4, D]), sb("wr", [P, 4, D])
        bl, g, be = sb("bl", [P, 4]), sb("g2", [P, 4]), sb("be2", [P, 4])
        mean_t = sb("mean_t", [P, 4, COLS])
        inv = sb("inv", [P, TILES])
        loaded, loaded_c, degree = k.sem("mean_loaded"), k.sem("counts_in"), k.sem("degree")
        with ExitStack() as inner:
            mean = inner.enter_context(nc.sbuf_tensor("mean", [P, TILES, D], F32))
            ct = inner.enter_context(nc.sbuf_tensor("ct", [P, TILES, COLS], F32))
            with ExitStack() as inmost:
                c = inmost.enter_context(nc.sbuf_tensor("c", [P, TILES, COLS], F32))
                nl = load(k, loaded_c, [(ct[:].rearrange("p t s -> p (t s)"), k.counts_d[:, :])])
                n = load(k, loaded, [(wl[:], weight(a["L2_gnn_W_l"])), (wr[:], weight(a["L2_gnn_W_r"])),
                                     (bl[:], columns(a["L2_gnn_b_l"])), (g[:], columns(a["L2_gnn_gamma"])),
                                     (be[:], columns(a["L2_gnn_beta"]))])
                flip(k, TILES, (lambda t, j: ct[:, t, j * P:(j + 1) * P], TILES),
                     lambda j, w, t: c[:, j:j + w, t * P:(t + 1) * P], [(loaded_c, nl)])
                with nc.Block() as block:
                    @block.sync
                    def _(sp):
                        sp.dma_start(k.by_target_d[:, :], c[:].rearrange("p t s -> p (t s)")).then_inc(loaded_c, 16)
                        sp.wait_ge(loaded_c, nl + 16)

                    @block.vector
                    def _(dve):
                        st = Steps(dve, degree)
                        st.done(nc.vector.tensor_reduce(inv[:], c[:], AX.X, ALU.add))
                        st.settle()
                        st.done(nc.vector.tensor_scalar(inv[:], inv[:], 1.0, None, ALU.max))
                        st.settle()
                        st.done(nc.vector.reciprocal(inv[:], inv[:]))
                        st.settle()

            def finish(act, t, ps):
                if act:
                    return nc.scalar.activation(mean[:, t], ps, ACT.Copy, scale=inv[:, t:t + 1])
                return nc.vector.tensor_scalar(mean[:, t], ps, inv[:, t:t + 1], None, ALU.mult)

            rows_out(k, lambda t: [(ct[:, s, t * P:(t + 1) * P], k.x[:, s], slice(0, D)) for s in range(TILES)], finish)
            flip(k, TILES, (lambda t, j: mean[:, t, j * P:(j + 1) * P], 4),
                 lambda j, w, t: mean_t[:, j:j + w, t * P:(t + 1) * P])
        xt, h = sb("xt2", [P, 4, COLS]), sb("h_2", [P, 4, COLS])
        flip(k, TILES, (lambda t, j: k.x[:, t, j * P:(j + 1) * P], 4),
             lambda j, w, t: xt[:, j:j + w, t * P:(t + 1) * P])
        features_out(k, 4, lambda j: [(wl[:, i, j * P:(j + 1) * P], mean_t[:, i]) for i in range(4)]
                     + [(wr[:, i, j * P:(j + 1) * P], xt[:, i]) for i in range(4)],
                     lambda act, j, at, ps: add_bias(k, act, h[:, j, at], ps, bl[:, j:j + 1], relu=True), [(loaded, n)])
        normalize(k, NODES, h, 4, COLS, scale=g, shift=be)
        join_rows(k, h)


def join_rows(k, h, scale=None, shift=None):
    with ExitStack() as ctx:
        rows = ctx.enter_context(k.nc.sbuf_tensor(f"rows{k.root_n}", [P, TILES, D], F32))
        batch = [(j, t) for j in range(4) for t in range(TILES)]

        def fill(n, bank):
            for j in range(4):
                last = k.nc.tensor.transpose(bank[:, j * P:(j + 1) * P], h[:, j, n * P:(n + 1) * P], k.ident[:])
            return last

        through_banks(k, TILES, fill, lambda act, n, bank: copy_to(k, act, rows[:, n], bank))
        if scale is not None:
            normalize(k, D, rows, TILES, D, scale=scale, shift=shift)

        def residual(v, st):
            st.done(v.tensor_tensor(k.x[:], k.x[:], rows[:], ALU.add))

        normalize(k, D, k.x, TILES, D, before=residual)


def attention(k, qt, kt, vr, agg):
    nc = k.nc
    with ExitStack() as ctx:
        k.names += 1
        names = k.names

        def sb(name, shape, dt=F32):
            return ctx.enter_context(nc.sbuf_tensor(f"{name}_{names}", shape, dt))

        def sem(name):
            return k.sem(f"{name}_{names}")

        c = [sb(f"c{b}", [P, COLS]) for b in range(2)]
        far = [sb(f"far{b}", [P, COLS]) for b in range(2)]
        q = [sb(f"q{b}", [P, 4, P]) for b in range(2)]
        s = [sb(f"s{b}", [P, COLS]) for b in range(2)]
        p = [sb(f"p{b}", [P, COLS]) for b in range(2)]
        pt = [sb(f"pt{b}", [P, TILES, P]) for b in range(2)]
        top = [sb(f"top{b}", [P, 4]) for b in range(4)]

        c_in = [sem(f"c_in{b}") for b in range(2)]
        q_in, far_ready = sem("q_in"), sem("far_ready")
        scored, masked, negated, raised = sem("scored"), sem("masked"), sem("negated"), sem("raised")
        weighed, inverted, turned, turned_out = sem("weighed"), sem("inverted"), sem("turned"), sem("turned_out")
        mixed, written = sem("mixed"), sem("written")

        ps_s = k.psum[:, 0:3].rearrange("p c n -> p (c n)")
        ps_t = k.psum[:, 3:6].rearrange("p c n -> p (c n)")
        ps_o = [k.psum[:, 6 + b, 0:DH] for b in range(2)]

        def heads(step):
            def tile(near):
                for h in range(HEADS):
                    step(lambda d: (near((h + d) // HEADS), (h + d) % HEADS))
            return tile

        with nc.Block() as block:
            @block.sync
            def _(sp):
                def fetch(near):
                    n = near(1)
                    if n.exists():
                        if n.reaches(2):
                            sp.wait_ge(weighed, (n.g - 1) * HEADS)
                            sp.wait_ge(far_ready, n.g - 1)
                        sp.dma_start(c[n.two][:], k.by_target_d[:, bass.ds(n.g * COLS, COLS)]).then_inc(c_in[n.two], 16)

                over_tiles(sp, fetch, 1, 0)

            @block.gpsimd
            def _(pool):
                def prepare(near):
                    n = near(1)
                    if n.exists():
                        if n.reaches(2):
                            pool.wait_ge(masked, (n.g - 1) * HEADS)
                            pool.sem_inc(k.pool_ready, 1)
                        nc.gpsimd.tensor_copy(q[n.two][:], qt[:, :, bass.ds(n.g * P, P)]).then_inc(q_in, 1)
                        pool.wait_ge(c_in[n.two], n.round * 16 + 16)
                        pool.sem_inc(k.pool_ready, 1)
                        nc.gpsimd.tensor_scalar(far[n.two][:], c[n.two][:], 0.0, FAR, ALU.is_equal, ALU.mult
                                                ).then_inc(far_ready, 1)

                over_tiles(pool, prepare, 1, 0)

            @block.tensor
            def _(pe):
                def score(n, h):
                    e = n.g * HEADS + h
                    if h == 0:
                        pe.wait_ge(q_in, n.g + 1)
                    if n.reaches(1) or h >= 1:
                        pe.wait_ge(masked, e)
                    rows = slice(DH * (h % 2), DH * (h % 2) + DH)
                    for c0, cw in CHUNKS:
                        last = nc.tensor.matmul(ps_s[:, c0:c0 + cw], q[n.two][rows, h // 2], kt[rows, h // 2, c0:c0 + cw],
                                                start=True, stop=True)
                    last.then_inc(scored, 1)

                def turn(n, h):
                    e = n.g * HEADS + h
                    pe.wait_ge(weighed, e + 1)
                    if n.reaches(1) or h >= 1:
                        pe.wait_ge(turned_out, e)
                    for j in range(TILES):
                        last = nc.tensor.transpose(ps_t[:, j * P:(j + 1) * P], p[h % 2][:, j * P:(j + 1) * P], k.ident[:])
                    last.then_inc(turned, 1)

                def mix(n, h):
                    e = n.g * HEADS + h
                    pe.wait_ge(turned_out, e + 1)
                    if n.reaches(1) or h >= 2:
                        pe.wait_ge(written, e - 1)
                    for j in range(TILES):
                        last = nc.tensor.matmul(ps_o[h % 2], pt[h % 2][:, j], vr[:, j, h * DH:(h + 1) * DH],
                                                start=j == 0, stop=j == TILES - 1)
                    last.then_inc(mixed, 1)

                def step(head):
                    if head(1)[0].exists():
                        score(*head(1))
                    if head(-1)[0].exists():
                        mix(*head(-1))
                    if head(0)[0].exists():
                        turn(*head(0))

                over_tiles(pe, heads(step), 1, 1)

            @block.scalar
            def _(act):
                def raise_(n, h):
                    act.wait_ge(negated, n.g * HEADS + h + 1)
                    nc.scalar.activation(s[h % 2][:], s[h % 2][:], ACT.Exp, bias=top[h % 4][:, 1:2]).then_inc(raised, 1)

                def turn(n, h):
                    e = n.g * HEADS + h
                    act.wait_ge(turned, e + 1)
                    if n.reaches(1) or h >= 2:
                        act.wait_ge(mixed, e - 1)
                    nc.scalar.activation(pt[h % 2][:], ps_t[:, 0:COLS].rearrange("p (j n) -> p j n", n=P),
                                         ACT.Copy).then_inc(turned_out, 1)

                def step(head):
                    if head(1)[0].exists():
                        raise_(*head(1))
                    if head(0)[0].exists():
                        turn(*head(0))

                over_tiles(act, heads(step), 1, 0)

            @block.vector
            def _(dve):
                v = nc.vector

                def mask(n, h):
                    e = n.g * HEADS + h
                    if h == 0:
                        dve.wait_ge(far_ready, n.g + 1)
                    dve.wait_ge(scored, e + 1)
                    if n.reaches(1) or h >= 2:
                        dve.wait_ge(weighed, e - 1)
                    if n.reaches(1) or h >= 4:
                        dve.wait_ge(written, e - 3)
                    dve.sem_inc(k.dve_ready, 1)
                    v.tensor_tensor_reduce(out=s[h % 2][:], in0=ps_s[:, 0:COLS], in1=far[n.two][:], scale=1.0,
                                           scalar=2 * FAR, op0=ALU.add, op1=ALU.max,
                                           accum_out=top[h % 4][:, 0:1]).then_inc(masked, 1)
                    dve.wait_ge(masked, e + 1)
                    v.tensor_scalar(top[h % 4][:, 1:2], top[h % 4][:, 0:1], -1.0, None, ALU.mult).then_inc(negated, 1)

                def weigh(n, h):
                    e = n.g * HEADS + h
                    dve.wait_ge(raised, e + 1)
                    if n.reaches(1) or h >= 2:
                        dve.wait_ge(turned, e - 1)
                    v.tensor_tensor_reduce(out=p[h % 2][:], in0=s[h % 2][:], in1=c[n.two][:], scale=1.0, scalar=0.0,
                                           op0=ALU.mult, op1=ALU.add, accum_out=top[h % 4][:, 2:3]).then_inc(weighed, 1)

                def invert(n, h):
                    e = n.g * HEADS + h
                    dve.wait_ge(weighed, e + 1)
                    v.tensor_scalar(top[h % 4][:, 3:4], top[h % 4][:, 2:3], 1e-16, None, ALU.add).then_inc(inverted, 1)
                    dve.wait_ge(inverted, 2 * e + 1)
                    v.reciprocal(top[h % 4][:, 3:4], top[h % 4][:, 3:4]).then_inc(inverted, 1)

                def write(n, h):
                    e = n.g * HEADS + h
                    dve.wait_ge(mixed, e + 1)
                    dve.wait_ge(inverted, 2 * e + 2)
                    v.tensor_scalar(agg[:, bass.ds(n.g * D + h * DH, DH)], ps_o[h % 2], top[h % 4][:, 3:4], None,
                                    ALU.mult).then_inc(written, 1)

                def step(head):
                    if head(0)[0].exists():
                        weigh(*head(0))
                    if head(1)[0].exists():
                        mask(*head(1))
                    if head(0)[0].exists():
                        invert(*head(0))
                    if head(-1)[0].exists():
                        write(*head(-1))

                over_tiles(dve, heads(step), 1, 1)


def attention_layers(k):
    nc, a = k.nc, k.a
    with ExitStack() as ctx:
        def sb(name, shape, dt=F32):
            return ctx.enter_context(nc.sbuf_tensor(name, shape, dt))

        wq, wk, wv, wo = (sb(n, [P, 4, D]) for n in ("wq", "wk", "wv", "wo"))
        w1, w2 = sb("wf1", [P, 4, FF]), sb("wf2", [P, 2, D])
        vectors = [("bq", 4), ("bo", 4), ("b1", 2), ("b2", 4), ("g1", 4), ("beta1", 4), ("g2", 4), ("beta2", 4)]
        small = {n: sb("l3_" + n, [P, w]) for n, w in vectors}
        lg, lb = sb("lg", [P, D]), sb("lb", [P, D])
        xt = sb("xt3", [P, 4, COLS])
        kept, loaded, scaled = k.sem("x_kept"), k.sem("att_loaded"), k.sem("bq_scaled")
        nl = 0
        flip(k, TILES, (lambda t, j: k.x[:, t, j * P:(j + 1) * P], 4),
             lambda j, w, t: xt[:, j:j + w, t * P:(t + 1) * P])
        with nc.Block() as block:
            @block.sync
            def _(sp):
                sp.dma_start(k.x_d[:, :], k.x[:].rearrange("p t d -> p (t d)")).then_inc(kept, 16)
                sp.wait_ge(kept, 16)
        agg = k.x[:].rearrange("p t d -> p (t d)")
        for layer in range(2):
            pairs = [(wq[:], weight(a["L3_gnn_Wq"][layer])), (wk[:], weight(a["L3_gnn_Wk"][layer])),
                     (wv[:], weight(a["L3_gnn_Wv"][layer])), (wo[:], weight(a["L3_gnn_Wo"][layer])),
                     (w1[:], weight(a["L3_gnn_W1"][layer])), (w2[:], weight(a["L3_gnn_W2"][layer]))]
            pairs += [(small[n][:], columns(a["L3_gnn_" + n][layer])) for n, _ in vectors]
            if layer == 0:
                pairs += [(lg[:], spread(a["L3_gnn_ln_g"])), (lb[:], spread(a["L3_gnn_ln_b"]))]
            nl += load(k, loaded, pairs)
            with nc.Block() as block:
                @block.vector
                def _(dve):
                    dve.wait_ge(loaded, nl)
                    nc.vector.tensor_scalar(small["bq"][:], small["bq"][:], DH ** -0.5, None, ALU.mult).then_inc(scaled, 1)
            with ExitStack() as inner:
                with ExitStack() as inmost:
                    qt = inmost.enter_context(nc.sbuf_tensor(f"qt{layer}", [P, 4, COLS], F32))
                    kt = inmost.enter_context(nc.sbuf_tensor(f"kt{layer}", [P, 4, COLS], F32))
                    vr = inmost.enter_context(nc.sbuf_tensor(f"vr{layer}", [P, TILES, D], F32))

                    def scaled_q(act, j, at, ps):
                        if act:
                            return nc.scalar.activation(qt[:, j, at], ps, ACT.Identity, bias=small["bq"][:, j:j + 1],
                                                        scale=DH ** -0.5)
                        return nc.vector.tensor_scalar(qt[:, j, at], ps, DH ** -0.5, small["bq"][:, j:j + 1], ALU.mult, ALU.add)

                    features_out(k, 4, lambda j: [(wq[:, i, j * P:(j + 1) * P], xt[:, i]) for i in range(4)], scaled_q,
                                 [(loaded, nl)])
                    features_out(k, 4, lambda j: [(wk[:, i, j * P:(j + 1) * P], xt[:, i]) for i in range(4)],
                                 lambda act, j, at, ps: copy_to(k, act, kt[:, j, at], ps))
                    rows_out(k, lambda t: [(xt[:, i, t * P:(t + 1) * P], wv[:, i], slice(0, D)) for i in range(4)],
                             lambda act, t, ps: copy_to(k, act, vr[:, t], ps))
                    attention(k, qt, kt, vr, agg)
                at_ = inner.enter_context(nc.sbuf_tensor(f"agg_t{layer}", [P, 4, COLS], F32))
                new = inner.enter_context(nc.sbuf_tensor(f"new{layer}", [P, 4, COLS], F32))
                ff = inner.enter_context(nc.sbuf_tensor(f"ff{layer}", [P, 2, COLS], F32))
                flip(k, TILES, (lambda t, j: agg[:, t * D + j * P:t * D + (j + 1) * P], 4),
                     lambda j, w, t: at_[:, j:j + w, t * P:(t + 1) * P])
                features_out(k, 4, lambda j: [(wo[:, i, j * P:(j + 1) * P], at_[:, i]) for i in range(4)],
                             lambda act, j, at, ps: add_bias(k, act, new[:, j, at], ps, small["bo"][:, j:j + 1]))

                def plus(v, st):
                    st.done(v.tensor_tensor(xt[:], xt[:], new[:], ALU.add))

                normalize(k, NODES, xt, 4, COLS, scale=small["g1"], shift=small["beta1"], before=plus)
                features_out(k, 2, lambda j: [(w1[:, i, j * P:(j + 1) * P], xt[:, i]) for i in range(4)],
                             lambda act, j, at, ps: add_bias(k, act, ff[:, j, at], ps, small["b1"][:, j:j + 1], relu=True))
                features_out(k, 4, lambda j: [(w2[:, i, j * P:(j + 1) * P], ff[:, i]) for i in range(2)],
                             lambda act, j, at, ps: add_bias(k, act, new[:, j, at], ps, small["b2"][:, j:j + 1]))
                normalize(k, NODES, xt, 4, COLS, scale=small["g2"], shift=small["beta2"], before=plus)
        with nc.Block() as block:
            @block.sync
            def _(sp):
                sp.dma_start(agg, k.x_d[:, :]).then_inc(kept, 16)
                sp.wait_ge(kept, 32)
        join_rows(k, xt, lg, lb)


def program(nc, a, out):
    with ExitStack() as ctx:
        ctx.enter_context(nc.allow_non_contiguous_dma("rows of records"))
        k = Core(nc, ctx, a)
        k.records = nc.dram_tensor("records", [GROUPS * GROUP, REC], F32).ap()
        k.counts_d = nc.dram_tensor("counts_d", [P, TILES * COLS], F32).ap()
        k.lane = k.keep("lane", [P, P], F16)
        k.node = k.keep("node", [P, COLS], F16)
        k.ident = k.keep("ident", [P, P])
        k.ident_b = k.keep("ident_b", [P, P], BF16)
        k.group_tile = k.keep("group_tile_i", [P, GROUPS], I32)
        k.sums_t = k.keep("sums_t", [EA96, COLS])
        k.ones = k.keep("ones_row", [P, P])
        k.x = k.keep("x_rows", [P, TILES, D])
        k.filled, k.by_act, k.by_dve = k.sem("bank_filled"), k.sem("bank_out_act"), k.sem("bank_out_dve")
        k.filled_n = k.by_act_n = k.by_dve_n = 0
        k.norm, k.variances, k.roots = k.sem("norm_steps"), k.sem("variances"), k.sem("roots")
        k.norm_n = k.root_n = 0
        k.p1_d = nc.dram_tensor("p1_d", [COLS, 384], F32).ap()
        k.xs_d = nc.dram_tensor("xs_d", [COLS, D], F32).ap()
        k.by_target_d = nc.dram_tensor("by_target_d", [P, TILES * COLS], F32).ap()
        k.x_d = nc.dram_tensor("x_d", [P, TILES * D], F32).ap()
        k.stack_d = nc.dram_tensor("stack_d", [GROUPS * 256, GROUP], BF16).ap()
        k.x_loaded = k.sem("x_loaded")
        k.pool_ready, k.dve_ready, k.sp_ready = k.sem("pool_ready"), k.sem("dve_ready"), k.sem("sp_ready")
        x_cleared = k.sem("x_cleared")
        with nc.Block() as block:
            @block.gpsimd
            def _(pool):
                nc.gpsimd.memset(k.x[:, TILES - 1], 0.0).then_inc(x_cleared, 1)
                nc.gpsimd.memset(k.ones[:], 1.0).then_inc(x_cleared, 1)

            @block.sync
            def _(sp):
                whole = (TILES - 1) * P
                sp.dma_start(k.x[:, 0:TILES - 1], a["x"][0:whole, :].rearrange("(t p) d -> p t d", p=P)).then_inc(k.x_loaded, 16)
                sp.wait_ge(x_cleared, 2)
                sp.dma_start(k.x[0:LAST, TILES - 1], a["x"][whole:NODES, :]).then_inc(k.x_loaded, 16)

        sort_edges(k)
        count_edges(k)
        mlp_layer(k)
        with ExitStack() as tensor_layer:
            tensor_nodes(k, tensor_layer)
            edge_hidden(k)
            summed_x = tensor_layer.enter_context(nc.sbuf_tensor("summed_x", [P, TILES * D], F32))
            edge_messages(k, summed_x)
            tensor_output(k, summed_x, None)
        mean_layer(k)
        attention_layers(k)
        if out is None:
            out = nc.dram_tensor("out", [NODES, D], F32, kind="ExternalOutput").ap()
        returned = k.sem("returned")
        with nc.Block() as block:
            @block.sync
            def _(sp):
                whole = (TILES - 1) * P
                sp.dma_start(out[0:whole, :].rearrange("(t p) d -> p t d", p=P), k.x[:, 0:TILES - 1]).then_inc(returned, 16)
                sp.dma_start(out[whole:NODES, :], k.x[0:LAST, TILES - 1]).then_inc(returned, 16)
                sp.wait_ge(returned, 32)


TURNED = ("L2_gnn_W_l", "L2_gnn_W_r", "L3_gnn_Wq", "L3_gnn_Wk", "L3_gnn_Wv", "L3_gnn_Wo", "L3_gnn_W1", "L3_gnn_W2")


def layout(name, array):
    return array.swapaxes(-1, -2) if name in TURNED else array


def kernel(**inputs):
    import numpy as np
    from concourse import bacc
    from concourse.bass_utils import run_bass_kernel_spmd

    nc = bacc.Bacc("TRN2", target_bir_lowering=False, num_devices=1)
    arrays, handles = {}, {}
    for name, array in inputs.items():
        arrays["in_" + name] = np.ascontiguousarray(layout(name, np.asarray(array)))
        handles[name] = nc.dram_tensor("in_" + name, arrays["in_" + name].shape,
                                       mybir.dt.from_np(arrays["in_" + name].dtype), kind="ExternalInput").ap()
    out = nc.dram_tensor("out_0", (NODES, D), F32, kind="ExternalOutput").ap()
    program(nc, handles, out)
    got = run_bass_kernel_spmd(nc, [arrays], core_ids=[0])
    return got.results[0]["out_0"]
```

```python
from contextlib import ExitStack

import concourse.bass as bass
from concourse import mybir

P = 128
NODES, EDGES, D = 1250, 40000, 512
TILES = -(-NODES // P)
COLS = TILES * P
LAST = NODES - (TILES - 1) * P
SUB = 4
SLOTS = 4
GROUP = SUB * P
GROUPS = (EDGES + TILES * (GROUP - 1)) // GROUP
GROUPS += -GROUPS % SLOTS
FULL = -(-EDGES // GROUP)
EP = 125
EF = EDGES // EP
CHUNK = 16
EA96, EA32, EA4 = 96, 32, 4
C_OTHER = EA96 + EA32 + EA4
C_KEY = C_OTHER + 1
REC = C_OTHER + 4
BANK = 512
CHUNKS = tuple((c, min(BANK, COLS - c)) for c in range(0, COLS, BANK))
EPS = 1e-5
HEADS, DH = 8, 64
FF = 256
FAR = -1.0e30
HID = 64
PAD = 3 * HID

F32 = mybir.dt.float32
F16 = mybir.dt.float16
BF16 = mybir.dt.bfloat16
I32 = mybir.dt.int32
ALU = mybir.AluOpType
ACT = mybir.ActivationFunctionType
AX = mybir.AxisListType


class Steps:

    def __init__(self, engine, sem, base=0):
        self.engine, self.sem, self.base, self.n = engine, sem, base, 0

    def done(self, ins):
        ins.then_inc(self.sem, 1)
        self.n += 1

    def settle(self):
        self.engine.wait_ge(self.sem, self.base + self.n)


class Core:

    def __init__(self, nc, ctx, a):
        self.nc, self.ctx, self.a = nc, ctx, a
        self.psum = ctx.enter_context(nc.psum_tensor("psum", [P, 8, BANK], F32))
        self.names = 0

    def sem(self, name):
        return self.ctx.enter_context(self.nc.semaphore(name))

    def keep(self, name, shape, dt=F32):
        return self.ctx.enter_context(self.nc.sbuf_tensor(name, shape, dt))


class Turn:

    def __init__(self, rnd, slot, slots, count):
        self.round, self.slot = rnd + slot // slots, slot % slots
        self.g = self.round * slots + self.slot
        self.count = count
        self.fixed = isinstance(rnd, int)
        self.two = self.slot % 2

    def exists(self):
        return not self.fixed or 0 <= self.g < self.count

    def reaches(self, g):
        return not self.fixed or self.g >= g


def in_turn(engine, step, ahead, behind, slots, count, peeled):
    def at(rnd, slot):
        step(lambda d: Turn(rnd, slot + d, slots, count))

    for g in range(-ahead, peeled * slots):
        at(0, g)
    with engine.Fori(peeled, count // slots - 1) as i:
        for slot in range(slots):
            at(i, slot)
    for g in range(count - slots, count + behind):
        at(0, g)


def over_groups(engine, step, ahead, behind):
    in_turn(engine, step, ahead, behind, SLOTS, GROUPS, 2)


def over_tiles(engine, step, ahead, behind):
    in_turn(engine, step, ahead, behind, 2, TILES, 1)


def sort_edges(k):
    nc, a = k.nc, k.a
    with ExitStack() as ctx:
        def sb(name, shape, dt=F32):
            return ctx.enter_context(nc.sbuf_tensor(name, shape, dt))

        key_i = sb("key_i", [EP, EF], I32)
        other_i = sb("other_i", [EP, EF], I32)
        other_f = sb("other_f", [EP, EF])
        tile_i = sb("tile_i", [EP, EF], I32)
        tile_f = sb("tile_f", [EP, EF])
        key_f = sb("key_f", [EP, EF])
        local = sb("local", [EP, EF])
        ones = sb("ones", [EP, EF])
        member = sb("member", [EP, TILES, EF])
        rank = sb("rank", [EP, TILES, EF])
        total = sb("total", [EP, TILES])
        before = sb("before", [EP, EP])
        every = sb("every", [EP, EP])
        cnt_i = sb("cnt_i", [EP, TILES], I32)
        grp_i = sb("grp_i", [EP, TILES], I32)
        grp = sb("grp", [EP, TILES])
        grp_end = sb("grp_end", [EP, TILES])
        grp_start = sb("grp_start", [EP, TILES])
        last_group = sb("last_group", [EP, TILES], I32)
        offset = sb("offset", [EP, TILES])
        group_no = sb("group_no", [EP, GROUPS])
        group_tile = sb("group_tile", [EP, GROUPS])
        slot_f = sb("slot_f", [EP, EF])
        slot_i = sb("slot_i", [EP, EF], I32)
        blank = sb("blank", [P, SUB, REC])
        stage = [sb(f"stage{b}", [EP, CHUNK, REC]) for b in range(SLOTS)]
        index = [sb(f"index{b}", [EP, CHUNK], I32) for b in range(SLOTS)]
        parts = [sb(f"attr_parts{b}", [EP, 3, CHUNK, EA96], BF16) for b in range(2)]
        other_c = [sb(f"other_c{b}", [EP, CHUNK]) for b in range(2)]
        rest = sb("attr_rest", [EP, CHUNK, EA96])
        hot = [sb(f"other_hot{f}", [EP, COLS], BF16) for f in range(CHUNK)]

        ends_loaded = k.sem("ends_loaded")
        masks_ready = k.sem("masks_ready")
        sorting = k.sem("sorting")
        totals_ready = k.sem("totals_ready")
        offsets_summed = k.sem("offsets_summed")
        blank_ready = k.sem("blank_ready")
        blanked, last_known = k.sem("blanked"), k.sem("last_known")
        features_in = [k.sem(f"features_in{b}") for b in range(SLOTS)]
        staged = [k.sem(f"staged{b}") for b in range(SLOTS)]
        k.scattered = [k.sem(f"scattered{b}") for b in range(SLOTS)]
        picked = k.sem("picked")
        split_act, split_dve = k.sem("split_act"), k.sem("split_dve")
        hot_ready, hot_used, sums_out = k.sem("hot_ready"), k.sem("hot_used"), k.sem("sums_out")
        ps_before, ps_every = k.psum[0:EP, 0, 0:TILES], k.psum[0:EP, 1, 0:TILES]
        ps_sums = k.psum[0:EA96, 2:5].rearrange("p c n -> p (c n)")
        chunks = EF // CHUNK

        def over_chunks(engine, step, between=None):
            def one(near):
                n = near(0)
                step(n)
                if between and n.fixed and n.g == 0:
                    between()

            in_turn(engine, one, 0, 0, SLOTS, chunks, 1)

        with nc.Block() as block:
            @block.sync
            def _(sp):
                sp.dma_start(key_i[:], a["src"].rearrange("(p f) -> p f", p=EP)).then_inc(ends_loaded, 16)
                sp.dma_start(other_i[:], a["dst"].rearrange("(p f) -> p f", p=EP)).then_inc(ends_loaded, 16)
                ea96 = a["edge_attr_96"].rearrange("(p f) d -> p f d", p=EP)
                ea32 = a["edge_attr_32"].rearrange("(p f) d -> p f d", p=EP)
                ea4 = a["edge_attr_4"].rearrange("(p f) d -> p f d", p=EP)

                def fetch(n):
                    b, at = n.slot, bass.ds(n.g * CHUNK, CHUNK)
                    if n.reaches(SLOTS):
                        sp.wait_ge(split_dve, 2 * (n.g - SLOTS + 1))
                        sp.wait_ge(k.scattered[b], n.round * 16 * CHUNK)
                    sp.dma_start(stage[b][:, :, 0:EA96], ea96[:, at]).then_inc(features_in[b], 16)
                    sp.dma_start(stage[b][:, :, EA96:EA96 + EA32], ea32[:, at]).then_inc(features_in[b], 16)
                    sp.dma_start(stage[b][:, :, EA96 + EA32:C_OTHER], ea4[:, at]).then_inc(features_in[b], 16)

                def write_blanks():
                    empty = blank[:].rearrange("p t c -> p (t c)")
                    sp.wait_ge(blank_ready, 1)
                    sp.dma_start(k.records[FULL * GROUP:, :].rearrange("(g p t) c -> p g (t c)", p=P, t=SUB),
                                 empty[:, None, :].broadcast_to([P, GROUPS - FULL, SUB * REC])).then_inc(blanked, 16)
                    sp.wait_ge(last_known, 1)
                    for b in range(TILES):
                        group = sp.value_load(last_group[0:1, b:b + 1], min_val=0, max_val=GROUPS - 1)
                        sp.wait_ge(blanked, 16 * (b + 1))
                        sp.dma_start(k.records[bass.ds(group * GROUP, GROUP), :].rearrange("(p t) c -> p (t c)", p=P),
                                     empty).then_inc(blanked, 16)

                def fetch_and_blank(n):
                    fetch(n)
                    if n.fixed and n.g == SLOTS - 1:
                        write_blanks()

                over_chunks(sp, fetch_and_blank)

            @block.gpsimd
            def _(pool):
                st = Steps(pool, masks_ready)
                st.done(nc.gpsimd.iota(group_no[:], pattern=[[1, GROUPS]], base=0, channel_multiplier=0,
                                       allow_small_or_imprecise_dtypes=True))
                st.done(nc.gpsimd.iota(k.lane[:], pattern=[[1, P]], base=0, channel_multiplier=0,
                                       allow_small_or_imprecise_dtypes=True))
                st.done(nc.gpsimd.iota(k.node[:], pattern=[[1, COLS]], base=0, channel_multiplier=0,
                                       allow_small_or_imprecise_dtypes=True))
                st.done(nc.gpsimd.memset(every[:], 1.0))
                st.done(nc.gpsimd.memset(before[:], 1.0))
                st.done(nc.gpsimd.memset(k.ident[:], 0.0))
                st.settle()
                st.done(nc.gpsimd.affine_select(out=before[:], in_=before[:], compare_op=ALU.is_gt, fill=0.0,
                                                base=0, pattern=[[1, EP]], channel_multiplier=-1))
                st.done(nc.gpsimd.affine_select(out=k.ident[:], in_=k.ident[:], compare_op=ALU.not_equal, fill=1.0,
                                                base=0, pattern=[[-1, P]], channel_multiplier=1))
                st.settle()

                def scatter(n):
                    b = n.slot
                    pool.wait_ge(staged[b], 2 * n.round + 2)
                    pool.wait_ge(blanked, 16 * (TILES + 1))
                    pool.sem_inc(k.pool_ready, 1)
                    for f in range(CHUNK):
                        nc.gpsimd.indirect_dma_start(
                            k.records[:, :], bass.IndirectOffsetOnAxis(ap=index[b][:, f:f + 1], axis=0),
                            stage[b][:, f, :], None).then_inc(k.scattered[b], 16)

                over_chunks(pool, scatter)

            @block.tensor
            def _(pe):
                def sum_totals():
                    pe.wait_ge(masks_ready, 8)
                    pe.wait_ge(totals_ready, 1)
                    nc.tensor.matmul(ps_before, before[:], total[:], start=True, stop=True)
                    nc.tensor.matmul(ps_every, every[:], total[:], start=True, stop=True).then_inc(offsets_summed, 1)

                def add_up(n):
                    pe.wait_ge(split_dve, 2 * n.g + 2)
                    for f in range(CHUNK):
                        pe.wait_ge(hot_ready, n.g * CHUNK + f + 1)
                        for j in range(3):
                            for c0, cw in CHUNKS:
                                mm = nc.tensor.matmul(ps_sums[:, c0:c0 + cw], parts[n.two][:, j, f], hot[f][:, c0:c0 + cw],
                                                      start=n.fixed and n.g == 0 and f == 0 and j == 0,
                                                      stop=n.fixed and n.g == chunks - 1 and f == CHUNK - 1 and j == 2)
                        mm.then_inc(hot_used, 1)

                over_chunks(pe, add_up, sum_totals)

            @block.scalar
            def _(act):
                def split(n):
                    act.wait_ge(features_in[n.slot], 48 * n.round + 48)
                    if n.reaches(2):
                        act.wait_ge(hot_used, (n.g - 1) * CHUNK)
                    nc.scalar.activation(parts[n.two][:, 0], stage[n.slot][:, :, 0:EA96], ACT.Copy).then_inc(split_act, 1)
                    act.wait_ge(split_dve, 2 * n.g + 1)
                    nc.scalar.activation(parts[n.two][:, 1], rest[:], ACT.Copy).then_inc(split_act, 1)

                over_chunks(act, split)
                act.wait_ge(hot_used, EF)
                nc.scalar.activation(k.sums_t[:], ps_sums[:, 0:COLS], ACT.Copy).then_inc(sums_out, 1)

            @block.vector
            def _(dve):
                v = nc.vector
                st = Steps(dve, sorting)
                st.done(v.memset(blank[:], 0.0))
                st.done(v.memset(ones[:], 1.0))
                st.settle()
                v.memset(blank[:, :, C_KEY:C_KEY + 1], -1.0).then_inc(blank_ready, 1)
                dve.wait_ge(masks_ready, 8)
                st.done(v.tensor_copy(k.ident_b[:], k.ident[:]))
                dve.wait_ge(ends_loaded, 32)

                def add_keys(n):
                    b, at = n.slot, bass.ds(n.g * CHUNK, CHUNK)
                    dve.wait_ge(features_in[b], 48 * n.round + 48)
                    if not n.reaches(SLOTS):
                        st.done(v.memset(stage[b][:, :, C_KEY + 1:REC], 0.0))
                    v.tensor_copy(index[b][:], slot_i[:, at])
                    v.tensor_copy(stage[b][:, :, C_OTHER:C_OTHER + 1].bitcast(I32),
                                  other_i[:, at].unsqueeze(2)).then_inc(staged[b], 1)
                    v.tensor_copy(stage[b][:, :, C_KEY:C_KEY + 1], local[:, at].unsqueeze(2)).then_inc(staged[b], 1)

                def use_features(n):
                    part, other = parts[n.two], other_c[n.two]
                    v.tensor_copy(other[:], other_f[:, bass.ds(n.g * CHUNK, CHUNK)]).then_inc(picked, 1)
                    dve.wait_ge(features_in[n.slot], 48 * n.round + 48)
                    dve.wait_ge(split_act, 2 * n.g + 1)
                    if n.reaches(1):
                        dve.wait_ge(split_dve, 2 * n.g)
                    v.tensor_tensor(rest[:], stage[n.slot][:, :, 0:EA96], part[:, 0], ALU.subtract).then_inc(split_dve, 1)
                    dve.wait_ge(split_act, 2 * n.g + 2)
                    v.tensor_tensor(part[:, 2], rest[:], part[:, 1], ALU.subtract).then_inc(split_dve, 1)
                    dve.wait_ge(picked, n.g + 1)
                    for f in range(CHUNK):
                        if n.reaches(1):
                            dve.wait_ge(hot_used, (n.g - 1) * CHUNK + f + 1)
                        v.tensor_scalar(hot[f][:], k.node[0:EP, :], other[:, f:f + 1], None,
                                        ALU.is_equal).then_inc(hot_ready, 1)

                st.done(v.tensor_scalar(tile_i[:], key_i[:], 7, None, ALU.arith_shift_right))
                st.done(v.tensor_copy(key_f[:], key_i[:]))
                st.done(v.tensor_copy(other_f[:], other_i[:]))
                st.settle()
                use_features(Turn(0, 0, SLOTS, chunks))
                st.done(v.tensor_copy(tile_f[:], tile_i[:]))
                st.settle()
                st.done(v.scalar_tensor_tensor(local[:], tile_f[:], -float(P), key_f[:], ALU.mult, ALU.add))
                for b in range(TILES):
                    st.done(v.tensor_scalar(member[:, b], tile_f[:], float(b), None, ALU.is_equal))
                st.settle()
                for b in range(TILES):
                    st.done(v.tensor_tensor_scan(rank[:, b], ones[:], member[:, b], 0.0, ALU.mult, ALU.add))
                st.settle()
                v.tensor_copy(total[:], rank[:, :, EF - 1]).then_inc(totals_ready, 1)
                use_features(Turn(0, 1, SLOTS, chunks))
                dve.wait_ge(offsets_summed, 1)
                st.done(v.tensor_scalar(cnt_i[:], ps_every, float(GROUP - 1), None, ALU.add))
                st.settle()
                st.done(v.tensor_scalar(grp_i[:], cnt_i[:], GROUP.bit_length() - 1, None, ALU.arith_shift_right))
                st.settle()
                st.done(v.tensor_copy(grp[:], grp_i[:]))
                st.settle()
                st.done(v.tensor_tensor_scan(grp_end[:], ones[:, 0:TILES], grp[:], 0.0, ALU.mult, ALU.add))
                st.settle()
                v.tensor_scalar(last_group[:], grp_end[:], -1.0, 0.0, ALU.add, ALU.max).then_inc(last_known, 1)
                st.done(v.tensor_tensor(grp_start[:], grp_end[:], grp[:], ALU.subtract))
                st.settle()
                st.done(v.scalar_tensor_tensor(offset[:], grp_start[:], float(GROUP), ps_before, ALU.mult, ALU.add))
                st.settle()
                for b in range(TILES):
                    st.done(v.scalar_tensor_tensor(rank[:, b], rank[:, b], offset[:, b:b + 1], member[:, b],
                                                   ALU.add, ALU.mult))
                st.settle()
                st.done(v.tensor_reduce(slot_f[:], rank[:].rearrange("p b f -> p f b"), AX.X, ALU.add))
                st.settle()
                st.done(v.tensor_scalar(slot_i[:], slot_f[:], -1.0, None, ALU.add))
                st.done(v.tensor_scalar(group_tile[:], group_no[:], grp_start[:, 1:2], None, ALU.is_ge))
                st.settle()
                for b in range(2, TILES):
                    st.done(v.scalar_tensor_tensor(group_tile[:], group_no[:], grp_start[:, b:b + 1], group_tile[:],
                                                   ALU.is_ge, ALU.add))
                    st.settle()
                st.done(v.tensor_copy(k.group_tile[0:EP, :], group_tile[:]))
                st.settle()

                def fill(n):
                    add_keys(n)
                    if n.reaches(2):
                        use_features(n)

                over_chunks(dve, fill)


def count_edges(k, loaded, loads):
    nc = k.nc
    with ExitStack() as ctx:
        def sb(name, shape, dt=F32):
            return ctx.enter_context(nc.sbuf_tensor(name, shape, dt))

        counts = sb("counts", [P, TILES * COLS])
        record = [sb(f"record{b}", [P, SUB, REC]) for b in range(SLOTS)]
        other_f = [sb(f"other_col{b}", [P, SUB]) for b in range(2)]
        key_hot = [sb(f"key_hot{b}", [P, SUB, P], BF16) for b in range(2)]
        other_hot = [sb(f"other_wide{t}", [P, COLS], BF16) for t in range(SUB)]
        minus_other = [sb(f"minus_other{b}", [P, 1]) for b in range(2)]
        distance = sb("distance", [P, COLS], F16)

        cleared = k.sem("cleared")
        rec_in = [k.sem(f"rec_in{b}") for b in range(SLOTS)]
        key_ready, other_float, other_ready = k.sem("key_ready"), k.sem("other_float"), k.sem("other_ready")
        negated, distanced, act_ready = k.sem("other_negated"), k.sem("other_distance"), k.sem("act_other_ready")
        tile_counted, group_added, counts_out = k.sem("tile_counted"), k.sem("group_added"), k.sem("counts_out")

        ps = [k.psum[:, 4 * b:4 * b + 4, :] for b in range(2)]
        with nc.Block() as block:
            @block.sync
            def _(sp):
                for b in range(SLOTS):
                    sp.wait_ge(k.scattered[b], EF // CHUNK // SLOTS * 16 * CHUNK)

                def fetch(near):
                    n = near(2)
                    if not n.exists():
                        return
                    if n.reaches(SLOTS):
                        sp.wait_ge(key_ready, n.g - SLOTS + 1)
                        sp.sem_inc(k.sp_ready, 1)
                    sp.dma_start(record[n.slot][:], k.records[bass.ds(n.g * GROUP, GROUP), :]
                                 .rearrange("(p t) c -> p t c", p=P)).then_inc(rec_in[n.slot], 16)
                    if n.fixed and SLOTS <= n.g < 2 * SLOTS + 2:
                        for out, in_ in loads[(n.g - SLOTS) * 2:(n.g - SLOTS) * 2 + 2]:
                            sp.dma_start(out, in_).then_inc(loaded, 16)

                over_groups(sp, fetch, 2, 0)
                sp.wait_ge(group_added, GROUPS)
                sp.dma_start(k.counts_d[:, :], counts[:]).then_inc(counts_out, 16)
                sp.wait_ge(counts_out, 16)

            @block.gpsimd
            def _(pool):
                nc.gpsimd.memset(counts[:], 0.0).then_inc(cleared, 1)

                def key_hots(near):
                    n = near(1)
                    if not n.exists():
                        return
                    pool.wait_ge(rec_in[n.slot], 16 * n.round + 16)
                    if n.reaches(2):
                        pool.wait_ge(tile_counted, (n.g - 1) * SUB)
                        pool.wait_ge(other_ready, (n.g - 1) * (SUB - 1))
                        pool.wait_ge(distanced, n.g - 1)
                    pool.sem_inc(k.pool_ready, 1)
                    nc.gpsimd.tensor_copy(other_f[n.two][:], record[n.slot][:, :, C_OTHER].bitcast(I32)
                                          ).then_inc(other_float, 1)
                    pool.wait_ge(other_float, n.g + 1)
                    pool.sem_inc(k.pool_ready, 1)
                    nc.gpsimd.tensor_scalar(minus_other[n.two][:], other_f[n.two][:, SUB - 1:SUB], -1.0, None, ALU.mult
                                            ).then_inc(negated, 1)
                    for t in range(SUB):
                        last = nc.gpsimd.tensor_scalar(key_hot[n.two][:, t], k.lane[:], record[n.slot][:, t, C_KEY:C_KEY + 1],
                                                       None, ALU.is_equal)
                    last.then_inc(key_ready, 1)

                over_groups(pool, key_hots, 1, 0)

            @block.scalar
            def _(act):
                def other(near):
                    n = near(0)
                    act.wait_ge(negated, n.g + 1)
                    if n.reaches(1):
                        act.wait_ge(act_ready, n.g)
                    nc.scalar.activation(distance[:], k.node[:], ACT.Abs, bias=minus_other[n.two][:, 0:1]
                                         ).then_inc(distanced, 1)
                    act.wait_ge(distanced, n.g + 1)
                    if n.reaches(1):
                        act.wait_ge(tile_counted, n.g * SUB)
                    nc.scalar.activation(other_hot[SUB - 1][:], distance[:], ACT.Relu, bias=k.ones[:, 0:1], scale=-1.0
                                         ).then_inc(act_ready, 1)

                over_groups(act, other, 0, 0)

            @block.tensor
            def _(pe):
                def count(near):
                    n = near(0)
                    pe.wait_ge(key_ready, n.g + 1)
                    if n.reaches(2):
                        pe.wait_ge(group_added, n.g - 1)
                    for t in range(SUB):
                        if t < SUB - 1:
                            pe.wait_ge(other_ready, n.g * (SUB - 1) + t + 1)
                        else:
                            pe.wait_ge(act_ready, n.g + 1)
                        for c, (c0, cw) in enumerate(CHUNKS):
                            last = nc.tensor.matmul(ps[n.two][:, c, 0:cw], key_hot[n.two][:, t], other_hot[t][:, c0:c0 + cw],
                                                    start=t == 0, stop=t == SUB - 1)
                        last.then_inc(tile_counted, 1)

                over_groups(pe, count, 0, 0)

            @block.vector
            def _(dve):
                v = nc.vector
                dve.wait_ge(cleared, 1)

                def other(n, t):
                    if t == 0:
                        dve.wait_ge(other_float, n.g + 1)
                    if n.reaches(1):
                        dve.wait_ge(tile_counted, (n.g - 1) * SUB + t + 1)
                    v.tensor_scalar(other_hot[t][:], k.node[:], other_f[n.two][:, t:t + 1], None,
                                    ALU.is_equal).then_inc(other_ready, 1)

                def add(n):
                    dve.wait_ge(tile_counted, n.g * SUB + SUB)
                    if n.reaches(1):
                        dve.wait_ge(group_added, n.g)
                    row_tile = dve.value_load(k.group_tile[0:1, bass.ds(n.g, 1)], min_val=0, max_val=TILES - 1)
                    here = counts[:, bass.ds(row_tile * COLS, COLS)]
                    v.tensor_tensor(here, here, ps[n.two].rearrange("p c n -> p (c n)")[:, 0:COLS],
                                    ALU.add).then_inc(group_added, 1)

                def step(near):
                    for t in range(SUB - 1):
                        if near(0).exists():
                            other(near(0), t)
                        if t == SUB - 2 and near(-1).exists():
                            add(near(-1))

                over_groups(dve, step, 0, 1)


def copy_to(k, act, out, in_):
    if act:
        return k.nc.scalar.activation(out, in_, ACT.Copy)
    return k.nc.vector.tensor_copy(out, in_)


def add_bias(k, act, out, in_, bias, relu=False):
    if act:
        return k.nc.scalar.activation(out, in_, ACT.Relu if relu else ACT.Identity, bias=bias)
    if relu:
        return k.nc.vector.tensor_scalar(out, in_, bias, 0.0, ALU.add, ALU.max)
    return k.nc.vector.tensor_scalar(out, in_, bias, None, ALU.add)


def load(k, sem, pairs):
    with k.nc.Block() as block:
        @block.scalar
        def _(act):
            for out, in_ in pairs:
                act.dma_start(out, in_).then_inc(sem, 16)
    return 16 * len(pairs)


def through_banks(k, count, fill, drain, needs=()):
    filled, by_act, by_dve = k.filled, k.by_act, k.by_dve
    f0, a0, d0 = k.filled_n, k.by_act_n, k.by_dve_n
    acts, dves = (count + 1) // 2, count // 2
    with k.nc.Block() as block:
        @block.tensor
        def _(pe):
            for sem, value in needs:
                pe.wait_ge(sem, value)
            for n in range(count):
                if n >= 8:
                    pe.wait_ge(*((by_dve, d0 + n // 2 - 3) if n % 2 else (by_act, a0 + n // 2 - 3)))
                fill(n, k.psum[:, n % 8]).then_inc(filled, 1)

        @block.scalar
        def _(act):
            for sem, value in needs:
                act.wait_ge(sem, value)
            for n in range(0, count, 2):
                act.wait_ge(filled, f0 + n + 1)
                drain(True, n, k.psum[:, n % 8]).then_inc(by_act, 1)

        @block.vector
        def _(dve):
            for sem, value in needs:
                dve.wait_ge(sem, value)
            for n in range(1, count, 2):
                dve.wait_ge(filled, f0 + n + 1)
                drain(False, n, k.psum[:, n % 8]).then_inc(by_dve, 1)

    k.filled_n, k.by_act_n, k.by_dve_n = f0 + count, a0 + acts, d0 + dves


def flip(k, tiles, pieces, out, needs=()):
    piece, wide = pieces
    batches = [(t, j, min(4, wide - j)) for t in range(tiles) for j in range(0, wide, 4)]

    def fill(n, bank):
        t, j, w = batches[n]
        for i in range(w):
            x = piece(t, j + i)
            last = k.nc.tensor.transpose(bank[0:x.shape[1], i * P:(i + 1) * P], x, k.ident[:])
        return last

    def drain(act, n, bank):
        t, j, w = batches[n]
        o = out(j, w, t)
        return copy_to(k, act, o, bank[0:o.shape[0], 0:w * P].rearrange("p (j c) -> p j c", j=w))

    through_banks(k, len(batches), fill, drain, needs)


def features_out(k, outs, terms, finish, needs=()):
    def fill(n, bank):
        j, (c0, cw) = n // len(CHUNKS), CHUNKS[n % len(CHUNKS)]
        ts = terms(j)
        for i, (w, x) in enumerate(ts):
            last = k.nc.tensor.matmul(bank[:, 0:cw], w, x[:, c0:c0 + cw], start=i == 0, stop=i == len(ts) - 1)
        return last

    def drain(act, n, bank):
        j, (c0, cw) = n // len(CHUNKS), CHUNKS[n % len(CHUNKS)]
        return finish(act, j, slice(c0, c0 + cw), bank[:, 0:cw])

    through_banks(k, outs * len(CHUNKS), fill, drain, needs)


def rows_out(k, terms, finish, needs=()):
    through_banks(k, TILES, row_products(k, terms), lambda act, n, bank: finish(act, n, bank), needs)


def measured(k, count, fill, drain, piece, stats, needs=(), meanwhile=None):
    filled, by_dve = k.filled, k.by_dve
    f0, d0 = k.filled_n, k.by_dve_n
    with k.nc.Block() as block:
        @block.tensor
        def _(pe):
            for sem, value in needs:
                pe.wait_ge(sem, value)
            for n in range(count):
                if n >= 8:
                    pe.wait_ge(by_dve, d0 + n - 7)
                fill(n, k.psum[:, n % 8]).then_inc(filled, 1)

        @block.vector
        def _(dve):
            for sem, value in needs:
                dve.wait_ge(sem, value)
            for n in range(count + 1):
                if n < count:
                    dve.wait_ge(filled, f0 + n + 1)
                    drain(n, k.psum[:, n % 8]).then_inc(by_dve, 1)
                if n > 0:
                    dve.wait_ge(by_dve, d0 + n)
                    k.nc.vector.bn_stats(stats(n - 1), piece(n - 1)).then_inc(k.norm, 1)

        if meanwhile:
            @block.gpsimd
            def _(pool):
                meanwhile(pool)
    k.filled_n, k.by_dve_n, k.norm_n = f0 + count, d0 + count, k.norm_n + count


def apply_norm(k, x, stats, width, scale=None, shift=None):
    nc = k.nc
    pieces = x.shape[1]
    with ExitStack() as ctx:
        k.names += 1
        mv = ctx.enter_context(nc.sbuf_tensor(f"mv{k.names}", [P, pieces, 2], F32))
        root = ctx.enter_context(nc.sbuf_tensor(f"root{k.names}", [P, pieces], F32))
        bias = ctx.enter_context(nc.sbuf_tensor(f"bias{k.names}", [P, pieces], F32))
        base, r0 = k.norm_n, k.root_n

        with nc.Block() as block:
            @block.scalar
            def _(act):
                act.wait_ge(k.variances, r0 + 1)
                nc.scalar.activation(root[:], mv[:, :, 1], ACT.Sqrt).then_inc(k.roots, 1)
                act.wait_ge(k.biased, r0 + 1)
                for t in range(0, pieces, 2):
                    nc.scalar.activation(x[:, t, 0:width], x[:, t, 0:width], ACT.Identity, bias=bias[:, t:t + 1],
                                         scale=root[:, t:t + 1]).then_inc(k.applied, 1)

            @block.vector
            def _(dve):
                v = nc.vector
                st = Steps(dve, k.norm, base)
                dve.wait_ge(k.norm, base)
                for t in range(pieces):
                    st.done(v.bn_aggr(mv[:, t], stats[:, t]))
                st.settle()
                v.tensor_scalar(mv[:, :, 1], mv[:, :, 1], EPS, None, ALU.add).then_inc(k.variances, 1)
                dve.wait_ge(k.roots, r0 + 1)
                st.done(v.reciprocal(root[:], root[:]))
                st.settle()
                if scale is not None:
                    st.done(v.tensor_tensor(root[:], root[:], scale[:], ALU.mult))
                    st.settle()
                st.done(v.scalar_tensor_tensor(bias[:], mv[:, :, 0], -1.0, root[:], ALU.mult, ALU.mult))
                st.settle()
                if shift is not None:
                    st.done(v.tensor_tensor(bias[:], bias[:], shift[:], ALU.add))
                    st.settle()
                dve.sem_inc(k.biased, 1)
                for t in range(1, pieces, 2):
                    st.done(v.tensor_scalar(x[:, t, 0:width], x[:, t, 0:width], root[:, t:t + 1], bias[:, t:t + 1],
                                            ALU.mult, ALU.add))
                st.settle()
                k.norm_n += st.n
        k.root_n += 1


def batch_normed(k, outs, terms, combine, x, scale, shift, needs=()):
    k.names += 1
    with k.nc.sbuf_tensor(f"stats{k.names}", [P, outs, len(CHUNKS), 6], F32) as stats:
        def where(n):
            return n // len(CHUNKS), CHUNKS[n % len(CHUNKS)]

        def fill(n, bank):
            j, (c0, cw) = where(n)
            ts = terms(j)
            for i, (w, act) in enumerate(ts):
                last = k.nc.tensor.matmul(bank[:, 0:cw], w, act[:, c0:c0 + cw], start=i == 0, stop=i == len(ts) - 1)
            return last

        def drain(n, bank):
            j, (c0, cw) = where(n)
            return combine(j, slice(c0, c0 + cw), bank[:, 0:cw])

        def piece(n):
            j, (c0, cw) = where(n)
            return x[:, j, c0:min(c0 + cw, NODES)]

        measured(k, outs * len(CHUNKS), fill, drain, piece, lambda n: stats[:, n // len(CHUNKS), n % len(CHUNKS)], needs)
        apply_norm(k, x, stats, NODES, scale, shift)


def rows_normed(k, fill, drain, x, needs=(), meanwhile=None):
    k.names += 1
    with k.nc.sbuf_tensor(f"stats{k.names}", [P, TILES, 1, 6], F32) as stats:
        measured(k, TILES, fill, drain, lambda t: x[:, t], lambda t: stats[:, t, 0], needs, meanwhile)
        apply_norm(k, x, stats, D)


def row_products(k, terms):
    def fill(n, bank):
        ts = terms(n)
        for i, (x, w, at) in enumerate(ts):
            last = k.nc.tensor.matmul(bank[:, at], x, w, start=i == 0 or ts[i - 1][2] != at,
                                      stop=i == len(ts) - 1 or ts[i + 1][2] != at)
        return last
    return fill


def add_scaled(k, y, g):
    nc = k.nc
    k.names += 1
    with nc.sbuf_tensor(f"stats{k.names}", [P, TILES, 1, 6], F32) as stats:
        base = k.norm_n
        with nc.Block() as block:
            @block.vector
            def _(dve):
                v = nc.vector
                st = Steps(dve, k.norm, base)
                for n in range(TILES + 2):
                    st.settle()
                    if n < TILES:
                        st.done(v.tensor_tensor(y[:, n], y[:, n], g[:], ALU.mult))
                    if 1 <= n <= TILES:
                        st.done(v.tensor_tensor(k.x[:, n - 1], k.x[:, n - 1], y[:, n - 1], ALU.add))
                    if n >= 2:
                        st.done(v.bn_stats(stats[:, n - 2, 0], k.x[:, n - 2]))
                k.norm_n += st.n
        apply_norm(k, k.x, stats, D)


def row_of(ap, n=D):
    return ap.rearrange("(o d) -> o d", o=1)


def spread(ap, n=D):
    return row_of(ap).broadcast_to([P, n])


def columns(ap):
    return ap.rearrange("(t p) -> p t", p=P)


def weight(ap):
    return ap.rearrange("(t p) j -> p t j", p=P)


def mlp_weights(k, scope):
    a = k.a

    def sb(name, shape):
        return scope.enter_context(k.nc.sbuf_tensor(name, shape, F32))

    w1, w1e, w2, w3 = sb("w1", [P, 4, 1024]), sb("w1e", [EA96, 1024]), sb("w2", [P, 8, 1024]), sb("w3", [P, 8, D])
    b1, b2, b3 = sb("b1", [P, 8]), sb("b2", [P, 8]), sb("b3", [1, D])
    g, be = sb("g0", [P, D]), sb("be0", [P, D])
    w2_rows = weight(a["L0_gnn_W2"])
    loads = [(w1[:], weight(a["L0_gnn_W1"][0:D, :])), (w1e[:], a["L0_gnn_W1"][D:D + EA96, :]),
             (b1[:], columns(a["L0_gnn_b1"])), (w2[:, 0:4], w2_rows[:, 0:4]), (w2[:, 4:8], w2_rows[:, 4:8]),
             (b2[:], columns(a["L0_gnn_b2"])), (w3[:], weight(a["L0_gnn_W3"])), (b3[:], row_of(a["L0_gnn_b3"])),
             (g[:], spread(a["L0_gnn_gamma"])), (be[:], spread(a["L0_gnn_beta"]))]
    return (w1, w1e, w2, w3, b1, b2, b3, g, be), k.sem("mlp_loaded"), loads


def mlp_layer(k, weights):
    nc = k.nc
    with ExitStack() as ctx:
        def sb(name, shape, dt=F32):
            return ctx.enter_context(nc.sbuf_tensor(name, shape, dt))

        (w1, w1e, w2, w3, b1, b2, b3, g, be), loaded, loads = weights
        needs = [(loaded, 16 * len(loads))]
        h1 = sb("h1", [P, 8, COLS])
        with ExitStack() as inner:
            xt = inner.enter_context(nc.sbuf_tensor("xt0", [P, 4, COLS], F32))
            flip(k, TILES, (lambda t, j: k.x[:, t, j * P:(j + 1) * P], 4),
                 lambda j, w, t: xt[:, j:j + w, t * P:(t + 1) * P], [(k.x_loaded, 32)])
            features_out(k, 8, lambda j: [(w1[:, i, j * P:(j + 1) * P], xt[:, i]) for i in range(4)]
                         + [(w1e[:, j * P:(j + 1) * P], k.sums_t)],
                         lambda act, j, at, ps: add_bias(k, act, h1[:, j, at], ps, b1[:, j:j + 1], relu=True), needs)
        h2 = sb("h2", [P, 8, COLS])
        features_out(k, 8, lambda j: [(w2[:, i, j * P:(j + 1) * P], h1[:, i]) for i in range(8)],
                     lambda act, j, at, ps: add_bias(k, act, h2[:, j, at], ps, b2[:, j:j + 1], relu=True))
        y = h1[:, 0:4].rearrange("p a b -> p (a b)").rearrange("p (t d) -> p t d", d=D)
        shifted = k.sem("x_shifted0")

        def shift_x(pool):
            nc.gpsimd.tensor_tensor(k.x[:], k.x[:], be[:][:, None, :].broadcast_to([P, TILES, D]), ALU.add).then_inc(shifted, 1)
            pool.wait_ge(shifted, 1)

        rows_normed(k, row_products(k, lambda t: [(h2[:, i, t * P:(t + 1) * P], w3[:, i], slice(0, D)) for i in range(8)]
                                    + [(k.ones[0:1, :], b3[:], slice(0, D))]),
                    lambda t, ps: nc.vector.tensor_copy(y[:, t], ps), y, meanwhile=shift_x)
        add_scaled(k, y, g)


def split3(k, v, st, src, parts, rest):
    st.done(v.tensor_copy(parts[0], src))
    st.settle()
    st.done(v.tensor_tensor(rest, src, parts[0], ALU.subtract))
    st.settle()
    st.done(v.tensor_copy(parts[1], rest))
    st.settle()
    st.done(v.tensor_tensor(parts[2], rest, parts[1], ALU.subtract))
    st.settle()


def tensor_nodes(k, outer):
    nc, a = k.nc, k.a

    def keep(name, shape, dt=F32):
        return outer.enter_context(nc.sbuf_tensor(name, shape, dt))

    k.p1_parts = keep("p1_parts", [P, TILES * 3 * 384], BF16)
    k.ph_parts = keep("ph_parts", [P, TILES * 3 * PAD], BF16)
    k.hid_f = keep("hid_f", [EA32, PAD])
    k.hid_s = keep("hid_s", [P, PAD])
    k.mix = keep("mix", [P, 2, 2, D], BF16)
    with ExitStack() as ctx:
        def sb(name, shape, dt=F32):
            return ctx.enter_context(nc.sbuf_tensor(name, shape, dt))

        wp0, wp1, wn0, wn1 = (sb(n, [P, P]) for n in ("wp0", "wp1", "wn0", "wn1"))
        bp0, bn0 = sb("bp0", [P, 1]), sb("bn0", [1, P])
        wg1, wg2, bg1, bg2 = sb("wg1", [P, 2, 256]), sb("wg2", [P, 2, 256]), sb("bg1", [P, 2]), sb("bg2", [P, 2])
        ws1 = sb("ws1", [P, 3, 32])
        wsum = sb("wsum", [P, HID])
        mixf = sb("mixf", [P, 2, D])
        part = sb("part", [P, 3, 2, D], BF16)
        rest = sb("rest", [P, 2, D])
        xp = sb("xp", [P, 4, COLS])
        p0 = sb("p0", [P, COLS])
        p1 = sb("p1", [P, TILES, 384 + HID])
        loaded = k.sem("node_loaded")
        pairs = [(wp0[:], a["L1_gnn_W_pre0"]), (wp1[:], a["L1_gnn_W_pre1"]), (wn0[:], a["L1_gnn_W_nd0"]),
                 (wn1[:], a["L1_gnn_W_nd1"]), (bp0[:], columns(a["L1_gnn_b_pre0"])), (bn0[:], row_of(a["L1_gnn_b_nd0"])),
                 (wg1[:], weight(a["L1_gnn_W_g1"])), (wg2[:], weight(a["L1_gnn_W_g2"])),
                 (bg1[:], columns(a["L1_gnn_b_g1"])), (bg2[:], columns(a["L1_gnn_b_g2"])),
                 (ws1[:], weight(a["L1_gnn_W_s1"]))]
        for r in range(4):
            pairs.append((mixf[32 * r:32 * r + 32, 0], a["L1_gnn_W_f2"]))
            pairs.append((mixf[32 * r:32 * r + 32, 1], a["L1_gnn_W_s2"]))
        pairs.append((k.hid_f[:, HID:HID + 32], a["L1_gnn_W_f1"]))
        n = load(k, loaded, pairs)
        steps, masked = k.sem("node_steps"), k.sem("node_masked")

        with nc.Block() as block:
            @block.gpsimd
            def _(pool):
                st = Steps(pool, masked)
                st.done(nc.gpsimd.memset(k.hid_f[:, 0:HID], 0.0))
                st.done(nc.gpsimd.memset(k.hid_f[:, HID + 32:PAD], 0.0))
                st.done(nc.gpsimd.memset(k.ph_parts[:], 0.0))
                st.done(nc.gpsimd.memset(k.hid_s[:], 0.0))
                st.done(nc.gpsimd.memset(wsum[:], 0.0))
                st.done(nc.gpsimd.memset(k.mix[:], 0.0))

            @block.vector
            def _(dve):
                v = nc.vector
                dve.wait_ge(loaded, n)
                dve.wait_ge(masked, 6)
                st = Steps(dve, steps)
                st.done(v.tensor_tensor(wsum[:, 32:HID], ws1[:, 0], ws1[:, 1], ALU.add))
                st.done(v.tensor_scalar(k.hid_s[:, HID + 32:2 * HID], ws1[:, 2], 1.0 / 3.0, None, ALU.mult))
                st.done(v.tensor_scalar(mixf[:, 1, 384:512], mixf[:, 1, 384:512], 3.0 ** -0.5, None, ALU.mult))
                st.settle()
                split3(k, v, st, mixf[:], [part[:, i] for i in range(3)], rest[:])
                for r, first, second in ((0, 0, None), (1, 0, 1), (2, 0, 1), (3, 2, None)):
                    rows = slice(32 * r, 32 * r + 32)
                    st.done(v.tensor_copy(k.mix[rows, :, 0], part[rows, first]))
                    if second:
                        st.done(v.tensor_copy(k.mix[rows, :, 1], part[rows, second]))
                st.settle()

        def planar(t, j):
            return k.x[:, t, 0:P] if j == 0 else k.x[:, t, P + j - 1:D:3]

        flip(k, TILES, (planar, 4), lambda j, w, t: xp[:, j:j + w, t * P:(t + 1) * P])
        features_out(k, 1, lambda j: [(wp0[:], xp[:, 0])],
                     lambda act, j, at, ps: add_bias(k, act, p0[:, at], ps, bp0[:, 0:1]))
        rows_out(k, lambda t: [(xp[:, 1 + m, t * P:(t + 1) * P], wp1[:], slice(m * P, m * P + P)) for m in range(3)]
                 + [(p0[:, t * P:(t + 1) * P], wsum[:], slice(384, 384 + HID))],
                 lambda act, t, ps: copy_to(k, act, p1[:, t], ps[:, 0:384 + HID]))
        s2 = k.sem("node_split")
        k.tables = k.sem("tables")
        rest2 = sb("rest2", [P, TILES, 384])
        with nc.Block() as block:
            @block.sync
            def _(sp):
                sp.dma_start(k.p1_d.rearrange("(t p) c -> p t c", p=P), p1[:, :, 0:384]).then_inc(k.tables, 16)
                sp.wait_ge(k.tables, 16)

            @block.vector
            def _(dve):
                st = Steps(dve, s2)
                pv = k.p1_parts[:].rearrange("p (t i c) -> p t i c", t=TILES, i=3)
                split3(k, nc.vector, st, p1[:, :, 0:384], [pv[:, :, i] for i in range(3)], rest2[:])
                pv = k.ph_parts[:].rearrange("p (t i c) -> p t i c", t=TILES, i=3)
                split3(k, nc.vector, st, p1[:, :, 384:384 + HID], [pv[:, :, i, HID:2 * HID] for i in range(3)],
                       rest2[:, :, 0:HID])

        n1 = sb("n1", [P, COLS])
        hid = sb("hid", [P, 2, COLS])
        gate = sb("gate", [P, COLS])
        s3, s4 = k.sem("norms_summed"), k.sem("norms_rooted")
        with nc.Block() as block:
            @block.scalar
            def _(act):
                act.wait_ge(s3, 4)
                nc.scalar.activation(n1[:], n1[:], ACT.Sqrt, scale=1.0 / 3.0).then_inc(s4, 1)

            @block.vector
            def _(dve):
                v = nc.vector
                st = Steps(dve, s3)
                st.done(v.tensor_tensor(hid[:, 0], xp[:, 1], xp[:, 1], ALU.mult))
                st.done(v.tensor_tensor(hid[:, 1], xp[:, 2], xp[:, 2], ALU.mult))
                st.settle()
                v.tensor_tensor(n1[:], hid[:, 0], hid[:, 1], ALU.add)
                st.done(v.tensor_tensor(gate[:], xp[:, 3], xp[:, 3], ALU.mult))
                st.settle()
                st.done(v.tensor_tensor(n1[:], n1[:], gate[:], ALU.add))
        sig = sb("sig", [P, 2, COLS])
        features_out(k, 2, lambda j: [(wg1[:, 0, j * P:(j + 1) * P], xp[:, 0]), (wg1[:, 1, j * P:(j + 1) * P], n1[:])],
                     lambda act, j, at, ps: add_bias(k, act, hid[:, j, at], ps, bg1[:, j:j + 1]))
        s5, s6 = k.sem("sigmoid_done"), k.sem("silu_done")
        with nc.Block() as block:
            @block.scalar
            def _(act):
                nc.scalar.activation(sig[:], hid[:], ACT.Sigmoid).then_inc(s5, 1)

            @block.vector
            def _(dve):
                dve.wait_ge(s5, 1)
                nc.vector.tensor_tensor(hid[:], hid[:], sig[:], ALU.mult).then_inc(s6, 1)
        g0 = sig[:, 0]
        features_out(k, 2, lambda j: [(wg2[:, i, j * P:(j + 1) * P], hid[:, i]) for i in range(2)],
                     lambda act, j, at, ps: add_bias(k, act, (gate if j else g0)[:, at], ps, bg2[:, j:j + 1]))
        s7 = k.sem("gated")
        with nc.Block() as block:
            @block.vector
            def _(dve):
                nc.vector.tensor_tensor(xp[:, 1:4], xp[:, 1:4], gate[:][:, None, :].broadcast_to([P, 3, COLS]),
                                        ALU.mult).then_inc(s7, 1)
        xs = sb("xs", [P, TILES, D])
        rows_out(k, lambda t: [(g0[:, t * P:(t + 1) * P], wn0[:], slice(0, P)), (k.ones[0:1, :], bn0[:], slice(0, P))]
                 + [(xp[:, 1 + m, t * P:(t + 1) * P], wn1[:], slice((1 + m) * P, (2 + m) * P)) for m in range(3)],
                 lambda act, t, ps: copy_to(k, act, xs[:, t], ps))
        with nc.Block() as block:
            @block.sync
            def _(sp):
                sp.dma_start(k.xs_d.rearrange("(t p) c -> p t c", p=P), xs[:]).then_inc(k.tables, 16)
                sp.wait_ge(k.tables, 32)


def edge_hidden(k):
    nc = k.nc
    with ExitStack() as ctx:
        def sb(name, shape, dt=F32):
            return ctx.enter_context(nc.sbuf_tensor(name, shape, dt))

        record = [sb(f"rec_h{b}", [P, SUB, REC]) for b in range(SLOTS)]
        source = [sb(f"source{b}", [P, SUB, 384]) for b in range(SLOTS)]
        hot = [sb(f"hot{b}", [P, SUB, P], BF16) for b in range(2)]
        hot_t = [sb(f"hot_t{b}", [P, GROUP], BF16) for b in range(2)]
        attr_t = [sb(f"attr_t{b}", [EA32, GROUP]) for b in range(2)]
        prod = [sb(f"prod{b}", [P, 3, P]) for b in range(2)]
        ip = [sb(f"ip{b}", [P, SUB, P]) for b in range(2)]
        ip_t = sb("ip_t", [P, GROUP])
        size = sb("size", [P, GROUP // 2])
        hidden = sb("hidden", [P, GROUP // 2])
        parts = [sb(f"parts{b}", [P, 3, GROUP // 2], BF16) for b in range(SLOTS)]
        half = sb("half", [P, 1])

        rec_in = [k.sem(f"h_rec_in{b}") for b in range(SLOTS)]
        source_in = [k.sem(f"h_source_in{b}") for b in range(SLOTS)]
        stored = [k.sem(f"h_stored{b}") for b in range(SLOTS)]
        hot_ready, flipped, hot_copied = k.sem("h_hot"), k.sem("h_flipped"), k.sem("h_hot_copied")
        attr_copied = k.sem("h_attr_copied")
        target_out, multiplied, summed = k.sem("h_target"), k.sem("h_multiplied"), k.sem("h_summed")
        ip_flipped, ip_copied = k.sem("h_ip_flipped"), k.sem("h_ip_copied")
        begun, hidden_in, soft, hidden_out = k.sem("h_begun"), k.sem("h_in"), k.sem("h_soft"), k.sem("h_out")
        cast, rest_out = k.sem("h_cast"), k.sem("h_rest")
        halved = k.sem("h_halved")
        k.stored = stored

        ps_hot = k.psum[:, 0].bitcast(BF16)[:, 0:GROUP]
        ps_attr = k.psum[0:EA32, 1]
        ps_target = [k.psum[:, 2 + b, 0:384] for b in range(2)]
        ps_ip = k.psum[:, 4]
        ps_hid = [k.psum[:, 5 + b, 0:GROUP // 2] for b in range(2)]
        halves = [(slice(0, GROUP // 2), HID), (slice(GROUP // 2, GROUP), 0)]

        with nc.Block() as block:
            @block.sync
            def _(sp):
                def fetch(n):
                    if n.reaches(SLOTS):
                        sp.wait_ge(flipped, n.g - SLOTS + 1)
                        sp.sem_inc(k.sp_ready, 1)
                        sp.wait_ge(source_in[n.slot], 64 * n.round)
                    sp.dma_start(record[n.slot][:], k.records[bass.ds(n.g * GROUP, GROUP), :]
                                 .rearrange("(p t) c -> p t c", p=P)).then_inc(rec_in[n.slot], 16)

                def store(n):
                    sp.wait_ge(cast, 2 * n.g + 2)
                    sp.sem_inc(k.sp_ready, 1)
                    sp.wait_ge(rest_out, 2 * n.g + 2)
                    for blk, part in enumerate((2, 0, 1, 0)):
                        sp.dma_start(k.stack_d[bass.ds(n.g * 512 + blk * 128, 128), :],
                                     parts[n.slot][:, part]).then_inc(stored[n.slot], 16)

                def step(near):
                    if near(3).exists():
                        fetch(near(3))
                    if near(-3).exists():
                        store(near(-3))

                over_groups(sp, step, 3, 3)

            @block.gpsimd
            def _(pool):
                nc.gpsimd.memset(half[:], 0.5).then_inc(halved, 1)

                def gather(near):
                    n = near(0)
                    pool.wait_ge(rec_in[n.slot], 16 * n.round + 16)
                    if n.reaches(SLOTS):
                        pool.wait_ge(multiplied, (n.g - SLOTS + 1) * SUB)
                    pool.wait_ge(k.tables, 32)
                    pool.sem_inc(k.pool_ready, 1)
                    for t in range(SUB):
                        nc.gpsimd.indirect_dma_start(
                            source[n.slot][:, t, :], None, k.p1_d[:, :],
                            bass.IndirectOffsetOnAxis(ap=record[n.slot][:, t, C_OTHER:C_OTHER + 1].bitcast(I32), axis=0)
                        ).then_inc(source_in[n.slot], 16)

                over_groups(pool, gather, 0, 0)

            @block.tensor
            def _(pe):
                def flips(n):
                    pe.wait_ge(hot_ready, n.g + 1)
                    if n.reaches(1):
                        pe.wait_ge(hot_copied, n.g)
                        pe.wait_ge(attr_copied, n.g)
                    for t in range(SUB):
                        nc.tensor.transpose(ps_hot[:, t * P:(t + 1) * P], hot[n.two][:, t], k.ident_b[:])
                    for t in range(SUB):
                        last = nc.tensor.transpose(ps_attr[:, t * P:(t + 1) * P], record[n.slot][:, t, EA96:EA96 + EA32],
                                                   k.ident[:])
                    last.then_inc(flipped, 1)

                def target(n, row_tile, t):
                    if n.reaches(1) or t >= 2:
                        pe.wait_ge(multiplied, n.g * SUB + t - 1)
                    for j in range(3):
                        last = nc.tensor.matmul(ps_target[t % 2], hot_t[n.two][:, t * P:(t + 1) * P],
                                                k.p1_parts[:, bass.ds(row_tile * (3 * 384) + j * 384, 384)],
                                                start=j == 0, stop=j == 2)
                    last.then_inc(target_out, 1)

                def ip_flips(n):
                    pe.wait_ge(summed, n.g * SUB + SUB)
                    if n.reaches(1):
                        pe.wait_ge(ip_copied, n.g)
                    for t in range(SUB):
                        last = nc.tensor.transpose(ps_ip[:, t * P:(t + 1) * P], ip[n.two][:, t], k.ident[:])
                    last.then_inc(ip_flipped, 1)

                def begin_hidden(n, row_tile):
                    pe.wait_ge(attr_copied, n.g + 1)
                    if n.reaches(2):
                        pe.wait_ge(hidden_out, n.g - 1)
                    for at, w0 in halves:
                        nc.tensor.matmul(ps_hid[n.two], k.hid_f[:, w0:w0 + P], attr_t[n.two][:, at],
                                         start=w0 == HID, stop=False)
                    for j in range(3):
                        for at, w0 in halves:
                            last = nc.tensor.matmul(ps_hid[n.two],
                                                    k.ph_parts[:, bass.ds(row_tile * (3 * PAD) + j * PAD + w0, P)],
                                                    hot_t[n.two][:, at], start=False, stop=False)
                    last.then_inc(begun, 1)

                def end_hidden(n):
                    pe.wait_ge(ip_copied, n.g + 1)
                    for at, w0 in halves:
                        last = nc.tensor.matmul(ps_hid[n.two], k.hid_s[:, w0:w0 + P], ip_t[:, at],
                                                start=False, stop=w0 == 0)
                    last.then_inc(hidden_in, 1)

                def step(near):
                    here, ahead, behind = near(0), near(1), near(-1)
                    if here.exists():
                        pe.wait_ge(hot_copied, here.g + 1)
                        row_tile = pe.value_load(k.group_tile[0:1, bass.ds(here.g, 1)], min_val=0, max_val=TILES - 1)
                        target(here, row_tile, 0)
                        target(here, row_tile, 1)
                    if behind.exists():
                        ip_flips(behind)
                    if ahead.exists():
                        flips(ahead)
                    if here.exists():
                        target(here, row_tile, 2)
                    if behind.exists():
                        end_hidden(behind)
                    if here.exists():
                        target(here, row_tile, 3)
                        begin_hidden(here, row_tile)

                over_groups(pe, step, 1, 1)

            @block.scalar
            def _(act):
                s = nc.scalar
                s.preload_act_table_set("natural_log_exp_and_others")
                act.wait_ge(halved, 1)

                def soften(n):
                    act.wait_ge(hidden_in, n.g + 1)
                    if n.reaches(1):
                        act.wait_ge(hidden_out, n.g)
                    s.activation(size[:], ps_hid[n.two], ACT.Abs).then_inc(soft, 1)
                    act.wait_ge(soft, 3 * n.g + 1)
                    s.activation(size[:], size[:], ACT.Exp, scale=-1.0).then_inc(soft, 1)
                    act.wait_ge(soft, 3 * n.g + 2)
                    s.activation(size[:], size[:], ACT.Ln, scale=0.5, bias=half[:, 0:1]).then_inc(soft, 1)

                def copy_ip(n):
                    act.wait_ge(ip_flipped, n.g + 1)
                    if n.reaches(1):
                        act.wait_ge(hidden_in, n.g)
                    s.activation(ip_t[:], ps_ip, ACT.Copy).then_inc(ip_copied, 1)

                def cast_part(n, j):
                    if j == 0:
                        act.wait_ge(hidden_out, n.g + 1)
                        if n.reaches(SLOTS):
                            act.wait_ge(stored[n.slot], 64 * n.round)
                    else:
                        act.wait_ge(rest_out, 2 * n.g + 1)
                    s.activation(parts[n.slot][:, j], hidden[:], ACT.Copy).then_inc(cast, 1)

                def copy_hot(n):
                    act.wait_ge(flipped, n.g + 1)
                    if n.reaches(2):
                        act.wait_ge(begun, n.g - 1)
                    s.activation(hot_t[n.two][:], ps_hot, ACT.Copy).then_inc(hot_copied, 1)

                def copy_attr(n):
                    s.activation(attr_t[n.two][:], ps_attr, ACT.Copy).then_inc(attr_copied, 1)

                def step(near):
                    ahead, behind, last = near(1), near(-1), near(-2)
                    if last.exists():
                        soften(last)
                    if behind.exists():
                        copy_ip(behind)
                    if ahead.exists():
                        copy_hot(ahead)
                    if last.exists():
                        cast_part(last, 0)
                    if ahead.exists():
                        copy_attr(ahead)
                    if last.exists():
                        cast_part(last, 1)

                over_groups(act, step, 1, 2)

            @block.vector
            def _(dve):
                v = nc.vector

                def one_hots(n):
                    dve.wait_ge(rec_in[n.slot], 16 * n.round + 16)
                    if n.reaches(2):
                        dve.wait_ge(flipped, n.g - 1)
                    for t in range(SUB):
                        last = v.tensor_scalar(hot[n.two][:, t], k.lane[:], record[n.slot][:, t, C_KEY:C_KEY + 1], None,
                                               ALU.is_equal)
                    last.then_inc(hot_ready, 1)

                def multiply(n, t):
                    e = n.g * SUB + t
                    if t == 0:
                        dve.wait_ge(source_in[n.slot], 64 * n.round + 64)
                    dve.wait_ge(target_out, e + 1)
                    if n.reaches(1) or t >= 2:
                        dve.wait_ge(summed, e - 1)
                    v.tensor_tensor(prod[t % 2][:], ps_target[t % 2].rearrange("p (m u) -> p m u", m=3),
                                    source[n.slot][:, t].rearrange("p (m u) -> p m u", m=3),
                                    ALU.mult).then_inc(multiplied, 1)

                def sum_up(n, t):
                    e = n.g * SUB + t
                    if t == 0 and n.reaches(2):
                        dve.wait_ge(ip_flipped, n.g - 1)
                    dve.wait_ge(multiplied, e + 1)
                    v.tensor_reduce(ip[n.two][:, t], prod[t % 2][:].rearrange("p m u -> p u m"), AX.X,
                                    ALU.add).then_inc(summed, 1)

                def join(n):
                    dve.wait_ge(soft, 3 * n.g + 3)
                    if n.reaches(1):
                        dve.wait_ge(rest_out, 2 * n.g)
                    v.scalar_tensor_tensor(hidden[:], ps_hid[n.two], 0.0, size[:], ALU.max, ALU.add
                                           ).then_inc(hidden_out, 1)

                def take_off(n, j):
                    dve.wait_ge(cast, 2 * n.g + j + 1)
                    if j:
                        dve.wait_ge(rest_out, 2 * n.g + 1)
                    v.tensor_tensor(hidden[:] if j == 0 else parts[n.slot][:, 2], hidden[:], parts[n.slot][:, j],
                                    ALU.subtract).then_inc(rest_out, 1)

                def step(near):
                    here, ahead, last = near(0), near(1), near(-2)
                    if ahead.exists():
                        one_hots(ahead)
                    if here.exists():
                        multiply(here, 0)
                        multiply(here, 1)
                        sum_up(here, 0)
                    if last.exists():
                        join(last)
                    if here.exists():
                        sum_up(here, 1)
                        multiply(here, 2)
                        multiply(here, 3)
                    if last.exists():
                        take_off(last, 0)
                    if here.exists():
                        sum_up(here, 2)
                        sum_up(here, 3)
                    if last.exists():
                        take_off(last, 1)

                over_groups(dve, step, 1, 2)


def edge_messages(k, summed_x):
    nc = k.nc
    with ExitStack() as ctx:
        def sb(name, shape, dt=F32):
            return ctx.enter_context(nc.sbuf_tensor(name, shape, dt))

        record = [sb(f"rec_m{b}", [P, SUB, REC]) for b in range(SLOTS)]
        source = [sb(f"xsrc{b}", [P, SUB, D]) for b in range(SLOTS)]
        stack = [sb(f"stack{b}", [P, 2, 2, GROUP // 2], BF16) for b in range(SLOTS)]
        hot = [sb(f"mhot{b}", [P, SUB, P]) for b in range(2)]
        left = [sb(f"left{b}", [P, 4, P]) for b in range(2)]
        w = [sb(f"weights{b}", [P, 4, P]) for b in range(2)]
        z = [sb(f"z{b}", [P, P]) for b in range(2)]
        vz = [sb(f"vz{b}", [P, P]) for b in range(2)]
        message = [sb(f"message{t}", [P, 4, P]) for t in range(SUB)]
        second = [sb(f"second{t}", [P, 3, P]) for t in range(SUB)]

        rec_in = [k.sem(f"m_rec_in{b}") for b in range(SLOTS)]
        stack_in = [k.sem(f"m_stack_in{b}") for b in range(SLOTS)]
        source_in = [k.sem(f"m_source_in{b}") for b in range(SLOTS)]
        own_in, hot_ready, weights_in, left_out = k.sem("m_own_in"), k.sem("m_hot"), k.sem("m_weights"), k.sem("m_left")
        work, message_ready, sent = k.sem("m_work"), k.sem("m_ready"), k.sem("m_sent")
        outer_done, added = k.sem("m_outer"), k.sem("m_added")
        z_begun, v_ready, second_ready = k.sem("m_z_begun"), k.sem("m_v_ready"), k.sem("m_second_ready")

        ps_f = [k.psum[:, b].rearrange("p (q u) -> p q u", q=4) for b in range(2)]
        ps_s = [k.psum[:, 2 + b].rearrange("p (q u) -> p q u", q=4) for b in range(2)]
        ps_sum = [k.psum[:, 4 + b] for b in range(2)]
        SH = EA96 + EA32
        WORK = 5

        def at(near, t):
            return near(t // SUB), t % SUB

        with nc.Block() as block:
            @block.sync
            def _(sp):
                for b in range(SLOTS):
                    sp.wait_ge(k.stored[b], GROUPS // SLOTS * 64)

                def fetch(near):
                    n = near(2)
                    if not n.exists():
                        return
                    if n.reaches(SLOTS):
                        sp.wait_ge(sent, (n.g - SLOTS + 1) * SUB)
                        sp.sem_inc(k.sp_ready, 1)
                        sp.wait_ge(source_in[n.slot], 64 * n.round)
                    sp.dma_start(record[n.slot][:], k.records[bass.ds(n.g * GROUP, GROUP), :]
                                 .rearrange("(p t) c -> p t c", p=P)).then_inc(rec_in[n.slot], 16)
                    for blk in range(4):
                        sp.dma_start(stack[n.slot][32 * blk:32 * blk + 32].rearrange("r h s c -> r (h s) c"),
                                     k.stack_d[bass.ds(n.g * 512 + blk * 128, 128), :]
                                     .rearrange("(b r) c -> r b c", r=32)).then_inc(stack_in[n.slot], 16)

                sp.dma_start(summed_x[:].rearrange("p (t c) -> p t c", c=D),
                             k.xs_d.rearrange("(t p) c -> p t c", p=P)).then_inc(own_in, 16)
                over_groups(sp, fetch, 2, 0)

            @block.gpsimd
            def _(pool):
                def gather(n, t):
                    if t == 0:
                        pool.wait_ge(rec_in[n.slot], 16 * n.round + 16)
                        if n.reaches(SLOTS):
                            pool.wait_ge(message_ready, (n.g - SLOTS + 1) * SUB)
                            pool.wait_ge(v_ready, (n.g - SLOTS + 1) * SUB)
                        pool.wait_ge(k.tables, 32)
                        pool.sem_inc(k.pool_ready, 1)
                    nc.gpsimd.indirect_dma_start(
                        source[n.slot][:, t, :], None, k.xs_d[:, :],
                        bass.IndirectOffsetOnAxis(ap=record[n.slot][:, t, C_OTHER:C_OTHER + 1].bitcast(I32), axis=0)
                    ).then_inc(source_in[n.slot], 16)

                def one_hot(n, t):
                    if n.reaches(2):
                        pool.wait_ge(sent, (n.g - 2) * SUB + t + 1)
                        pool.sem_inc(k.pool_ready, 1)
                    nc.gpsimd.tensor_scalar(hot[n.two][:, t], k.lane[:], record[n.slot][:, t, C_KEY:C_KEY + 1],
                                            None, ALU.is_equal).then_inc(hot_ready, 1)

                def scalar_message(n, t):
                    e = n.g * SUB + t
                    if t == 0:
                        pool.wait_ge(source_in[n.slot], 64 * n.round + 64)
                    pool.wait_ge(outer_done, e + 1)
                    if n.reaches(1) or t >= 2:
                        pool.wait_ge(second_ready, e - 1)
                    nc.gpsimd.tensor_tensor(vz[t % 2][:], w[t % 2][:, 1], source[n.slot][:, t, 0:P],
                                            ALU.mult).then_inc(v_ready, 1)

                def step(near):
                    for t in range(SUB):
                        if near(2).exists():
                            gather(near(2), t)
                        if near(1).exists():
                            one_hot(near(1), t)
                        if near(0).exists():
                            scalar_message(near(0), t)

                over_groups(pool, step, 2, 0)

            @block.tensor
            def _(pe):
                def mix(n, t):
                    e = n.g * SUB + t
                    if t == 0:
                        pe.wait_ge(stack_in[n.slot], 64 * n.round + 64)
                    if n.reaches(1) or t >= 2:
                        pe.wait_ge(outer_done, e - 1)
                    for ps, kind in ((ps_f, 0), (ps_s, 1)):
                        for j in range(2):
                            last = nc.tensor.matmul(ps[t % 2].rearrange("p q u -> p (q u)"),
                                                    stack[n.slot][:, t // 2, kind, (t % 2) * P:(t % 2 + 1) * P], k.mix[:, kind, j],
                                                    start=j == 0, stop=j == 1)
                    last.then_inc(weights_in, 1)

                def send(n, t):
                    e = n.g * SUB + t
                    pe.wait_ge(hot_ready, e + 1)
                    if t == 0 and n.reaches(2):
                        pe.wait_ge(added, n.g - 1)
                    pe.wait_ge(message_ready, e + 1)
                    nc.tensor.matmul(ps_sum[n.two], hot[n.two][:, t], message[t][:].rearrange("p q u -> p (q u)"),
                                     start=t == 0, stop=False)
                    pe.wait_ge(second_ready, e + 1)
                    nc.tensor.matmul(ps_sum[n.two][:, P:D], hot[n.two][:, t], second[t][:].rearrange("p q u -> p (q u)"),
                                     start=False, stop=t == SUB - 1).then_inc(sent, 1)

                def step(near):
                    for t in range(SUB):
                        if at(near, t + 1)[0].exists():
                            mix(*at(near, t + 1))
                        if at(near, t - 2)[0].exists():
                            send(*at(near, t - 2))

                over_groups(pe, step, 1, 1)

            @block.scalar
            def _(act):
                def left_factor(n, t):
                    e = n.g * SUB + t
                    if t == 0:
                        act.wait_ge(rec_in[n.slot], 16 * n.round + 16)
                    act.wait_ge(weights_in, e + 1)
                    if n.reaches(1) or t >= 2:
                        act.wait_ge(outer_done, e - 1)
                    nc.scalar.activation(left[t % 2][:, 0:4:2], ps_f[t % 2][:, 0:4:2], ACT.Copy,
                                         scale=record[n.slot][:, t, SH:SH + 1]).then_inc(left_out, 1)
                    nc.scalar.activation(left[t % 2][:, 1:4:2], ps_f[t % 2][:, 1:4:2], ACT.Copy).then_inc(left_out, 1)

                def begin_z(n, t):
                    e = n.g * SUB + t
                    if t == 0:
                        act.wait_ge(source_in[n.slot], 64 * n.round + 64)
                    if n.reaches(1) or t >= 2:
                        act.wait_ge(message_ready, e - 1)
                    nc.scalar.activation(z[t % 2][:], source[n.slot][:, t, P:2 * P], ACT.Copy,
                                         scale=record[n.slot][:, t, SH + 1:SH + 2]).then_inc(z_begun, 1)

                def second_part(n, t):
                    e = n.g * SUB + t
                    act.wait_ge(v_ready, e + 1)
                    if n.reaches(1):
                        act.wait_ge(sent, e - SUB + 1)
                    for m in range(3):
                        last = nc.scalar.activation(second[t][:, m], vz[t % 2][:], ACT.Copy,
                                                    scale=record[n.slot][:, t, SH + 1 + m:SH + 2 + m])
                    last.then_inc(second_ready, 1)

                def step(near):
                    for t in range(SUB):
                        if at(near, t + 1)[0].exists():
                            left_factor(*at(near, t + 1))
                            begin_z(*at(near, t + 1))
                        if near(0).exists():
                            second_part(near(0), t)

                over_groups(act, step, 1, 0)

            @block.vector
            def _(dve):
                v = nc.vector
                dve.wait_ge(own_in, 16)

                def tile(n, t):
                    e = n.g * SUB + t
                    st = Steps(dve, work, e * WORK)
                    x0 = source[n.slot][:, t, 0:P]
                    x1 = source[n.slot][:, t, P:D].rearrange("p (m u) -> p m u", m=3)
                    sh = [record[n.slot][:, t, SH + 1 + m:SH + 2 + m] for m in range(3)]
                    wt, zt, mt = w[t % 2], z[t % 2], message[t]
                    if n.reaches(1) or t >= 2:
                        dve.wait_ge(message_ready, e - 1)
                        dve.wait_ge(v_ready, e - 1)
                    dve.wait_ge(z_begun, e + 1)
                    st.done(v.scalar_tensor_tensor(zt[:], x1[:, 1], sh[1], zt[:], ALU.mult, ALU.add))
                    dve.wait_ge(left_out, 2 * e + 2)
                    v.tensor_tensor(wt[:], left[t % 2][:], ps_s[t % 2], ALU.mult).then_inc(outer_done, 1)
                    st.settle()
                    st.done(v.scalar_tensor_tensor(zt[:], x1[:, 2], sh[2], zt[:], ALU.mult, ALU.add))
                    if n.reaches(1):
                        dve.wait_ge(sent, e - SUB + 1)
                    dve.wait_ge(outer_done, e + 1)
                    st.done(v.tensor_tensor(mt[:, 0], wt[:, 0], x0, ALU.mult))
                    dve.wait_ge(work, e * WORK + 2)
                    st.done(v.tensor_tensor(zt[:], zt[:], wt[:, 3], ALU.mult))
                    st.done(v.tensor_tensor(mt[:, 1:4], x1, wt[:, 2:3].broadcast_to([P, 3, P]), ALU.mult))
                    dve.wait_ge(work, e * WORK + 4)
                    v.tensor_tensor(mt[:, 0], mt[:, 0], zt[:], ALU.add).then_inc(message_ready, 1)
                    assert st.n == WORK

                def add(n):
                    dve.wait_ge(sent, n.g * SUB + SUB)
                    if n.reaches(1):
                        dve.wait_ge(added, n.g)
                    nt = dve.value_load(k.group_tile[0:1, bass.ds(n.g, 1)], min_val=0, max_val=TILES - 1)
                    here = summed_x[:, bass.ds(nt * D, D)]
                    v.tensor_tensor(here, here, ps_sum[n.two], ALU.add).then_inc(added, 1)

                def step(near):
                    for t in range(SUB):
                        if near(0).exists():
                            if t == 0:
                                dve.wait_ge(source_in[near(0).slot], 64 * near(0).round + 64)
                            tile(near(0), t)
                        if t == 2 and near(-1).exists():
                            add(near(-1))

                over_groups(dve, step, 0, 1)


def tensor_output(k, summed_x):
    nc, a = k.nc, k.a
    with ExitStack() as ctx:
        def sb(name, shape, dt=F32):
            return ctx.enter_context(nc.sbuf_tensor(name, shape, dt))

        wo0, wo1, bo0 = sb("wo0", [P, P]), sb("wo1", [P, P]), sb("bo0", [1, P])
        zt = sb("zt", [P, 4, COLS])
        loaded = k.sem("out_loaded")
        n = load(k, loaded, [(wo0[:], a["L1_gnn_W_o0"]), (wo1[:], a["L1_gnn_W_o1"]), (bo0[:], row_of(a["L1_gnn_b_o0"]))])
        flip(k, TILES, (lambda t, j: summed_x[:, t * D + j * P:t * D + j * P + P], 4),
             lambda j, w, t: zt[:, j:j + w, t * P:(t + 1) * P], [(loaded, n)])

        def residual(t, ps):
            nc.vector.scalar_tensor_tensor(k.x[:, t, 0:P], k.x[:, t, 0:P], 2.0, ps[:, 0:P], ALU.mult, ALU.add)
            x1 = k.x[:, t, P:D].rearrange("p (u m) -> p m u", m=3)
            return nc.vector.scalar_tensor_tensor(x1, x1, 2.0, ps[:, P:D].rearrange("p (m u) -> p m u", m=3),
                                                  ALU.mult, ALU.add)

        rows_normed(k, row_products(k, lambda t: [(zt[:, 0, t * P:(t + 1) * P], wo0[:], slice(0, P)),
                                                  (k.ones[0:1, :], bo0[:], slice(0, P))]
                                    + [(zt[:, 1 + m, t * P:(t + 1) * P], wo1[:], slice((1 + m) * P, (2 + m) * P))
                                       for m in range(3)]),
                    residual, k.x)


def mean_layer(k, next_weights):
    nc, a = k.nc, k.a
    with ExitStack() as ctx:
        def sb(name, shape, dt=F32):
            return ctx.enter_context(nc.sbuf_tensor(name, shape, dt))

        inv = sb("inv", [P, TILES])
        mean = sb("mean", [P, TILES, D])
        loaded, loaded_c, degree = k.sem("mean_loaded"), k.sem("counts_in"), k.sem("degree")
        with nc.sbuf_tensor("ct", [P, TILES, COLS], F32) as ct, nc.sbuf_tensor("c", [P, TILES, COLS], F32) as c:
            nl = load(k, loaded_c, [(ct[:].rearrange("p t s -> p (t s)"), k.counts_d[:, :])])
            flip(k, TILES, (lambda t, j: ct[:, t, j * P:(j + 1) * P], TILES),
                 lambda j, w, t: c[:, j:j + w, t * P:(t + 1) * P], [(loaded_c, nl)])
            with nc.Block() as block:
                @block.sync
                def _(sp):
                    sp.dma_start(k.by_target_d[:, :], c[:].rearrange("p t s -> p (t s)")).then_inc(loaded_c, 16)

                @block.vector
                def _(dve):
                    st = Steps(dve, degree)
                    st.done(nc.vector.tensor_reduce(inv[:], c[:], AX.X, ALU.add))
                    st.settle()
                    st.done(nc.vector.tensor_scalar(inv[:], inv[:], 1.0, None, ALU.max))
                    st.settle()
                    st.done(nc.vector.reciprocal(inv[:], inv[:]))
                    st.settle()

            def finish(act, t, ps):
                if act:
                    return nc.scalar.activation(mean[:, t], ps, ACT.Copy, scale=inv[:, t:t + 1])
                return nc.vector.tensor_scalar(mean[:, t], ps, inv[:, t:t + 1], None, ALU.mult)

            next_weights.load_first()
            rows_out(k, lambda t: [(ct[:, s, t * P:(t + 1) * P], k.x[:, s], slice(0, D)) for s in range(TILES)], finish)
            with nc.Block() as block:
                @block.sync
                def _(sp):
                    sp.wait_ge(loaded_c, nl + 16)
        wl, wr = sb("wl", [P, 4, D]), sb("wr", [P, 4, D])
        bl, g, be = sb("bl", [P, 4]), sb("g2", [P, 4]), sb("be2", [P, 4])
        mean_t, xt, h = (sb(n, [P, 4, COLS]) for n in ("mean_t", "xt2", "h_2"))
        n = load(k, loaded, [(wl[:], weight(a["L2_gnn_W_l"])), (wr[:], weight(a["L2_gnn_W_r"])),
                             (bl[:], columns(a["L2_gnn_b_l"])), (g[:], columns(a["L2_gnn_gamma"])),
                             (be[:], columns(a["L2_gnn_beta"]))])
        flip(k, TILES, (lambda t, j: mean[:, t, j * P:(j + 1) * P], 4),
             lambda j, w, t: mean_t[:, j:j + w, t * P:(t + 1) * P])
        flip(k, TILES, (lambda t, j: k.x[:, t, j * P:(j + 1) * P], 4),
             lambda j, w, t: xt[:, j:j + w, t * P:(t + 1) * P])
        batch_normed(k, 4, lambda j: [(wl[:, i, j * P:(j + 1) * P], mean_t[:, i]) for i in range(4)]
                     + [(wr[:, i, j * P:(j + 1) * P], xt[:, i]) for i in range(4)],
                     lambda j, at, ps: nc.vector.tensor_scalar(h[:, j, at], ps, bl[:, j:j + 1], 0.0, ALU.add, ALU.max),
                     h, g, be, [(loaded, n)])
        rows_normed(k, row_flips(k, h), lambda t, ps: nc.vector.tensor_tensor(k.x[:, t], k.x[:, t], ps, ALU.add), k.x)


class AttentionWeights:

    def __init__(self, k, scope):
        def sb(name, shape):
            return scope.enter_context(k.nc.sbuf_tensor(name, shape, F32))

        self.k = k
        self.wq, self.wk, self.wv, self.wo = (sb(n, [P, 4, D]) for n in ("wq", "wk", "wv", "wo"))
        self.w1, self.w2 = sb("wf1", [P, 4, FF]), sb("wf2", [P, 2, D])
        vectors = [("bq", 4), ("bo", 4), ("b1", 2), ("b2", 4), ("g1", 4), ("beta1", 4), ("g2", 4), ("beta2", 4)]
        self.small = {n: sb("l3_" + n, [P, w]) for n, w in vectors}
        self.lg, self.lb = sb("lg", [P, D]), sb("lb", [P, D])
        self.front_in, self.back_in = k.sem("qkv_loaded"), k.sem("ff_loaded")
        self.n_front = self.n_back = 0

    def front_loads(self, block):
        a = self.k.a
        self.n_front += 16 * 4
        return [(self.wq[:], weight(a["L3_gnn_Wq"][block])), (self.small["bq"][:], columns(a["L3_gnn_bq"][block])),
                (self.wk[:], weight(a["L3_gnn_Wk"][block])), (self.wv[:], weight(a["L3_gnn_Wv"][block]))]

    def load_first(self):
        load(self.k, self.front_in, self.front_loads(0))
        self.load_back(0, [(self.lg[:], spread(self.k.a["L3_gnn_ln_g"])), (self.lb[:], spread(self.k.a["L3_gnn_ln_b"]))])

    def load_back(self, block, more=()):
        a = self.k.a
        self.n_back += load(self.k, self.back_in, [
            (self.wo[:], weight(a["L3_gnn_Wo"][block])), (self.w1[:], weight(a["L3_gnn_W1"][block])),
            (self.w2[:], weight(a["L3_gnn_W2"][block])), *more,
            *((self.small[n][:], columns(a["L3_gnn_" + n][block])) for n in self.small if n != "bq")])


def row_flips(k, h):
    def fill(t, bank):
        for j in range(4):
            last = k.nc.tensor.transpose(bank[:, j * P:(j + 1) * P], h[:, j, t * P:(t + 1) * P], k.ident[:])
        return last
    return fill


def attention(k, qt, kt, vr, agg, loaded, loads):
    nc = k.nc
    with ExitStack() as ctx:
        k.names += 1
        names = k.names

        def sb(name, shape, dt=F32):
            return ctx.enter_context(nc.sbuf_tensor(f"{name}_{names}", shape, dt))

        def sem(name):
            return k.sem(f"{name}_{names}")

        c = [sb(f"c{b}", [P, COLS]) for b in range(2)]
        far = [sb(f"far{b}", [P, COLS]) for b in range(2)]
        q = [sb(f"q{b}", [P, 4, P]) for b in range(2)]
        s = [sb(f"s{b}", [P, COLS]) for b in range(2)]
        p = [sb(f"p{b}", [P, COLS]) for b in range(2)]
        pt = [sb(f"pt{b}", [P, TILES, P]) for b in range(2)]
        top = [sb(f"top{b}", [P, 4]) for b in range(4)]

        c_in = [sem(f"c_in{b}") for b in range(2)]
        q_in, far_ready = sem("q_in"), sem("far_ready")
        scored, masked, negated, raised = sem("scored"), sem("masked"), sem("negated"), sem("raised")
        weighed, inverted, turned, turned_out = sem("weighed"), sem("inverted"), sem("turned"), sem("turned_out")
        mixed, written = sem("mixed"), sem("written")

        ps_s = k.psum[:, 0:3].rearrange("p c n -> p (c n)")
        ps_t = k.psum[:, 3:6].rearrange("p c n -> p (c n)")
        ps_o = [k.psum[:, 6 + b, 0:DH] for b in range(2)]

        def heads(step):
            def tile(near):
                for h in range(HEADS):
                    step(lambda d: (near((h + d) // HEADS), (h + d) % HEADS))
            return tile

        with nc.Block() as block:
            @block.sync
            def _(sp):
                def fetch(near):
                    n = near(1)
                    if n.exists():
                        if n.reaches(2):
                            sp.wait_ge(weighed, (n.g - 1) * HEADS)
                            sp.wait_ge(far_ready, n.g - 1)
                        sp.dma_start(c[n.two][:], k.by_target_d[:, bass.ds(n.g * COLS, COLS)]).then_inc(c_in[n.two], 16)
                    if near(0).fixed and near(0).g == 1:
                        for out, in_ in loads:
                            sp.dma_start(out, in_).then_inc(loaded, 16)

                over_tiles(sp, fetch, 1, 0)

            @block.gpsimd
            def _(pool):
                def prepare(near):
                    n = near(1)
                    if n.exists():
                        if n.reaches(2):
                            pool.wait_ge(masked, (n.g - 1) * HEADS)
                            pool.sem_inc(k.pool_ready, 1)
                        nc.gpsimd.tensor_copy(q[n.two][:], qt[:, :, bass.ds(n.g * P, P)]).then_inc(q_in, 1)
                        pool.wait_ge(c_in[n.two], n.round * 16 + 16)
                        pool.sem_inc(k.pool_ready, 1)
                        nc.gpsimd.tensor_scalar(far[n.two][:], c[n.two][:], 0.0, FAR, ALU.is_equal, ALU.mult
                                                ).then_inc(far_ready, 1)

                over_tiles(pool, prepare, 1, 0)

            @block.tensor
            def _(pe):
                def score(n, h):
                    e = n.g * HEADS + h
                    if h == 0:
                        pe.wait_ge(q_in, n.g + 1)
                    if n.reaches(1) or h >= 1:
                        pe.wait_ge(masked, e)
                    rows = slice(DH * (h % 2), DH * (h % 2) + DH)
                    for c0, cw in CHUNKS:
                        last = nc.tensor.matmul(ps_s[:, c0:c0 + cw], q[n.two][rows, h // 2], kt[rows, h // 2, c0:c0 + cw],
                                                start=True, stop=True)
                    last.then_inc(scored, 1)

                def turn(n, h):
                    e = n.g * HEADS + h
                    pe.wait_ge(weighed, e + 1)
                    if n.reaches(1) or h >= 1:
                        pe.wait_ge(turned_out, e)
                    for j in range(TILES):
                        last = nc.tensor.transpose(ps_t[:, j * P:(j + 1) * P], p[h % 2][:, j * P:(j + 1) * P], k.ident[:])
                    last.then_inc(turned, 1)

                def mix(n, h):
                    e = n.g * HEADS + h
                    pe.wait_ge(turned_out, e + 1)
                    if n.reaches(1) or h >= 2:
                        pe.wait_ge(written, e - 1)
                    for j in range(TILES):
                        last = nc.tensor.matmul(ps_o[h % 2], pt[h % 2][:, j], vr[:, j, h * DH:(h + 1) * DH],
                                                start=j == 0, stop=j == TILES - 1)
                    last.then_inc(mixed, 1)

                def step(head):
                    if head(1)[0].exists():
                        score(*head(1))
                    if head(-1)[0].exists():
                        mix(*head(-1))
                    if head(0)[0].exists():
                        turn(*head(0))

                over_tiles(pe, heads(step), 1, 1)

            @block.scalar
            def _(act):
                def raise_(n, h):
                    act.wait_ge(negated, n.g * HEADS + h + 1)
                    nc.scalar.activation(s[h % 2][:], s[h % 2][:], ACT.Exp, bias=top[h % 4][:, 1:2]).then_inc(raised, 1)

                def turn(n, h):
                    e = n.g * HEADS + h
                    act.wait_ge(turned, e + 1)
                    if n.reaches(1) or h >= 2:
                        act.wait_ge(mixed, e - 1)
                    nc.scalar.activation(pt[h % 2][:], ps_t[:, 0:COLS].rearrange("p (j n) -> p j n", n=P),
                                         ACT.Copy).then_inc(turned_out, 1)

                def step(head):
                    if head(1)[0].exists():
                        raise_(*head(1))
                    if head(0)[0].exists():
                        turn(*head(0))

                over_tiles(act, heads(step), 1, 0)

            @block.vector
            def _(dve):
                v = nc.vector

                def mask(n, h):
                    e = n.g * HEADS + h
                    if h == 0:
                        dve.wait_ge(far_ready, n.g + 1)
                    dve.wait_ge(scored, e + 1)
                    if n.reaches(1) or h >= 2:
                        dve.wait_ge(weighed, e - 1)
                    if n.reaches(1) or h >= 4:
                        dve.wait_ge(written, e - 3)
                    dve.sem_inc(k.dve_ready, 1)
                    v.tensor_tensor_reduce(out=s[h % 2][:], in0=ps_s[:, 0:COLS], in1=far[n.two][:], scale=1.0,
                                           scalar=2 * FAR, op0=ALU.add, op1=ALU.max,
                                           accum_out=top[h % 4][:, 0:1]).then_inc(masked, 1)
                    dve.wait_ge(masked, e + 1)
                    v.tensor_scalar(top[h % 4][:, 1:2], top[h % 4][:, 0:1], -1.0, None, ALU.mult).then_inc(negated, 1)

                def weigh(n, h):
                    e = n.g * HEADS + h
                    dve.wait_ge(raised, e + 1)
                    if n.reaches(1) or h >= 2:
                        dve.wait_ge(turned, e - 1)
                    v.tensor_tensor_reduce(out=p[h % 2][:], in0=s[h % 2][:], in1=c[n.two][:], scale=1.0, scalar=0.0,
                                           op0=ALU.mult, op1=ALU.add, accum_out=top[h % 4][:, 2:3]).then_inc(weighed, 1)

                def invert(n, h):
                    e = n.g * HEADS + h
                    dve.wait_ge(weighed, e + 1)
                    v.tensor_scalar(top[h % 4][:, 3:4], top[h % 4][:, 2:3], 1e-16, None, ALU.add).then_inc(inverted, 1)
                    dve.wait_ge(inverted, 2 * e + 1)
                    v.reciprocal(top[h % 4][:, 3:4], top[h % 4][:, 3:4]).then_inc(inverted, 1)

                def write(n, h):
                    e = n.g * HEADS + h
                    dve.wait_ge(mixed, e + 1)
                    dve.wait_ge(inverted, 2 * e + 2)
                    v.tensor_scalar(agg[:, bass.ds(n.g * D + h * DH, DH)], ps_o[h % 2], top[h % 4][:, 3:4], None,
                                    ALU.mult).then_inc(written, 1)

                def step(head):
                    if head(0)[0].exists():
                        weigh(*head(0))
                    if head(1)[0].exists():
                        mask(*head(1))
                    if head(0)[0].exists():
                        invert(*head(0))
                    if head(-1)[0].exists():
                        write(*head(-1))

                over_tiles(dve, heads(step), 1, 1)


def attention_layers(k, w):
    nc = k.nc
    with ExitStack() as ctx:
        def sb(name, shape, dt=F32):
            return ctx.enter_context(nc.sbuf_tensor(name, shape, dt))

        wq, wk, wv, wo, w1, w2 = w.wq, w.wk, w.wv, w.wo, w.w1, w.w2
        small, lg, lb = w.small, w.lg, w.lb
        xt = sb("xt3", [P, 4, COLS])
        kept, scaled = k.sem("x_kept"), k.sem("bq_scaled")
        flip(k, TILES, (lambda t, j: k.x[:, t, j * P:(j + 1) * P], 4),
             lambda j, w, t: xt[:, j:j + w, t * P:(t + 1) * P])
        with nc.Block() as block:
            @block.sync
            def _(sp):
                sp.dma_start(k.x_d[:, :], k.x[:].rearrange("p t d -> p (t d)")).then_inc(kept, 16)
                sp.wait_ge(kept, 16)
        agg = k.x[:].rearrange("p t d -> p (t d)")
        for layer in range(2):
            with nc.Block() as block:
                @block.vector
                def _(dve):
                    dve.wait_ge(w.front_in, w.n_front)
                    nc.vector.tensor_scalar(small["bq"][:], small["bq"][:], DH ** -0.5, None, ALU.mult).then_inc(scaled, 1)
            with ExitStack() as inner:
                with ExitStack() as inmost:
                    qt = inmost.enter_context(nc.sbuf_tensor(f"qt{layer}", [P, 4, COLS], F32))
                    kt = inmost.enter_context(nc.sbuf_tensor(f"kt{layer}", [P, 4, COLS], F32))
                    vr = inmost.enter_context(nc.sbuf_tensor(f"vr{layer}", [P, TILES, D], F32))

                    def scaled_q(act, j, at, ps):
                        if act:
                            return nc.scalar.activation(qt[:, j, at], ps, ACT.Identity, bias=small["bq"][:, j:j + 1],
                                                        scale=DH ** -0.5)
                        return nc.vector.tensor_scalar(qt[:, j, at], ps, DH ** -0.5, small["bq"][:, j:j + 1], ALU.mult, ALU.add)

                    features_out(k, 4, lambda j: [(wq[:, i, j * P:(j + 1) * P], xt[:, i]) for i in range(4)], scaled_q,
                                 [(w.front_in, w.n_front)])
                    features_out(k, 4, lambda j: [(wk[:, i, j * P:(j + 1) * P], xt[:, i]) for i in range(4)],
                                 lambda act, j, at, ps: copy_to(k, act, kt[:, j, at], ps))
                    rows_out(k, lambda t: [(xt[:, i, t * P:(t + 1) * P], wv[:, i], slice(0, D)) for i in range(4)],
                             lambda act, t, ps: copy_to(k, act, vr[:, t], ps))
                    attention(k, qt, kt, vr, agg, w.front_in, w.front_loads(1) if layer == 0 else [])
                at_ = inner.enter_context(nc.sbuf_tensor(f"agg_t{layer}", [P, 4, COLS], F32))
                ff = inner.enter_context(nc.sbuf_tensor(f"ff{layer}", [P, 2, COLS], F32))
                flip(k, TILES, (lambda t, j: agg[:, t * D + j * P:t * D + (j + 1) * P], 4),
                     lambda j, w, t: at_[:, j:j + w, t * P:(t + 1) * P])
                def onto_x(bias):
                    return lambda j, at, ps: nc.vector.scalar_tensor_tensor(xt[:, j, at], ps, bias[:, j:j + 1], xt[:, j, at],
                                                                            ALU.add, ALU.add)

                batch_normed(k, 4, lambda j: [(wo[:, i, j * P:(j + 1) * P], at_[:, i]) for i in range(4)],
                             onto_x(small["bo"]), xt, small["g1"], small["beta1"], [(w.back_in, w.n_back)])
                features_out(k, 2, lambda j: [(w1[:, i, j * P:(j + 1) * P], xt[:, i]) for i in range(4)],
                             lambda act, j, at, ps: add_bias(k, act, ff[:, j, at], ps, small["b1"][:, j:j + 1], relu=True))
                batch_normed(k, 4, lambda j: [(w2[:, i, j * P:(j + 1) * P], ff[:, i]) for i in range(2)],
                             onto_x(small["b2"]), xt, small["g2"], small["beta2"])
                if layer == 0:
                    w.load_back(1)
        with nc.Block() as block:
            @block.sync
            def _(sp):
                sp.dma_start(agg, k.x_d[:, :]).then_inc(kept, 16)
                sp.wait_ge(kept, 32)
        rows = sb("rows3", [P, TILES, D])
        shifted = k.sem("x_shifted3")

        def shift_x(pool):
            nc.gpsimd.tensor_tensor(k.x[:], k.x[:], lb[:][:, None, :].broadcast_to([P, TILES, D]), ALU.add).then_inc(shifted, 1)
            pool.wait_ge(shifted, 1)

        rows_normed(k, row_flips(k, xt), lambda t, ps: nc.vector.tensor_copy(rows[:, t], ps), rows, meanwhile=shift_x)
        add_scaled(k, rows, lg)


def program(nc, a, out):
    with ExitStack() as ctx:
        ctx.enter_context(nc.allow_non_contiguous_dma("rows of records"))
        k = Core(nc, ctx, a)
        k.records = nc.dram_tensor("records", [GROUPS * GROUP, REC], F32).ap()
        k.counts_d = nc.dram_tensor("counts_d", [P, TILES * COLS], F32).ap()
        k.lane = k.keep("lane", [P, P], F16)
        k.node = k.keep("node", [P, COLS], F16)
        k.ident = k.keep("ident", [P, P])
        k.ident_b = k.keep("ident_b", [P, P], BF16)
        k.group_tile = k.keep("group_tile_i", [P, GROUPS], I32)
        k.sums_t = k.keep("sums_t", [EA96, COLS])
        k.ones = k.keep("ones_row", [P, P])
        k.x = k.keep("x_rows", [P, TILES, D])
        k.filled, k.by_act, k.by_dve = k.sem("bank_filled"), k.sem("bank_out_act"), k.sem("bank_out_dve")
        k.filled_n = k.by_act_n = k.by_dve_n = 0
        k.norm, k.variances, k.roots = k.sem("norm_steps"), k.sem("variances"), k.sem("roots")
        k.biased, k.applied = k.sem("norm_biased"), k.sem("norm_applied")
        k.norm_n = k.root_n = 0
        k.p1_d = nc.dram_tensor("p1_d", [COLS, 384], F32).ap()
        k.xs_d = nc.dram_tensor("xs_d", [COLS, D], F32).ap()
        k.by_target_d = nc.dram_tensor("by_target_d", [P, TILES * COLS], F32).ap()
        k.x_d = nc.dram_tensor("x_d", [P, TILES * D], F32).ap()
        k.stack_d = nc.dram_tensor("stack_d", [GROUPS * 512, GROUP // 2], BF16).ap()
        k.x_loaded = k.sem("x_loaded")
        k.pool_ready, k.dve_ready, k.sp_ready = k.sem("pool_ready"), k.sem("dve_ready"), k.sem("sp_ready")
        x_cleared = k.sem("x_cleared")
        with nc.Block() as block:
            @block.gpsimd
            def _(pool):
                nc.gpsimd.memset(k.x[:, TILES - 1], 0.0).then_inc(x_cleared, 1)
                nc.gpsimd.memset(k.ones[:], 1.0).then_inc(x_cleared, 1)

            @block.sync
            def _(sp):
                whole = (TILES - 1) * P
                sp.dma_start(k.x[:, 0:TILES - 1], a["x"][0:whole, :].rearrange("(t p) d -> p t d", p=P)).then_inc(k.x_loaded, 16)
                sp.wait_ge(x_cleared, 2)
                sp.dma_start(k.x[0:LAST, TILES - 1], a["x"][whole:NODES, :]).then_inc(k.x_loaded, 16)

        sort_edges(k)
        with ExitStack() as scope:
            weights = mlp_weights(k, scope)
            count_edges(k, weights[1], weights[2])
            mlp_layer(k, weights)
        with ExitStack() as tensor_layer:
            tensor_nodes(k, tensor_layer)
            edge_hidden(k)
            summed_x = tensor_layer.enter_context(nc.sbuf_tensor("summed_x", [P, TILES * D], F32))
            edge_messages(k, summed_x)
            tensor_output(k, summed_x)
        prepared = AttentionWeights(k, ctx)
        mean_layer(k, prepared)
        attention_layers(k, prepared)
        if out is None:
            out = nc.dram_tensor("out", [NODES, D], F32, kind="ExternalOutput").ap()
        returned = k.sem("returned")
        with nc.Block() as block:
            @block.sync
            def _(sp):
                whole = (TILES - 1) * P
                sp.dma_start(out[0:whole, :].rearrange("(t p) d -> p t d", p=P), k.x[:, 0:TILES - 1]).then_inc(returned, 16)
                sp.dma_start(out[whole:NODES, :], k.x[0:LAST, TILES - 1]).then_inc(returned, 16)
                sp.wait_ge(returned, 32)


TURNED = ("L2_gnn_W_l", "L2_gnn_W_r", "L3_gnn_Wq", "L3_gnn_Wk", "L3_gnn_Wv", "L3_gnn_Wo", "L3_gnn_W1", "L3_gnn_W2")


def layout(name, array):
    return array.swapaxes(-1, -2) if name in TURNED else array


def kernel(**inputs):
    import numpy as np
    from concourse import bacc
    from concourse.bass_utils import run_bass_kernel_spmd

    nc = bacc.Bacc("TRN2", target_bir_lowering=False, num_devices=1)
    arrays, handles = {}, {}
    for name, array in inputs.items():
        arrays["in_" + name] = np.ascontiguousarray(layout(name, np.asarray(array)))
        handles[name] = nc.dram_tensor("in_" + name, arrays["in_" + name].shape,
                                       mybir.dt.from_np(arrays["in_" + name].dtype), kind="ExternalInput").ap()
    out = nc.dram_tensor("out_0", (NODES, D), F32, kind="ExternalOutput").ap()
    program(nc, handles, out)
    got = run_bass_kernel_spmd(nc, [arrays], core_ids=[0])
    return got.results[0]["out_0"]
```
